# Optimizing a Trainium2 kernel written in Bass

```python
import numpy as np
import jax
import jax.numpy as jnp

def _softmax(x, axis=-1):
    return jax.nn.softmax(x, axis=axis)

def _gelu(x):
    return jax.nn.gelu(x, approximate=True)

def _silu(x):
    return jax.nn.silu(x)

def _sigmoid(x):
    return jax.nn.sigmoid(x)

def _layernorm(x, axis=-1, eps=1e-05):
    m = jnp.mean(x, axis=axis, keepdims=True)
    v = jnp.var(x, axis=axis, keepdims=True)
    return (x - m) / jnp.sqrt(v + eps)

def _scatter_add(tgt, idx, src, axis=0):
    return tgt.at[idx].add(src)

def _segment_sum(src, seg, n):
    return jax.ops.segment_sum(src, seg, n)
kernel_name = 'mk_gnn_ffn_d1_gnn_r8_50ce30'

def setup_inputs(seed: int=0):
    np.random.seed(seed)
    _w = jnp.asarray

    def _rec_inputs():
        import jax
        import jax.numpy as jnp
        _gk = jax.random.key(seed)
        x = -0.0002117 + 1 * jax.random.normal(jax.random.fold_in(_gk, 1), (6250, 256), jnp.float32)
        src = jax.random.randint(jax.random.fold_in(_gk, 2), (200000,), 0, 6250, jnp.int32)
        dst = jnp.minimum((6250 * jax.random.uniform(jax.random.fold_in(_gk, 3), (200000,)) ** 2.0).astype(jnp.int32), 49999)
        _o = jnp.argsort(dst, stable=True)
        src = src[_o]
        dst = dst[_o]
        edge_weight = jax.random.uniform(jax.random.fold_in(_gk, 12), (200000,), jnp.float32, 0.0, 0.999998)
        edge_weight_n2 = jax.random.uniform(jax.random.fold_in(_gk, 13), (200000,), jnp.float32, 0.0, 0.999998)
        return (x, src, dst, edge_weight, edge_weight_n2)
    x, src, dst, edge_weight, edge_weight_n2 = _rec_inputs()

    def _L0_gnn_setup():
        import jax, jax.numpy as jnp
        import numpy as np
        N_NODES = 12500
        N_EDGES = 100000
        DIM = 256
        EPS = 1e-05
        key = jax.random.key(seed)
        ks = jax.random.split(key, 12)
        H = DIM
        s = 1.0 / np.sqrt(H)
        s2 = 1.0 / np.sqrt(2 * H)
        return {'feat': jax.random.normal(ks[0], (N_NODES, DIM), dtype=jnp.float32), 'src': jax.random.randint(ks[1], (N_EDGES,), 0, N_NODES, dtype=jnp.int32), 'dst': jax.random.randint(ks[2], (N_EDGES,), 0, N_NODES, dtype=jnp.int32), 'iw': jax.random.uniform(ks[3], (N_EDGES,), dtype=jnp.float32), 'ow': jax.random.uniform(ks[4], (N_EDGES,), dtype=jnp.float32), 'gamma': jnp.ones((DIM,), jnp.float32), 'beta': jnp.zeros((DIM,), jnp.float32), 'W_in': jax.random.uniform(ks[5], (H, H), jnp.float32, -s, s), 'b_in': jax.random.uniform(ks[6], (H,), jnp.float32, -s, s), 'W_out': jax.random.uniform(ks[7], (H, H), jnp.float32, -s, s), 'b_out': jax.random.uniform(ks[8], (H,), jnp.float32, -s, s), 'W_x2i': jax.random.uniform(ks[9], (2 * H, 2 * H), jnp.float32, -s2, s2), 'b_x2i': jax.random.uniform(ks[10], (2 * H,), jnp.float32, -s2, s2), 'W_h2h': jax.random.uniform(ks[11], (H, 2 * H), jnp.float32, -s, s)}
    _L0_gnn_all = _L0_gnn_setup()
    _L0_gnn_in = {k: v for k, v in _L0_gnn_all.items() if k in ('gamma', 'beta', 'W_in', 'b_in', 'W_out', 'b_out', 'W_x2i', 'b_x2i', 'W_h2h')}
    del _L0_gnn_all

    def _L0_ffn_setup():
        import jax, jax.numpy as jnp
        import numpy as np
        B, S, D = (8, 512, 256)
        H = 4 * D
        CAPACITY = 0.5
        key = jax.random.key(seed)
        ks = jax.random.split(key, 6)
        x = jax.random.normal(ks[0], (B, S, D), dtype=jnp.float32)
        attention_mask = jnp.zeros((B, 1, 1, S), dtype=jnp.float32)
        wr = jax.random.normal(ks[1], (D, 1), dtype=jnp.float32) * 0.02
        br = jnp.zeros((1,), dtype=jnp.float32)
        w1 = jax.random.normal(ks[2], (D, H), dtype=jnp.float32) * 0.02
        b1 = jnp.zeros((H,), dtype=jnp.float32)
        w2 = jax.random.normal(ks[3], (H, D), dtype=jnp.float32) * 0.02
        b2 = jnp.zeros((D,), dtype=jnp.float32)
        return {'x': x, 'attention_mask': attention_mask, 'wr': wr, 'br': br, 'w1': w1, 'b1': b1, 'w2': w2, 'b2': b2}
    _L0_ffn_all = _L0_ffn_setup()
    _L0_ffn_in = {k: v for k, v in _L0_ffn_all.items() if k in ('attention_mask', 'wr', 'br', 'w1', 'b1', 'w2', 'b2')}
    del _L0_ffn_all
    return {'x': x, 'src': src, 'dst': dst, 'edge_weight': edge_weight, 'edge_weight_n2': edge_weight_n2, 'L0_gnn_gamma': _L0_gnn_in['gamma'], 'L0_gnn_beta': _L0_gnn_in['beta'], 'L0_gnn_W_in': _L0_gnn_in['W_in'], 'L0_gnn_b_in': _L0_gnn_in['b_in'], 'L0_gnn_W_out': _L0_gnn_in['W_out'], 'L0_gnn_b_out': _L0_gnn_in['b_out'], 'L0_gnn_W_x2i': _L0_gnn_in['W_x2i'], 'L0_gnn_b_x2i': _L0_gnn_in['b_x2i'], 'L0_gnn_W_h2h': _L0_gnn_in['W_h2h'], 'L0_ffn_attention_mask': _L0_ffn_in['attention_mask'], 'L0_ffn_wr': _L0_ffn_in['wr'], 'L0_ffn_br': _L0_ffn_in['br'], 'L0_ffn_w1': _L0_ffn_in['w1'], 'L0_ffn_b1': _L0_ffn_in['b1'], 'L0_ffn_w2': _L0_ffn_in['w2'], 'L0_ffn_b2': _L0_ffn_in['b2']}

def reference(x, src, dst, edge_weight, edge_weight_n2, L0_gnn_gamma, L0_gnn_beta, L0_gnn_W_in, L0_gnn_b_in, L0_gnn_W_out, L0_gnn_b_out, L0_gnn_W_x2i, L0_gnn_b_x2i, L0_gnn_W_h2h, L0_ffn_attention_mask, L0_ffn_wr, L0_ffn_br, L0_ffn_w1, L0_ffn_b1, L0_ffn_w2, L0_ffn_b2):
    import jax
    import jax.numpy as jnp

    def _L0_gnn_ref(feat, src, dst, iw, ow, gamma, beta, W_in, b_in, W_out, b_out, W_x2i, b_x2i, W_h2h):
        import jax, jax.numpy as jnp
        import numpy as np
        N_NODES = 12500
        N_EDGES = 100000
        DIM = 256
        EPS = 1e-05
        N = feat.shape[0]
        num_steps = 1
        mean = jnp.mean(feat, axis=0)
        var = jnp.var(feat, axis=0)
        h = (feat - mean) * jax.lax.rsqrt(var + EPS) * gamma + beta
        for _ in range(num_steps):
            feat_in = h @ W_in + b_in
            feat_out = h @ W_out + b_out
            a_in = jax.ops.segment_sum(feat_in[src] * iw[:, None], dst, num_segments=N)
            a_out = jax.ops.segment_sum(feat_out[dst] * ow[:, None], src, num_segments=N)
            a = jnp.concatenate((a_in, a_out), axis=1)
            xi = a @ W_x2i + b_x2i
            hh = h @ W_h2h
            i_i, i_n = jnp.split(xi, 2, axis=1)
            h_i, h_n = jnp.split(hh, 2, axis=1)
            input_gate = jax.nn.sigmoid(i_i + h_i)
            new_gate = jnp.tanh(i_n + h_n)
            h = new_gate + input_gate * (h - new_gate)
        return h

    def _L0_ffn_ref(x, attention_mask, wr, br, w1, b1, w2, b2):
        import jax, jax.numpy as jnp
        import numpy as np
        B, S, D = (8, 512, 256)
        H = 4 * D
        CAPACITY = 0.5
        b, s, d = x.shape
        weights = (jnp.einsum('bsd,do->bso', x, wr) + br)[..., 0]
        k = max(1, int(CAPACITY * s))
        kk = k - 1 if k > 1 else 1
        _, idx = jax.lax.top_k(weights, k)
        sel_idx = idx[:, :kk]
        sel = jnp.take_along_axis(x, sel_idx[:, :, None], axis=1)
        h = jax.nn.gelu(jnp.einsum('bkd,dh->bkh', sel, w1) + b1)
        y = jnp.einsum('bkh,hd->bkd', h, w2) + b2
        w_sel = jnp.take_along_axis(weights, sel_idx, axis=1)
        y = y * w_sel[..., None]
        batch_idx = jnp.arange(b)[:, None]
        processed = jnp.zeros_like(x).at[batch_idx, sel_idx].set(y)
        return processed + x
    x = x + _L0_gnn_ref(_layernorm(x, axis=-1), src, dst, edge_weight, edge_weight_n2, L0_gnn_gamma, L0_gnn_beta, L0_gnn_W_in, L0_gnn_b_in, L0_gnn_W_out, L0_gnn_b_out, L0_gnn_W_x2i, L0_gnn_b_x2i, L0_gnn_W_h2h)
    x = x + _L0_ffn_ref(_layernorm(x, axis=-1)[None], L0_ffn_attention_mask, L0_ffn_wr, L0_ffn_br, L0_ffn_w1, L0_ffn_b1, L0_ffn_w2, L0_ffn_b2)[0]
    return x

_drawn_inputs = setup_inputs


def setup_inputs(seed=0):
    import zlib

    import numpy as np

    out = dict(_drawn_inputs(seed))
    spreads = {'L0_gnn_gamma': (1.0, 0.2),
     'L0_gnn_beta': (0.0, 0.1),
     'L0_ffn_b1': (0.0, 0.8),
     'L0_ffn_b2': (0.0, 0.8)}
    factors = {'L0_gnn_b_x2i': 7.9, 'L0_ffn_wr': 4.688, 'L0_ffn_w1': 5.118, 'L0_ffn_w2': 4.793}
    for name, (base, spread) in spreads.items():
        noise = np.random.default_rng([zlib.crc32(name.encode()), seed]).standard_normal(out[name].shape)
        drawn = base * np.exp(spread * noise) if base else spread * noise
        out[name] = jnp.asarray(drawn.astype(out[name].dtype))
    for name, factor in factors.items():
        out[name] = (out[name] * factor).astype(out[name].dtype)
    return out
```

```python
import numpy as np
import concourse.bass as bass
from concourse import mybir
from contextlib import ExitStack

P = 128
EPS = 1e-5


def gnn_ffn(nc, x, src, dst, iw, ow, gamma, beta, w_in, b_in, w_out, b_out, w_x2i, b_x2i, w_h2h,
            wr, br, w1, b1, w2, b2, out):
    f32, bf16, i32 = mybir.dt.float32, mybir.dt.bfloat16, mybir.dt.int32
    ALU, ACT, AX = mybir.AluOpType, mybir.ActivationFunctionType, mybir.AxisListType

    NODES, D = x.shape
    EDGES = src.shape[0]
    H = w1.shape[1]
    NB = -(-NODES // P)
    LAST = NODES - (NB - 1) * P
    NPAD = NB * P
    TILES = -(-EDGES // P)
    FULL = EDGES // P
    TAIL = EDGES - FULL * P
    G = 4
    GROUPS = -(-(TILES + NB - 1) // G)
    GROUPS += GROUPS % 2
    EC = -(-((GROUPS + 2) * G) // P)
    NT = EC * P
    CF, REST = FULL // P, FULL % P
    assert EC == CF + 1 and TILES < NT
    TOPK = max(1, NODES // 2) - 1
    PLACE = 8
    assert NT % (2 * PLACE) == 0
    XC = 7
    NX = NB // XC
    assert NX * XC == NB and D == 2 * P
    HC = H // P

    records = nc.dram_tensor("edge_records", [NT, 4 * P], f32, kind="Internal").ap()
    record_list = records.rearrange("t (e f) -> (t e) f", f=4)
    feat_in_table = nc.dram_tensor("feat_in_table", [NPAD, D], f32, kind="Internal").ap()
    a_out_tables = [nc.dram_tensor(f"a_out_table{k}", [NPAD + P, D], f32, kind="Internal").ap() for k in range(G)]
    block_list = nc.dram_tensor("pair_blocks", [NT], i32, kind="Internal").ap()

    with ExitStack() as ctx:
        def sem(name):
            return ctx.enter_context(nc.semaphore(name))

        node_h = ctx.enter_context(nc.sbuf_tensor("node_h", [P, NB, D], f32))
        node_f = ctx.enter_context(nc.sbuf_tensor("node_f", [P, NB, D], f32))
        node_a = ctx.enter_context(nc.sbuf_tensor("node_a", [P, NB, D], f32))
        WORK = 15400
        work = ctx.enter_context(nc.sbuf_tensor("work", [P, WORK], f32))
        banks = [ctx.enter_context(nc.psum_tensor(f"bank{i}", [P, 512], f32)) for i in range(8)]

        class Cut:
            def __init__(self, tensor, words, at=0):
                self.tensor, self.words, self.at = tensor, words, at

            def take(self, n):
                a = self.tensor[:, self.at:self.at + n]
                self.at += n
                assert self.at <= self.words, self.at
                return a

        fixed = Cut(work, WORK)
        ident = fixed.take(P)
        ones = fixed.take(P)
        lower = fixed.take(P)
        upper = fixed.take(P)
        number = fixed.take(NT // P)
        spare_row = fixed.take(1)
        col_b = fixed.take(P // 2).bitcast(bf16)
        flags = fixed.take(6)
        WORDS_FIXED = fixed.at
        assert WORDS_FIXED % 4 == 0

        cut = Cut(work, WORK, WORDS_FIXED)
        pair_src = cut.take(NT)
        pair_iw = cut.take(NT)
        pair_ow = cut.take(NT)
        pair_dloc = cut.take(NT // 2).bitcast(bf16)
        pair_block = cut.take(NT).bitcast(i32)
        ring_at = cut.at
        hot = cut.take(G * P).rearrange("p (u n) -> p u n", u=G)
        hot_iw = [cut.take(G * P).rearrange("p (u n) -> p u n", u=G) for _ in range(2)]
        same_ow = cut.take(G * P).rearrange("p (u n) -> p u n", u=G)
        eq = cut.take(G * P).rearrange("p (u n) -> p u n", u=G)
        mix = cut.take(G * P).rearrange("p (u n) -> p u n", u=G)
        rows = [[cut.take(D) for _ in range(G)] for _ in range(2)]
        out_rows = [cut.take(G * D) for _ in range(2)]
        gather_idx = [cut.take(G).bitcast(i32) for _ in range(2)]
        scatter_idx = [cut.take(G).bitcast(i32) for _ in range(2)]
        earlier = [cut.take(G) for _ in range(2)]
        spare = cut.take(G)

        pre = Cut(work, WORK, ring_at)
        w_io = pre.take(2 * 2 * D).rearrange("p (k n) -> p k n", k=2)
        b_io = pre.take(2 * D)
        gamma_b = pre.take(D)
        beta_b = pre.take(D)
        mean_b = pre.take(D)
        scale_b = pre.take(D)
        tmp_b = pre.take(D)
        sq = [pre.take(D) for _ in range(2)]
        hT = [pre.take(D).rearrange("p (k n) -> p k n", k=2) for _ in range(2)]
        fi_stage = [pre.take(D) for _ in range(2)]
        assert pre.at <= WORK
        stats = node_a[:, 0:2, :].rearrange("p a b -> p (a b)")[:, 0:NB * 6].rearrange("p (t s) -> p t s", t=NB)
        mv = node_a[:, 2, 0:NB * 2].rearrange("p (t s) -> p t s", t=NB)
        rstd = node_a[:, 3, 0:NB]

        edge = Cut(node_f[:, :, :].rearrange("p t d -> p (t d)"), NB * D)
        src_i = edge.take(NT).bitcast(i32).rearrange("p (c e) -> p c e", e=P)
        dst_i = edge.take(NT).bitcast(i32).rearrange("p (c e) -> p c e", e=P)
        iw_f = edge.take(NT).rearrange("p (c e) -> p c e", e=P)
        ow_f = edge.take(NT).rearrange("p (c e) -> p c e", e=P)
        keys = edge.take(NT)
        diag = edge.take(NT).rearrange("p (c e) -> p c e", e=P)
        junk = edge.take(NT)
        next_i = junk.bitcast(i32).rearrange("p (c e) -> p c e", e=P)
        key_i = edge.take(EC).bitcast(i32)
        key_f = edge.take(EC)
        tile_f = edge.take(EC)
        tile_i = edge.take(EC).bitcast(i32)
        blk_f = edge.take(EC)
        blk_i = edge.take(EC).bitcast(i32)
        blk_off = edge.take(EC)
        first_dst = edge.take(EC)
        first_i = edge.take(EC).bitcast(i32)
        wrong = edge.take(1)
        disorder = edge.take(1).bitcast(i32)
        edge2 = Cut(node_a[:, :, :].rearrange("p t d -> p (t d)"), NB * D, 4 * D)
        rec = edge2.take(EC * 4 * P).rearrange("p (c e f) -> p c e f", c=EC, f=4)

        flat = "p c e -> p (c e)"
        blk_e, place, member, count_e = junk, keys, src_i.bitcast(f32).rearrange(flat), diag.rearrange(flat)
        zero_e, at_e = iw_f.rearrange(flat), ow_f.rearrange(flat)
        place_i = dst_i.rearrange(flat)
        base = edge2.take(1)
        this_blk = edge2.take(1)
        off_e = edge2.take(1)
        edge2.take(1)
        place_rec = [edge2.take(PLACE * 4).rearrange("p (k f) -> p k f", f=4) for _ in range(2)]
        place_idx = [edge2.take(PLACE).bitcast(i32) for _ in range(2)]

        disorder_known = sem("disorder_known")
        wrong_ready = sem("wrong_ready")
        wrong_sum = sem("wrong_sum")
        records_final = sem("records_final")
        first_in = sem("first_in")
        placed = sem("placed")
        placed_out = [sem(f"placed_out{i}") for i in range(2)]
        issued_place = sem("issued_place")
        place_own = sem("place_own")
        place_cnt = sem("place_cnt")
        place_off = sem("place_off")
        const_ready = sem("const_ready")
        const_dep = sem("const_dep")
        pads_ready = sem("pads_ready")
        edges_in = sem("edges_in")
        x_in = sem("x_in")
        x_pad = sem("x_pad")
        params_in = sem("params_in")
        rec_int = sem("rec_int")
        rec_flt = sem("rec_flt")
        rec_saved = sem("rec_saved")
        diag_ready = sem("diag_ready")
        keys_row = sem("keys_row")
        dve = sem("dve")
        tiles_known = sem("tiles_known")
        blocks_known = sem("blocks_known")
        block_saved = sem("block_saved")
        block_row = sem("block_row")
        rec_back = sem("rec_back")
        dloc_ready = sem("dloc_ready")
        recT = sem("recT")
        rec_done = sem("rec_done")
        node_a_free = sem("node_a_free")
        node_a_zero = sem("node_a_zero")
        tables_zero = sem("tables_zero")
        var_ready = sem("var_ready")
        std_ready = sem("std_ready")
        xhat_ready = sem("xhat_ready")
        colsum = sem("colsum")
        centered = sem("centered")
        sq_ready = sem("sq_ready")
        sq_used = sem("sq_used")
        cvar_ready = sem("cvar_ready")
        cstd_ready = sem("cstd_ready")
        h_ready = sem("h_ready")
        hT_psum = sem("hT_psum")
        hT_ready = sem("hT_ready")
        feat_psum = sem("feat_psum")
        feat_ready = sem("feat_ready")
        fi_saved = [sem(f"fi_saved{i}") for i in range(2)]

        diag_done = sem("diag_done")
        bcast_done = sem("bcast_done")
        sel_done = sem("sel_done")
        sel_own = sem("sel_own")
        gidx_ready = sem("gidx_ready")
        sidx_ready = sem("sidx_ready")
        idx_own = sem("idx_own")
        iw_done = sem("iw_done")
        issued = sem("issued")
        post_own = sem("post_own")
        mix_psum = sem("mix_psum")
        mix_ready = sem("mix_ready")
        out_psum = sem("out_psum")
        out_ready = sem("out_ready")
        in_psum = sem("in_psum")
        in_added = sem("in_added")
        gathered = [[sem(f"gathered{h}{u}") for u in range(G)] for h in range(2)]
        scattered = [sem(f"scattered{u}") for u in range(G)]

        post = Cut(work, WORK, WORDS_FIXED)
        wx = post.take(4 * 2 * D).rearrange("p (k n) -> p k n", k=4)
        wh = post.take(2 * 2 * D).rearrange("p (k n) -> p k n", k=2)
        w1_s = post.take(2 * H).rearrange("p (k n) -> p k n", k=2)
        w2_s = post.take(HC * D).rearrange("p (k n) -> p k n", k=HC)
        bx_b = post.take(2 * D)
        b2_b = post.take(D)
        wr_b = post.take(D)
        br_b = post.take(1)
        b1_c = post.take(HC)
        w_all = post.take(NB)
        small = post.take(NB * 8).rearrange("p (k t) -> p k t", k=8)
        minus_half = post.take(1)
        st6 = [post.take(6) for _ in range(2)]
        mv2 = [post.take(2) for _ in range(2)]
        rs2 = [post.take(1) for _ in range(2)]
        u32s = post.take(8).bitcast(i32)
        cnts = post.take(2)
        acc_t = post.take(G * D).rearrange("p (k d) -> p k d", k=G)
        x_t = post.take(D)
        ao = post.take(D)
        aT = post.take(6 * P).rearrange("p (k n) -> p k n", k=6)
        gates = post.take(2 * D)
        th = post.take(2 * D)
        x1 = post.take(D)
        xn = post.take(D)
        assert post.at <= WORK, post.at
        ffn = Cut(node_h[:, :, :].rearrange("p t d -> p (t d)"), NB * D)
        hid = [ffn.take(HC * 512).rearrange("p (k n) -> p k n", k=HC) for _ in range(2)]
        y_t = [ffn.take(D) for _ in range(2)]
        o_t = [ffn.take(D) for _ in range(2)]

        main_done = sem("main_done")
        post_w = sem("post_w")
        acc_in_s = sem("acc_in_s")
        acc_used = sem("acc_used")
        xr_in = sem("xr_in")
        pool_sum = sem("pool_sum")
        ao_ready = sem("ao_ready")
        trans6 = sem("trans6")
        aT_ready = sem("aT_ready")
        gate_psum = sem("gate_psum")
        gate_in = sem("gate_in")
        gate_out = sem("gate_out")
        var2 = sem("var2")
        rs2_ready = sem("rs2_ready")
        xn_ready = sem("xn_ready")
        xnT_psum = sem("xnT_psum")
        xnT_ready = sem("xnT_ready")
        pconst = sem("pconst")
        w_done = sem("w_done")
        w_padded = sem("w_padded")
        cnt_ready = sem("cnt_ready")
        tot_ready = sem("tot_ready")
        hid_psum = sem("hid_psum")
        hid_ready = sem("hid_ready")
        y_psum = sem("y_psum")
        y_taken = sem("y_taken")
        o_ready = sem("o_ready")
        o_saved = [sem(f"o_saved{i}") for i in range(2)]

        THRESH_ROUNDS = 32
        FG = -(-NB // 4)
        nblk = [min(4, NB - 4 * g) for g in range(FG)]

        block = ctx.enter_context(nc.Block())

        @block.sync
        def _(sp):
            sp.wait_ge(pads_ready, 5)
            for a, s in ((src, src_i), (dst, dst_i), (iw, iw_f), (ow, ow_f)):
                sp.dma_start(s[:, 0:CF, :], a[0:CF * P * P].rearrange("(c q e) -> q c e", q=P, e=P)).then_inc(edges_in, 16)
                sp.dma_start(s[0:REST, CF, :], a[CF * P * P:FULL * P].rearrange("(q e) -> q e", e=P)).then_inc(edges_in, 16)
                sp.dma_start(s[REST:REST + 1, CF, 0:TAIL], a[FULL * P:EDGES].rearrange("(q e) -> q e", q=1)).then_inc(edges_in, 16)
            sp.dma_start(next_i[:, 0:CF, :], dst[1:CF * P * P + 1].rearrange("(c q e) -> q c e", q=P, e=P)).then_inc(edges_in, 16)
            sp.dma_start(next_i[0:REST, CF, :], dst[CF * P * P + 1:FULL * P + 1].rearrange("(q e) -> q e", e=P)).then_inc(edges_in, 16)
            sp.dma_start(next_i[REST:REST + 1, CF, 0:TAIL - 1], dst[FULL * P + 1:EDGES].rearrange("(q e) -> q e", q=1)).then_inc(edges_in, 16)
            sp.wait_ge(x_pad, 1)
            whole = x[0:(NB - 1) * P, :].rearrange("(t p) d -> p t d", p=P)
            for c in range(NX):
                n = min(XC, NB - 1 - c * XC)
                sp.dma_start(node_h[:, c * XC:c * XC + n, :], whole[:, c * XC:c * XC + n, :]).then_inc(x_in, 16)
            sp.dma_start(node_h[0:LAST, NB - 1, :], x[(NB - 1) * P:NODES, :]).then_inc(x_in, 16)
            sp.wait_ge(rec_int, 2)
            sp.wait_ge(rec_flt, 2)
            sp.dma_start(records.rearrange("(c q) f -> q c f", q=P), rec.rearrange("p c e f -> p c (e f)")).then_inc(rec_saved, 16)
            sp.wait_ge(records_final, 1)
            with nc.allow_non_contiguous_dma(reason="one word per tile"):
                sp.dma_start(first_dst, records[:, 1:2].rearrange("(c q) f -> q (c f)", q=P)).then_inc(first_in, 16)
            sp.wait_ge(blocks_known, 1)
            with nc.allow_non_contiguous_dma(reason="one word per pair"):
                sp.dma_start(block_list.rearrange("(c q) -> q c", q=P), blk_i).then_inc(block_saved, 16)
            sp.wait_ge(block_saved, 16)
            sp.dma_start(pair_block[0:1, :], block_list.rearrange("(a n) -> a n", a=1)).then_inc(block_row, 16)
            sp.wait_ge(node_a_zero, 1)
            for t in a_out_tables:
                sp.dma_start(t[0:NPAD, :].rearrange("(t p) d -> p t d", p=P), node_a[:, :, :]).then_inc(tables_zero, 16)
                sp.dma_start(t[NPAD:NPAD + P, :], node_a[:, 0, :]).then_inc(tables_zero, 16)
            for t in range(NB):
                sp.wait_ge(feat_ready, t + 1)
                sp.dma_start(feat_in_table[t * P:(t + 1) * P, :], fi_stage[t % 2]).then_inc(fi_saved[t % 2], 16)

            sp.wait_ge(main_done, 3)
            sp.dma_start(wx, w_x2i.rearrange("(k p) n -> p k n", p=P)).then_inc(post_w, 16)
            sp.dma_start(wh, w_h2h.rearrange("(k p) n -> p k n", p=P)).then_inc(post_w, 16)
            sp.dma_start(w1_s, w1.rearrange("(k p) n -> p k n", p=P)).then_inc(post_w, 16)
            sp.dma_start(w2_s, w2.rearrange("(k p) n -> p k n", p=P)).then_inc(post_w, 16)
            sp.dma_start(bx_b, b_x2i.partition_broadcast(P)).then_inc(post_w, 16)
            sp.dma_start(b2_b, b2.partition_broadcast(P)).then_inc(post_w, 16)
            sp.dma_start(wr_b, wr.rearrange("d o -> (o d)").partition_broadcast(P)).then_inc(post_w, 16)
            sp.dma_start(br_b, br.partition_broadcast(P)).then_inc(post_w, 16)
            with nc.allow_non_contiguous_dma(reason="b1 by hidden unit"):
                sp.dma_start(b1_c, b1.rearrange("(k p) -> p k", p=P)).then_inc(post_w, 16)
            for t in range(NB):
                n = P if t < NB - 1 else LAST
                if t:
                    sp.wait_ge(acc_used, 2 * t)
                for k in range(G):
                    sp.dma_start(acc_t[:, k, :], a_out_tables[k][t * P:(t + 1) * P, :]).then_inc(acc_in_s, 16)
                sp.dma_start(x_t[0:n, :], x[t * P:t * P + n, :]).then_inc(xr_in, 16)
            for t in range(NB):
                n = P if t < NB - 1 else LAST
                sp.wait_ge(o_ready, t + 1)
                sp.dma_start(out[t * P:t * P + n, :], o_t[t % 2][0:n, :]).then_inc(o_saved[t % 2], 16)
            sp.wait_ge(o_saved[0], 16 * ((NB + 1) // 2))
            sp.wait_ge(o_saved[1], 16 * (NB // 2))

        @block.gpsimd
        def _(pool):
            pool.memset(src_i[:, CF, :], 0).then_inc(pads_ready, 1)
            pool.memset(dst_i[:, CF, :], NPAD).then_inc(pads_ready, 1)
            pool.memset(next_i[:, CF, :], NPAD).then_inc(pads_ready, 1)
            pool.memset(iw_f[:, CF, :], 0.0).then_inc(pads_ready, 1)
            pool.memset(ow_f[:, CF, :], 0.0).then_inc(pads_ready, 1)
            pool.memset(node_h[:, NB - 1, :], 0.0).then_inc(x_pad, 1)
            pool.memset(ident, 0.0).then_inc(const_dep, 1)
            pool.memset(lower, 1.0).then_inc(const_dep, 1)
            pool.memset(upper, 1.0).then_inc(const_dep, 1)
            pool.memset(ones, 1.0).then_inc(const_ready, 1)
            pool.iota(number, pattern=[[P, EC]], base=0, channel_multiplier=1,
                      allow_small_or_imprecise_dtypes=True).then_inc(const_ready, 1)
            pool.iota(spare_row, pattern=[[0, 1]], base=NPAD, channel_multiplier=1,
                      allow_small_or_imprecise_dtypes=True).then_inc(const_ready, 1)
            pool.iota(col_b, pattern=[[1, P]], base=0, channel_multiplier=0,
                      allow_small_or_imprecise_dtypes=True).then_inc(const_ready, 1)
            pool.wait_ge(const_dep, 3)
            pool.affine_select(out=ident, in_=ident, pattern=[[-1, P]], compare_op=ALU.not_equal, fill=1.0,
                               base=0, channel_multiplier=1).then_inc(const_ready, 1)
            pool.affine_select(out=lower, in_=lower, pattern=[[-1, P]], compare_op=ALU.is_gt, fill=0.0,
                               base=0, channel_multiplier=1).then_inc(const_ready, 1)
            pool.affine_select(out=upper, in_=upper, pattern=[[1, P]], compare_op=ALU.is_gt, fill=0.0,
                               base=0, channel_multiplier=-1).then_inc(const_ready, 1)
            pool.wait_ge(rec_saved, 16)
            pool.wait_ge(disorder_known, 1)
            with pool.If(pool.value_load(disorder[0:1, 0:1], min_val=0, max_val=1) > 0):
                for half in range(2):
                    pool.wait_ge(placed, half + 1)
                    for k in range(PLACE):
                        pool.indirect_dma_start(record_list, bass.IndirectOffsetOnAxis(place_idx[half][:, k:k + 1], 0),
                                                place_rec[half][:, k, :], None).then_inc(placed_out[half], 16)
                with pool.Fori(1, NT // (2 * PLACE)) as step:
                    for half in range(2):
                        pool.wait_ge(placed, step * 2 + half + 1)
                        pool.sem_inc(issued_place, 1)
                        for k in range(PLACE):
                            pool.indirect_dma_start(record_list, bass.IndirectOffsetOnAxis(place_idx[half][:, k:k + 1], 0),
                                                    place_rec[half][:, k, :], None).then_inc(placed_out[half], 16)
                for half in range(2):
                    pool.wait_ge(placed_out[half], 16 * PLACE * (NT // (2 * PLACE)))
            pool.memset(flags[:, 4:5], 0.0).then_inc(records_final, 1)
            pool.wait_ge(tiles_known, 1)
            for c in range(EC):
                pool.indirect_dma_start(rec[:, c, :, :].rearrange("p e f -> p (e f)"), None, records,
                                        bass.IndirectOffsetOnAxis(tile_i[:, c:c + 1], 0)).then_inc(rec_back, 16)
            pool.wait_ge(node_a_free, 1)
            pool.memset(node_a[:, :, :], 0.0).then_inc(node_a_zero, 1)

            pool.wait_ge(tables_zero, 32 * G)
            pool.wait_ge(fi_saved[0], 16 * ((NB + 1) // 2))
            pool.wait_ge(fi_saved[1], 16 * (NB // 2))

            def gather(g, h, u, first):
                pool.wait_ge(gidx_ready, g + 1)
                if not first:
                    pool.wait_ge(in_psum, G * (g - 2) + u + 1)
                pool.sem_inc(issued, 1)
                pool.indirect_dma_start(rows[h][u], None, feat_in_table,
                                        bass.IndirectOffsetOnAxis(gather_idx[h][:, u:u + 1], 0)).then_inc(gathered[h][u], 16)

            def scatter(g, h, u, first):
                pool.wait_ge(sidx_ready, g + 1)
                pool.wait_ge(out_ready, G * g + u + 1)
                if not first:
                    pool.wait_ge(scattered[u], 16 * g)
                pool.sem_inc(issued, 1)
                pool.indirect_dma_start(a_out_tables[u], bass.IndirectOffsetOnAxis(scatter_idx[h][:, u:u + 1], 0),
                                        out_rows[h][:, u * D:(u + 1) * D], None, compute_op=ALU.add).then_inc(scattered[u], 16)

            def turn_of(g, h, first_gather, first_scatter):
                for u in range(G):
                    gather(g, h, u, first_gather)
                    scatter(g - 1, 1 - h, u, first_scatter)

            for u in range(G):
                gather(0, 0, u, True)
            turn_of(1, 1, True, True)
            with pool.Fori(1, GROUPS // 2) as turn:
                for h in range(2):
                    turn_of(turn * 2 + h, h, False, False)
            for u in range(G):
                scatter(GROUPS - 1, 1, u, False)
            for u in range(G):
                pool.wait_ge(scattered[u], 16 * GROUPS)
            pool.memset(flags[:, 2:3], 0.0).then_inc(main_done, 1)

            pool.wait_ge(main_done, 3)
            pool.memset(minus_half, -0.5).then_inc(pconst, 1)
            pool.wait_ge(pconst, 1)
            for t in range(NB):
                pool.wait_ge(acc_in_s, 16 * G * (t + 1))
                pool.tensor_tensor(out=acc_t[:, 0, :], in0=acc_t[:, 0, :], in1=acc_t[:, 1, :], op=ALU.add).then_inc(pool_sum, 1)
                pool.tensor_tensor(out=acc_t[:, 2, :], in0=acc_t[:, 2, :], in1=acc_t[:, 3, :], op=ALU.add).then_inc(pool_sum, 1)
                pool.wait_ge(var2, t + 1)
                pool.tensor_tensor(out=rs2[t % 2], in0=mv2[t % 2][:, 1:2], in1=minus_half, op=ALU.pow).then_inc(rs2_ready, 1)
            pool.wait_ge(w_done, 1)
            pool.affine_select(out=w_all, in_=w_all, pattern=[[-P, NB]], compare_op=ALU.is_ge, fill=-3.0e38,
                               base=NODES - 1, channel_multiplier=-1).then_inc(w_padded, 1)

        @block.scalar
        def _(act):
            with nc.allow_non_contiguous_dma(reason="parameters"):
                act.dma_start(w_io[:, :, 0:D], w_in.rearrange("(k p) n -> p k n", p=P)).then_inc(params_in, 16)
                act.dma_start(w_io[:, :, D:2 * D], w_out.rearrange("(k p) n -> p k n", p=P)).then_inc(params_in, 16)
                act.dma_start(b_io[:, 0:D], b_in.partition_broadcast(P)).then_inc(params_in, 16)
                act.dma_start(b_io[:, D:2 * D], b_out.partition_broadcast(P)).then_inc(params_in, 16)
                act.dma_start(gamma_b, gamma.partition_broadcast(P)).then_inc(params_in, 16)
                act.dma_start(beta_b, beta.partition_broadcast(P)).then_inc(params_in, 16)
            act.wait_ge(edges_in, 16 * 15)
            nc.scalar.activation(rec[:, :, :, 2], iw_f, ACT.Copy).then_inc(rec_flt, 1)
            nc.scalar.activation(rec[:, :, :, 3], ow_f, ACT.Copy).then_inc(rec_flt, 1)
            for c in range(EC):
                act.wait_ge(recT, c + 1)
                b = banks[4 + c % 4]
                s = slice(c * P, (c + 1) * P)
                nc.scalar.activation(pair_src[:, s], b[:, 0:P], ACT.Copy)
                nc.scalar.activation(pair_dloc[:, s], b[:, P:2 * P], ACT.Copy)
                nc.scalar.activation(pair_iw[:, s], b[:, 2 * P:3 * P], ACT.Copy)
                nc.scalar.activation(pair_ow[:, s], b[:, 3 * P:4 * P], ACT.Copy).then_inc(rec_done, 1)
            act.wait_ge(var_ready, 1)
            nc.scalar.activation(rstd, rstd, ACT.Sqrt).then_inc(std_ready, 1)
            for t in range(NB):
                act.wait_ge(centered, t // XC + 1)
                if t >= 2:
                    act.wait_ge(sq_used, t - 1)
                nc.scalar.activation(sq[t % 2], node_h[:, t, :], ACT.Square).then_inc(sq_ready, 1)
            act.wait_ge(cvar_ready, 1)
            nc.scalar.activation(tmp_b, tmp_b, ACT.Sqrt).then_inc(cstd_ready, 1)
            for t in range(NB):
                act.wait_ge(hT_psum, t + 1)
                if t >= 2:
                    act.wait_ge(feat_psum, t - 1)
                nc.scalar.activation(hT[t % 2], banks[t % 2][:, 0:D].rearrange("p (k n) -> p k n", k=2),
                                     ACT.Copy).then_inc(hT_ready, 1)

            def group(g, h, first):
                act.wait_ge(mix_psum, g + 1)
                if not first:
                    act.wait_ge(out_psum, G * g)
                nc.scalar.activation(mix, banks[1][:, :].rearrange("p (u n) -> p u n", u=G), ACT.Copy).then_inc(mix_ready, 1)
                for u in range(0, G, 2):
                    act.wait_ge(out_psum, G * g + u + 2)
                    if first is False:
                        act.wait_ge(scattered[u], 16 * (g - 1))
                        act.wait_ge(scattered[u + 1], 16 * (g - 1))
                    nc.scalar.activation(out_rows[h][:, u * D:(u + 2) * D], banks[2 + u // 2][:, :],
                                         ACT.Copy).then_inc(out_ready, 2)

            group(0, 0, True)
            group(1, 1, None)
            with act.Fori(1, GROUPS // 2) as turn:
                for h in range(2):
                    group(turn * 2 + h, h, False)

            for t in range(NB):
                act.wait_ge(trans6, t + 1)
                if t:
                    act.wait_ge(gate_psum, t)
                nc.scalar.activation(aT[:, 0:4, :], banks[0][:, :].rearrange("p (k n) -> p k n", k=4), ACT.Copy)
                nc.scalar.activation(aT[:, 4:6, :], banks[1][:, 0:2 * P].rearrange("p (k n) -> p k n", k=2),
                                     ACT.Copy).then_inc(aT_ready, 1)
                act.wait_ge(gate_in, t + 1)
                nc.scalar.activation(th[:, 0:D], gates[:, 0:D], ACT.Tanh, scale=0.5)
                nc.scalar.activation(th[:, D:2 * D], gates[:, D:2 * D], ACT.Tanh).then_inc(gate_out, 1)
                act.wait_ge(xnT_psum, t + 1)
                nc.scalar.activation(node_a[:, t, :], banks[3][:, 0:D], ACT.Copy).then_inc(xnT_ready, 1)
            k = 0
            for g in range(FG):
                n = nblk[g] * P
                for c in range(HC):
                    act.wait_ge(hid_psum, k + 1)
                    if g >= 2 and c == 0:
                        act.wait_ge(y_psum, 4 * (g - 1))
                    nc.scalar.activation(hid[g % 2][:, c, 0:n], banks[4 + k % 2][:, 0:n], ACT.Gelu_apprx_tanh,
                                         bias=b1_c[:, c:c + 1]).then_inc(hid_ready, 1)
                    k += 1

        @block.vector
        def _(v):
            chain = [0]

            def own(ins):
                chain[0] += 1
                ins.then_inc(dve, 1)
                v.wait_ge(dve, chain[0])

            v.wait_ge(edges_in, 16 * 15)
            nc.vector.tensor_copy(rec[:, :, :, 0], src_i).then_inc(rec_int, 1)
            nc.vector.tensor_copy(rec[:, :, :, 1], dst_i).then_inc(rec_int, 1)
            v.wait_ge(rec_int, 2)
            blk_now, blk_next = keys.bitcast(i32), count_e.bitcast(i32)
            own(nc.vector.tensor_scalar(blk_now, dst_i.rearrange(flat), 7, None, ALU.logical_shift_right))
            own(nc.vector.tensor_scalar(blk_next, next_i.rearrange(flat), 7, None, ALU.logical_shift_right))
            own(nc.vector.tensor_tensor(member, blk_next, blk_now, ALU.is_lt))
            nc.vector.tensor_reduce(wrong, member, AX.X, ALU.max).then_inc(wrong_ready, 1)
            v.wait_ge(wrong_sum, 1)
            nc.vector.tensor_scalar(disorder, banks[4][:, 0:1], 0.0, None, ALU.is_gt).then_inc(disorder_known, 1)
            v.wait_ge(disorder_known, 1)
            with v.If(v.value_load(disorder[0:1, 0:1], min_val=0, max_val=1) > 0):
                v.wait_ge(rec_flt, 2)
                nc.vector.memset(zero_e, 0.0).then_inc(place_own, 1)
                nc.vector.tensor_copy(blk_e, blk_now).then_inc(place_own, 1)
                v.wait_ge(place_own, 2)
                nc.vector.memset(place, 0.0).then_inc(place_own, 1)
                nc.vector.memset(base, -1.0).then_inc(place_own, 1)
                nc.vector.memset(this_blk, 0.0).then_inc(place_own, 1)
                v.wait_ge(place_own, 5)
                OWN = 6
                with v.Fori(0, NB + 1) as b:
                    nc.vector.tensor_scalar(member, blk_e, this_blk, None, ALU.is_equal).then_inc(place_own, 1)
                    v.wait_ge(place_own, b * OWN + 6)
                    nc.vector.tensor_tensor_scan(count_e, member, zero_e, 0.0, ALU.add, ALU.add).then_inc(place_cnt, 1)
                    v.wait_ge(place_off, b + 1)
                    nc.vector.tensor_tensor(off_e, banks[4][:, 0:1], base, ALU.add).then_inc(place_own, 1)
                    v.wait_ge(place_own, b * OWN + 7)
                    nc.vector.scalar_tensor_tensor(at_e, count_e, off_e, member, ALU.add, ALU.mult).then_inc(place_own, 1)
                    v.wait_ge(place_own, b * OWN + 8)
                    nc.vector.tensor_tensor(place, place, at_e, ALU.add).then_inc(place_own, 1)
                    nc.vector.tensor_tensor(base, banks[4][:, 1:2], base, ALU.add).then_inc(place_own, 1)
                    nc.vector.tensor_scalar(this_blk, this_blk, 1.0, None, ALU.add).then_inc(place_own, 1)
                    v.wait_ge(place_own, b * OWN + 11)
                nc.vector.tensor_copy(place_i, place).then_inc(place_own, 1)
                v.wait_ge(place_own, (NB + 1) * OWN + 6)
                rec_flat = rec.rearrange("p c e f -> p (c e) f")

                def stage(step, half):
                    at = (step * 2 + half) * PLACE
                    nc.vector.tensor_scalar(place_idx[half], place_i[:, bass.ds(at, PLACE)], 0.0, None, ALU.add)
                    nc.vector.tensor_scalar(place_rec[half], rec_flat[:, bass.ds(at, PLACE), :], 0.0, None,
                                            ALU.add).then_inc(placed, 1)

                for half in range(2):
                    stage(0, half)
                with v.Fori(1, NT // (2 * PLACE)) as step:
                    for half in range(2):
                        v.wait_ge(placed_out[half], step * (16 * PLACE))
                        stage(step, half)
            v.wait_ge(first_in, 16)
            own(nc.vector.tensor_copy(first_i, first_dst))
            own(nc.vector.tensor_scalar(key_i, first_i, 7, None, ALU.logical_shift_right))
            v.wait_ge(const_ready, 7)
            own(nc.vector.tensor_tensor(key_f, key_i, number, ALU.add))
            own(nc.vector.memset(key_f[0:1, 0:1], 0.0))
            nc.vector.tensor_tensor(diag, ident.unsqueeze(1).to_broadcast([P, EC, P]),
                                    key_f.unsqueeze(2).to_broadcast([P, EC, P]), ALU.mult).then_inc(diag_ready, 1)
            v.wait_ge(keys_row, 1)
            for b in range(4):
                n = min(512, NT - 512 * b)
                ins = nc.vector.tensor_copy(keys[:, 512 * b:512 * b + n], banks[b][:, 0:n])
            own(ins)
            for c in range(EC):
                own(nc.vector.tensor_scalar(junk, keys, number[:, c:c + 1], 0.0, ALU.is_le, ALU.add,
                                            accum_out=tile_f[:, c:c + 1]))
            own(nc.vector.tensor_scalar(tile_f, tile_f, -1.0, None, ALU.add))
            nc.vector.tensor_copy(tile_i, tile_f).then_inc(tiles_known, 1)
            own(nc.vector.tensor_tensor(blk_f, number, tile_f, ALU.subtract))
            nc.vector.tensor_scalar(blk_i, blk_f, float(NB - 1), None, ALU.min).then_inc(blocks_known, 1)
            own(nc.vector.tensor_scalar(blk_off, blk_f, float(P), None, ALU.mult))
            v.wait_ge(rec_back, 16 * EC)
            nc.vector.tensor_tensor(rec[:, :, :, 1], rec[:, :, :, 1], blk_off.unsqueeze(2).to_broadcast([P, EC, P]),
                                    ALU.subtract).then_inc(dloc_ready, 1)

            v.wait_ge(x_in, 16 * (NX + 1))
            for t in range(NB):
                ins = nc.vector.bn_stats(stats[:, t, :], node_h[:, t, :])
            own(ins)
            for t in range(NB):
                ins = nc.vector.bn_aggr(mv[:, t, :], stats[:, t, :])
            own(ins)
            nc.vector.tensor_scalar(rstd, mv[:, :, 1], EPS, None, ALU.add).then_inc(var_ready, 1)
            v.wait_ge(std_ready, 1)
            own(nc.vector.reciprocal(rstd, rstd))
            for t in range(NB):
                nc.vector.tensor_scalar(node_h[:, t, :], node_h[:, t, :], mv[:, t, 0:1], rstd[:, t:t + 1],
                                        ALU.subtract, ALU.mult).then_inc(xhat_ready, 1)
            v.wait_ge(params_in, 16 * 6)
            v.wait_ge(colsum, 1)
            own(nc.vector.tensor_scalar(mean_b, banks[0][:, 0:D], 1.0 / NODES, None, ALU.mult))
            v.wait_ge(xhat_ready, NB)
            for c in range(NX):
                s = node_h[:, c * XC:(c + 1) * XC, :]
                nc.vector.tensor_tensor(s, s, mean_b.unsqueeze(1).to_broadcast([P, XC, D]),
                                        ALU.subtract).then_inc(centered, 1)
            v.wait_ge(colsum, 2)
            nc.vector.tensor_scalar(tmp_b, banks[1][:, 0:D], 1.0 / NODES, EPS, ALU.mult, ALU.add).then_inc(cvar_ready, 1)
            v.wait_ge(cstd_ready, 1)
            own(nc.vector.reciprocal(scale_b, tmp_b))
            own(nc.vector.tensor_tensor(scale_b, scale_b, gamma_b, ALU.mult))
            v.wait_ge(sq_ready, NB)
            for c in range(NX):
                s = node_h[:, c * XC:(c + 1) * XC, :]
                own(nc.vector.tensor_tensor(s, s, scale_b.unsqueeze(1).to_broadcast([P, XC, D]), ALU.mult))
                nc.vector.tensor_tensor(s, s, beta_b.unsqueeze(1).to_broadcast([P, XC, D]),
                                        ALU.add).then_inc(h_ready, 1)
            v.wait_ge(rec_done, EC)
            nc.vector.memset(flags[:, 0:1], 0.0).then_inc(node_a_free, 1)
            for t in range(NB):
                v.wait_ge(feat_psum, t + 1)
                b = banks[2 + t % 2]
                if t >= 2:
                    v.wait_ge(fi_saved[t % 2], 16 * (t // 2))
                nc.vector.tensor_tensor(node_f[:, t, :], b[:, D:2 * D], b_io[:, D:2 * D], ALU.add)
                nc.vector.tensor_tensor(fi_stage[t % 2], b[:, 0:D], b_io[:, 0:D], ALU.add).then_inc(feat_ready, 1)

            v.wait_ge(fi_saved[0], 16 * ((NB + 1) // 2))
            v.wait_ge(fi_saved[1], 16 * (NB // 2))
            v.wait_ge(node_a_zero, 1)

            def cols(a, g):
                return a[:, bass.ds(g * G, G)]

            def wide(a):
                return a.unsqueeze(2).to_broadcast([P, G, P])

            def rows4(a):
                return a.unsqueeze(1).to_broadcast([P, G, P])

            def spread(g, first):
                if not first:
                    v.wait_ge(sel_own, 4 * g)
                nc.vector.tensor_tensor(eq, rows4(ident), wide(cols(pair_src, g)), ALU.mult).then_inc(diag_done, 1)

            def select(g, first):
                if not first:
                    v.wait_ge(mix_psum, g)
                    v.wait_ge(iw_done, g)
                nc.vector.tensor_tensor(hot, rows4(col_b), wide(cols(pair_dloc, g)), ALU.is_equal).then_inc(sel_own, 1)
                v.wait_ge(bcast_done, g + 1)
                nc.vector.tensor_tensor(eq, banks[0][:, :].rearrange("p (u n) -> p u n", u=G), wide(cols(pair_src, g)),
                                        ALU.is_equal).then_inc(sel_own, 1)
                v.wait_ge(sel_own, 4 * g + 2)
                nc.vector.tensor_tensor(same_ow, eq, wide(cols(pair_ow, g)), ALU.mult).then_inc(sel_done, 1)
                v.wait_ge(sel_done, g + 1)
                nc.vector.tensor_tensor(eq, eq, rows4(lower), ALU.mult).then_inc(sel_own, 1)
                v.wait_ge(sel_own, 4 * g + 3)

            def reduce(g, h):
                nc.vector.tensor_reduce(earlier[h], eq, AX.X, ALU.max).then_inc(sel_own, 1)
                v.wait_ge(sel_own, 4 * g + 4)

            def weigh(g, h, first):
                if not first:
                    v.wait_ge(in_psum, G * (g - 1))
                nc.vector.tensor_tensor(hot_iw[h], hot, wide(cols(pair_iw, g)), ALU.mult).then_inc(iw_done, 1)
                nc.vector.tensor_scalar(gather_idx[h], cols(pair_src, g), 0.0, None, ALU.add).then_inc(gidx_ready, 1)

            def index(g, h, first):
                if not first:
                    for u in range(G):
                        v.wait_ge(scattered[u], 16 * (g - 1))
                nc.vector.tensor_scalar(spare, earlier[h], spare_row[:, 0:1], None, ALU.mult).then_inc(idx_own, 1)
                v.wait_ge(idx_own, g + 1)
                nc.vector.tensor_tensor(scatter_idx[h], spare, cols(pair_src, g), ALU.max).then_inc(sidx_ready, 1)

            def add(g, blocks):
                for u in range(G):
                    v.wait_ge(in_psum, G * g + u // 2 * 2 + 2)
                    if not (isinstance(g, int) and g == 0 and u == 0):
                        v.wait_ge(in_added, G * g + u)
                    a = node_a[:, bass.ds(blocks[u], 1), :].rearrange("p a d -> p (a d)")
                    nc.vector.tensor_tensor(a, a, banks[4 + u // 2][:, (u % 2) * D:(u % 2 + 1) * D],
                                            ALU.add).then_inc(in_added, 1)

            def load_blocks(g):
                return nc.values_load_multi_w_load_instructions(
                    pair_block[0:1, bass.ds(g * G, G)], engines=[mybir.EngineType.DVE], min_val=0, max_val=NB - 1,
                    skip_runtime_bounds_check_because="block numbers lie in the range by construction")[1]

            def turn_of(g, h, start):
                if start != 0:
                    blocks = load_blocks(g - 1)
                select(g + 1, False)
                reduce(g + 1, 1 - h)
                spread(g + 2, False)
                weigh(g + 1, 1 - h, start == 0)
                index(g, h, start < 2)
                if start != 0:
                    add(g - 1, blocks)

            v.wait_ge(rec_done, EC)
            v.wait_ge(block_row, 16)
            spread(0, True)
            select(0, True)
            reduce(0, 0)
            spread(1, False)
            weigh(0, 0, True)
            turn_of(0, 0, 0)
            turn_of(1, 1, 1)
            with v.Fori(1, GROUPS // 2) as turn:
                for h in range(2):
                    turn_of(turn * 2 + h, h, 2)
            add(GROUPS - 1, load_blocks(GROUPS - 1))
            nc.vector.memset(flags[:, 1:2], 0.0).then_inc(main_done, 1)

            v.wait_ge(post_w, 16 * 9)
            v.wait_ge(main_done, 3)
            post = [0]

            def link(ins):
                post[0] += 1
                ins.then_inc(post_own, 1)
                v.wait_ge(post_own, post[0])

            for t in range(NB):
                v.wait_ge(pool_sum, 2 * t + 2)
                if t:
                    v.wait_ge(trans6, t)
                nc.vector.tensor_tensor(ao, acc_t[:, 0, :], acc_t[:, 2, :], ALU.add).then_inc(ao_ready, 1)
                v.wait_ge(gate_psum, t + 1)
                nc.vector.tensor_tensor(gates, banks[2][:, :], bx_b, ALU.add).then_inc(gate_in, 1)
                v.wait_ge(gate_out, t + 1)
                new = th[:, D:2 * D]
                link(nc.vector.tensor_tensor(x1, node_h[:, t, :], new, ALU.subtract))
                link(nc.vector.scalar_tensor_tensor(x1, th[:, 0:D], 1.0, x1, ALU.add, ALU.mult))
                link(nc.vector.scalar_tensor_tensor(x1, x1, 0.5, new, ALU.mult, ALU.add))
                v.wait_ge(xr_in, 16 * (t + 1))
                n = P if t < NB - 1 else LAST
                link(nc.vector.tensor_tensor(x1[0:n, :], x1[0:n, :], x_t[0:n, :], ALU.add))
                link(nc.vector.bn_stats(st6[t % 2], x1))
                link(nc.vector.bn_aggr(mv2[t % 2], st6[t % 2]))
                nc.vector.tensor_scalar(mv2[t % 2][:, 1:2], mv2[t % 2][:, 1:2], EPS, None, ALU.add).then_inc(var2, 1)
                v.wait_ge(rs2_ready, t + 1)
                if t:
                    v.wait_ge(xnT_psum, t)
                nc.vector.tensor_scalar(xn, x1, mv2[t % 2][:, 0:1], rs2[t % 2], ALU.subtract, ALU.mult).then_inc(xn_ready, 1)
                v.wait_ge(xn_ready, t + 1)
                link(nc.vector.scalar_tensor_tensor(gates[:, 0:D], xn, 1.0, wr_b, ALU.mult, ALU.mult,
                                                    accum_out=w_all[:, t:t + 1]))
                nc.vector.tensor_tensor(node_f[:, t, :], x1, xn, ALU.add).then_inc(acc_used, 2)
            link(nc.vector.tensor_scalar(w_all, w_all, br_b, None, ALU.add))
            nc.vector.memset(flags[:, 3:4], 0.0).then_inc(w_done, 1)
            v.wait_ge(w_padded, 1)
            cur, cand, msk, bits = (u32s[:, k:k + 1] for k in range(4))
            link(nc.vector.memset(cur, 0))
            for r in range(THRESH_ROUNDS):
                bit = 1 << (31 - r)
                bit = bit - (1 << 32) if r == 0 else bit
                link(nc.vector.tensor_scalar(cand, cur, bit, None, ALU.bitwise_or))
                link(nc.vector.tensor_scalar(msk, cand, 31, None, ALU.arith_shift_right))
                link(nc.vector.tensor_scalar(msk, msk, -1, -(1 << 31), ALU.bitwise_xor, ALU.bitwise_or))
                link(nc.vector.tensor_tensor(bits, cand, msk, ALU.bitwise_xor))
                nc.vector.tensor_scalar(small[:, 0, :], w_all, bits.bitcast(f32), 0.0, ALU.is_ge, ALU.add,
                                        accum_out=cnts[:, 0:1]).then_inc(cnt_ready, 1)
                v.wait_ge(tot_ready, r + 1)
                link(nc.vector.tensor_scalar(msk, banks[6][:, 0:1], float(TOPK), -1.0, ALU.is_ge, ALU.mult))
                link(nc.vector.tensor_scalar(msk, msk, bit, None, ALU.bitwise_and))
                link(nc.vector.tensor_tensor(cur, cur, msk, ALU.bitwise_or))
            link(nc.vector.tensor_scalar(msk, cur, 31, None, ALU.arith_shift_right))
            link(nc.vector.tensor_scalar(msk, msk, -1, -(1 << 31), ALU.bitwise_xor, ALU.bitwise_or))
            link(nc.vector.tensor_tensor(bits, cur, msk, ALU.bitwise_xor))
            thr = bits.bitcast(f32)
            above, equal, incl, rank, pick = (small[:, k, :] for k in range(1, 6))
            link(nc.vector.tensor_scalar(above, w_all, thr, 0.0, ALU.is_gt, ALU.add, accum_out=cnts[:, 0:1]))
            nc.vector.tensor_scalar(equal, w_all, thr, None, ALU.is_equal).then_inc(cnt_ready, 1)
            v.wait_ge(tot_ready, THRESH_ROUNDS + 1)
            link(nc.vector.tensor_copy(pick, banks[6][:, 64:64 + NB]))
            link(nc.vector.memset(small[:, 6, :], 0.0))
            link(nc.vector.tensor_tensor_scan(incl, pick, small[:, 6, :], 0.0, ALU.add, ALU.add))
            link(nc.vector.tensor_tensor(incl, incl, pick, ALU.subtract))
            link(nc.vector.tensor_tensor(rank, incl, banks[6][:, 128:128 + NB], ALU.add))
            link(nc.vector.tensor_scalar(rank, rank, banks[6][:, 0:1], None, ALU.add))
            link(nc.vector.scalar_tensor_tensor(pick, rank, float(TOPK), equal, ALU.is_lt, ALU.mult))
            link(nc.vector.tensor_tensor(pick, pick, above, ALU.add))
            link(nc.vector.tensor_tensor(w_all, w_all, pick, ALU.mult))
            for t in range(NB):
                v.wait_ge(y_psum, t + 1)
                b = banks[2 + t % 2][:, 0:D]
                nc.vector.tensor_tensor(y_t[t % 2], b, b2_b, ALU.add).then_inc(y_taken, 1)
                v.wait_ge(y_taken, t + 1)
                if t >= 2:
                    v.wait_ge(o_saved[t % 2], 16 * (t // 2))
                nc.vector.scalar_tensor_tensor(o_t[t % 2], y_t[t % 2], w_all[:, t:t + 1], node_f[:, t, :],
                                               ALU.mult, ALU.add).then_inc(o_ready, 1)

        @block.tensor
        def _(pe):
            mm, tr = nc.tensor.matmul, nc.tensor.transpose
            pe.wait_ge(const_ready, 7)
            pe.wait_ge(wrong_ready, 1)
            mm(banks[4][:, 0:1], ones, wrong, start=True, stop=True).then_inc(wrong_sum, 1)
            pe.wait_ge(disorder_known, 1)
            with pe.If(pe.value_load(disorder[0:1, 0:1], min_val=0, max_val=1) > 0):
                with pe.Fori(0, NB + 1) as b:
                    pe.wait_ge(place_cnt, b + 1)
                    mm(banks[4][:, 0:1], upper, count_e[:, NT - 1:NT], start=True, stop=True)
                    mm(banks[4][:, 1:2], ones, count_e[:, NT - 1:NT], start=True, stop=True).then_inc(place_off, 1)
            pe.wait_ge(diag_ready, 1)
            diags = diag.rearrange(flat)
            for b in range(4):
                n = min(512, NT - 512 * b)
                ins = mm(banks[b][:, 0:n], ones, diags[:, 512 * b:512 * b + n], start=True, stop=True)
            ins.then_inc(keys_row, 1)
            pe.wait_ge(dloc_ready, 1)
            for c in range(EC):
                if c >= 4:
                    pe.wait_ge(rec_done, c - 3)
                for f in range(4):
                    ins = tr(banks[4 + c % 4][:, f * P:(f + 1) * P], rec[:, c, :, f], ident)
                ins.then_inc(recT, 1)
            for t in range(NB):
                n = P if t < NB - 1 else LAST
                pe.wait_ge(xhat_ready, t + 1)
                ins = mm(banks[0][:, 0:D], ones[0:n, :], node_h[0:n, t, :], start=t == 0, stop=t == NB - 1)
            ins.then_inc(colsum, 1)
            for t in range(NB):
                n = P if t < NB - 1 else LAST
                pe.wait_ge(sq_ready, t + 1)
                ins = mm(banks[1][:, 0:D], ones[0:n, :], sq[t % 2][0:n, :], start=t == 0, stop=t == NB - 1)
                ins.then_inc(sq_used, 1)
            pe.wait_ge(sq_used, NB)
            pe.nop().then_inc(colsum, 1)
            pe.wait_ge(params_in, 16 * 6)
            pe.wait_ge(cvar_ready, 1)
            for t in range(NB):
                pe.wait_ge(h_ready, t // XC + 1)
                if t >= 2:
                    pe.wait_ge(hT_ready, t - 1)
                tr(banks[t % 2][:, 0:P], node_h[:, t, 0:P], ident)
                tr(banks[t % 2][:, P:2 * P], node_h[:, t, P:2 * P], ident).then_inc(hT_psum, 1)
                pe.wait_ge(hT_ready, t + 1)
                if t >= 2:
                    pe.wait_ge(feat_ready, t - 1)
                mm(banks[2 + t % 2][:, :], hT[t % 2][:, 0, :], w_io[:, 0, :], start=True, stop=False)
                mm(banks[2 + t % 2][:, :], hT[t % 2][:, 1, :], w_io[:, 1, :], start=False, stop=True).then_inc(feat_psum, 1)

            pe.wait_ge(feat_ready, NB)
            pe.wait_ge(block_row, 16)

            def src_rows(g):
                pe.wait_ge(diag_done, g + 1)
                mm(banks[0][:, :], ones, eq.rearrange("p u n -> p (u n)"), start=True, stop=True).then_inc(bcast_done, 1)

            def sums(g, count, start):
                h = (start + 1) % 2
                for u in range(G):
                    if u == 0:
                        pe.wait_ge(iw_done, g + 1)
                    pe.wait_ge(gathered[h][u], 16 * count)
                    if u % 2 == 0 and not (isinstance(g, int) and g == 0):
                        pe.wait_ge(in_added, G * (g - 1) + u + 2)
                    mm(banks[4 + u // 2][:, (u % 2) * D:(u % 2 + 1) * D], hot_iw[h][:, u, :], rows[h][u],
                       start=True, stop=True).then_inc(in_psum, 1)

            def group(turn, h, first):
                g = turn * 2 + h
                blocks = nc.values_load_multi_w_load_instructions(
                    pair_block[0:1, bass.ds(g * G, G)], engines=[mybir.EngineType.PE], min_val=0, max_val=NB - 1,
                    skip_runtime_bounds_check_because="block numbers lie in the range by construction")[1]
                pe.wait_ge(sel_done, g + 1)
                if not first:
                    pe.wait_ge(mix_ready, g)
                for u in range(G):
                    ins = mm(banks[1][:, u * P:(u + 1) * P], hot[:, u, :], same_ow[:, u, :], start=True, stop=True)
                ins.then_inc(mix_psum, 1)
                if not first:
                    sums(g - 1, turn + h, h)
                pe.wait_ge(mix_ready, g + 1)
                for u in range(G):
                    if not first and u % 2 == 0:
                        pe.wait_ge(out_ready, G * (g - 1) + u + 2)
                    f = node_f[:, bass.ds(blocks[u], 1), :].rearrange("p a d -> p (a d)")
                    mm(banks[2 + u // 2][:, (u % 2) * D:(u % 2 + 1) * D], mix[:, u, :], f,
                       start=True, stop=True).then_inc(out_psum, 1)
                src_rows(g + 2)

            src_rows(0)
            src_rows(1)
            group(0, 0, True)
            group(0, 1, False)
            with pe.Fori(1, GROUPS // 2) as turn:
                for h in range(2):
                    group(turn, h, False)
            sums(GROUPS - 1, GROUPS // 2, 0)
            pe.wait_ge(in_psum, G * GROUPS)
            pe.nop().then_inc(main_done, 1)

            pe.wait_ge(main_done, 3)
            pe.wait_ge(post_w, 16 * 9)
            for t in range(NB):
                if t:
                    pe.wait_ge(aT_ready, t)
                for k in range(2):
                    tr(banks[0][:, k * P:(k + 1) * P], node_a[:, t, k * P:(k + 1) * P], ident)
                    tr(banks[1][:, k * P:(k + 1) * P], node_h[:, t, k * P:(k + 1) * P], ident)
                pe.wait_ge(ao_ready, t + 1)
                for k in range(2):
                    ins = tr(banks[0][:, (2 + k) * P:(3 + k) * P], ao[:, k * P:(k + 1) * P], ident)
                ins.then_inc(trans6, 1)
                pe.wait_ge(aT_ready, t + 1)
                if t:
                    pe.wait_ge(gate_in, t)
                for k in range(6):
                    ins = mm(banks[2][:, :], aT[:, k, :], wx[:, k, :] if k < 4 else wh[:, k - 4, :],
                             start=k == 0, stop=k == 5)
                ins.then_inc(gate_psum, 1)
                pe.wait_ge(xn_ready, t + 1)
                if t:
                    pe.wait_ge(xnT_ready, t)
                for k in range(2):
                    ins = tr(banks[3][:, k * P:(k + 1) * P], xn[:, k * P:(k + 1) * P], ident)
                ins.then_inc(xnT_psum, 1)
            for r in range(THRESH_ROUNDS):
                pe.wait_ge(cnt_ready, r + 1)
                mm(banks[6][:, 0:1], ones, cnts[:, 0:1], start=True, stop=True).then_inc(tot_ready, 1)
            pe.wait_ge(cnt_ready, THRESH_ROUNDS + 1)
            mm(banks[6][:, 0:1], ones, cnts[:, 0:1], start=True, stop=True)
            mm(banks[6][:, 64:64 + NB], ones, small[:, 2, :], start=True, stop=True)
            mm(banks[6][:, 128:128 + NB], upper, small[:, 2, :], start=True, stop=True).then_inc(tot_ready, 1)
            pe.wait_ge(xnT_ready, NB)
            k = 0
            y = 0
            for g in range(FG):
                n = nblk[g]
                for c in range(HC):
                    if k >= 2:
                        pe.wait_ge(hid_ready, k - 1)
                    for kk in range(2):
                        ins = mm(banks[4 + k % 2][:, 0:n * P], w1_s[:, kk, c * P:(c + 1) * P],
                                 node_a[:, 4 * g:4 * g + n, kk * P:(kk + 1) * P], start=kk == 0, stop=kk == 1)
                    ins.then_inc(hid_psum, 1)
                    k += 1
                pe.wait_ge(hid_ready, k)
                for b in range(n):
                    if y >= 2:
                        pe.wait_ge(y_taken, y - 1)
                    for c in range(HC):
                        ins = mm(banks[2 + y % 2][:, 0:D], hid[g % 2][:, c, b * P:(b + 1) * P],
                                 w2_s[:, c, :], start=c == 0, stop=c == HC - 1)
                    ins.then_inc(y_psum, 1)
                    y += 1


def kernel(x, src, dst, edge_weight, edge_weight_n2, L0_gnn_gamma, L0_gnn_beta, L0_gnn_W_in, L0_gnn_b_in,
           L0_gnn_W_out, L0_gnn_b_out, L0_gnn_W_x2i, L0_gnn_b_x2i, L0_gnn_W_h2h, L0_ffn_attention_mask,
           L0_ffn_wr, L0_ffn_br, L0_ffn_w1, L0_ffn_b1, L0_ffn_w2, L0_ffn_b2):
    import concourse.bacc as bacc
    from concourse.bass_utils import run_bass_kernel_spmd
    nc = bacc.Bacc("TRN2", target_bir_lowering=False, num_devices=1)
    given = dict(x=x, src=src, dst=dst, iw=edge_weight, ow=edge_weight_n2, gamma=L0_gnn_gamma, beta=L0_gnn_beta,
                 w_in=L0_gnn_W_in, b_in=L0_gnn_b_in, w_out=L0_gnn_W_out, b_out=L0_gnn_b_out, w_x2i=L0_gnn_W_x2i,
                 b_x2i=L0_gnn_b_x2i, w_h2h=L0_gnn_W_h2h, wr=L0_ffn_wr, br=L0_ffn_br, w1=L0_ffn_w1, b1=L0_ffn_b1,
                 w2=L0_ffn_w2, b2=L0_ffn_b2)
    arrays, args = {}, []
    for name, a in given.items():
        a = np.ascontiguousarray(a)
        arrays[f"{name}_dram"] = a
        args.append(nc.dram_tensor(f"{name}_dram", a.shape, mybir.dt.from_np(a.dtype), kind="ExternalInput").ap())
    args.append(nc.dram_tensor("out_dram", x.shape, mybir.dt.float32, kind="ExternalOutput").ap())
    gnn_ffn(nc, *args)
    return run_bass_kernel_spmd(nc, [arrays], core_ids=[0]).results[0]["out_dram"]
```

```python
import numpy as np
import concourse.bass as bass
from concourse import mybir
from contextlib import ExitStack

P = 128
EPS = 1e-5


def gnn_ffn(nc, x, src, dst, iw, ow, gamma, beta, w_in, b_in, w_out, b_out, w_x2i, b_x2i, w_h2h,
            wr, br, w1, b1, w2, b2, out):
    f32, bf16, i32 = mybir.dt.float32, mybir.dt.bfloat16, mybir.dt.int32
    ALU, ACT, AX = mybir.AluOpType, mybir.ActivationFunctionType, mybir.AxisListType

    NODES, D = x.shape
    EDGES = src.shape[0]
    H = w1.shape[1]
    NB = -(-NODES // P)
    LAST = NODES - (NB - 1) * P
    NPAD = NB * P
    TILES = -(-EDGES // P)
    FULL = EDGES // P
    TAIL = EDGES - FULL * P
    G = 4
    GROUPS = -(-(TILES + NB - 1) // G)
    GROUPS += GROUPS % 2
    EC = -(-((GROUPS + 2) * G) // P)
    NT = EC * P
    CF, REST = FULL // P, FULL % P
    assert EC == CF + 1 and TILES < NT
    TOPK = max(1, NODES // 2) - 1
    PLACE = 8
    assert NT % (2 * PLACE) == 0
    XC = 7
    NX = NB // XC
    assert NX * XC == NB and D == 2 * P
    HC = H // P
    KEYS_AT = 4 * XC
    COUNTS_FIRST = 5
    REC_AT = 3 * XC + 3

    records = nc.dram_tensor("edge_records", [NT, 4 * P], f32, kind="Internal").ap()
    record_list = records.rearrange("t (e f) -> (t e) f", f=4)
    feat_in_table = nc.dram_tensor("feat_in_table", [NPAD, D], f32, kind="Internal").ap()
    a_out_tables = [nc.dram_tensor(f"a_out_table{k}", [NPAD + P, D], f32, kind="Internal").ap() for k in range(G)]
    block_list = nc.dram_tensor("pair_blocks", [NT], i32, kind="Internal").ap()

    with ExitStack() as ctx:
        def sem(name):
            return ctx.enter_context(nc.semaphore(name))

        node_h = ctx.enter_context(nc.sbuf_tensor("node_h", [P, NB, D], f32))
        node_f = ctx.enter_context(nc.sbuf_tensor("node_f", [P, NB, D], f32))
        node_a = ctx.enter_context(nc.sbuf_tensor("node_a", [P, NB, D], f32))
        WORK = 15576
        work = ctx.enter_context(nc.sbuf_tensor("work", [P, WORK], f32))
        banks = [ctx.enter_context(nc.psum_tensor(f"bank{i}", [P, 512], f32)) for i in range(8)]

        class Cut:
            def __init__(self, tensor, words, at=0):
                self.tensor, self.words, self.at = tensor, words, at

            def take(self, n):
                a = self.tensor[:, self.at:self.at + n]
                self.at += n
                assert self.at <= self.words, self.at
                return a

        fixed = Cut(work, WORK)
        ident = fixed.take(P)
        ones = fixed.take(P)
        lower = fixed.take(P)
        upper = fixed.take(P)
        number = fixed.take(NT // P)
        spare_row = fixed.take(1)
        col_b = fixed.take(P // 2).bitcast(bf16)
        flags = fixed.take(6)
        WORDS_FIXED = fixed.at
        assert WORDS_FIXED % 4 == 0

        cut = Cut(work, WORK, WORDS_FIXED)
        pair_src = cut.take(NT)
        pair_iw = cut.take(NT)
        pair_ow = cut.take(NT)
        pair_dloc = cut.take(NT // 2).bitcast(bf16)
        pair_block = cut.take(NT).bitcast(i32)
        ring_at = cut.at
        hot = cut.take(G * P).rearrange("p (u n) -> p u n", u=G)
        hot_iw = [cut.take(G * P).rearrange("p (u n) -> p u n", u=G) for _ in range(2)]
        same_ow = cut.take(G * P).rearrange("p (u n) -> p u n", u=G)
        eq = cut.take(G * P).rearrange("p (u n) -> p u n", u=G)
        mix = cut.take(G * P).rearrange("p (u n) -> p u n", u=G)
        rows = [[cut.take(D) for _ in range(G)] for _ in range(2)]
        out_rows = [cut.take(G * D) for _ in range(2)]
        gather_idx = [cut.take(G).bitcast(i32) for _ in range(2)]
        scatter_idx = [cut.take(G).bitcast(i32) for _ in range(2)]
        earlier = [cut.take(G) for _ in range(2)]
        spare = cut.take(G)

        pre = Cut(work, WORK, ring_at)
        w_io = pre.take(2 * 2 * D).rearrange("p (k n) -> p k n", k=2)
        b_io = pre.take(2 * D)
        gamma_b = pre.take(D)
        beta_b = pre.take(D)
        mean_b = pre.take(D)
        scale_b = pre.take(D)
        tmp_b = pre.take(D)
        sq = [pre.take(D) for _ in range(2)]
        hT = [pre.take(D).rearrange("p (k n) -> p k n", k=2) for _ in range(2)]
        fi_stage = [pre.take(D) for _ in range(2)]
        zero_row = pre.take(D)
        assert pre.at <= WORK
        stats = node_a[:, 0:2, :].rearrange("p a b -> p (a b)")[:, 0:NB * 6].rearrange("p (t s) -> p t s", t=NB)
        mv = node_a[:, 2, 0:NB * 2].rearrange("p (t s) -> p t s", t=NB)
        rstd = node_a[:, 3, 0:NB]
        shift = node_a[:, 3, NB:2 * NB]

        edge = Cut(node_f[:, :, :].rearrange("p t d -> p (t d)"), NB * D)
        src_i = edge.take(NT).bitcast(i32).rearrange("p (c e) -> p c e", e=P)
        dst_i = edge.take(NT).bitcast(i32).rearrange("p (c e) -> p c e", e=P)
        iw_f = edge.take(NT).rearrange("p (c e) -> p c e", e=P)
        ow_f = edge.take(NT).rearrange("p (c e) -> p c e", e=P)
        keys = edge.take(NT)
        diag = edge.take(NT).rearrange("p (c e) -> p c e", e=P)
        junk = edge.take(NT)
        next_i = junk.bitcast(i32).rearrange("p (c e) -> p c e", e=P)
        key_i = edge.take(EC).bitcast(i32)
        key_f = edge.take(EC)
        tile_f = edge.take(EC)
        blk_f = edge.take(EC)
        first_dst = edge.take(EC)
        first_i = edge.take(EC).bitcast(i32)
        wrong = edge.take(1)
        disorder = edge.take(1).bitcast(i32)
        edge2 = Cut(node_a[:, :, :].rearrange("p t d -> p (t d)"), NB * D, 4 * D)
        rec = edge2.take(EC * 4 * P).rearrange("p (c e f) -> p c e f", c=EC, f=4)
        tile_i = edge2.take(EC).bitcast(i32)
        blk_i = edge2.take(EC).bitcast(i32)
        blk_off = edge2.take(EC)

        flat = "p c e -> p (c e)"
        blk_e, place, member, count_e = junk, keys, src_i.bitcast(f32).rearrange(flat), diag.rearrange(flat)
        zero_e, at_e = iw_f.rearrange(flat), ow_f.rearrange(flat)
        place_i = dst_i.rearrange(flat)
        base = edge2.take(1)
        this_blk = edge2.take(1)
        off_e = edge2.take(1)
        edge2.take(1)
        place_rec = [edge2.take(PLACE * 4).rearrange("p (k f) -> p k f", f=4) for _ in range(2)]
        place_idx = [edge2.take(PLACE).bitcast(i32) for _ in range(2)]

        disorder_known = sem("disorder_known")
        wrong_ready = sem("wrong_ready")
        wrong_sum = sem("wrong_sum")
        records_final = sem("records_final")
        first_in = sem("first_in")
        placed = sem("placed")
        placed_out = [sem(f"placed_out{i}") for i in range(2)]
        issued_place = sem("issued_place")
        place_own = sem("place_own")
        place_cnt = sem("place_cnt")
        place_off = sem("place_off")
        const_ready = sem("const_ready")
        const_dep = sem("const_dep")
        pads_ready = sem("pads_ready")
        edges_in = sem("edges_in")
        x_in = [sem(f"x_in{c}") for c in range(NX)]
        x_pad = sem("x_pad")
        params_in = sem("params_in")
        rec_int = sem("rec_int")
        rec_flt = sem("rec_flt")
        rec_saved = sem("rec_saved")
        diag_ready = sem("diag_ready")
        keys_row = sem("keys_row")
        dve = sem("dve")
        tiles_known = sem("tiles_known")
        blocks_known = sem("blocks_known")
        block_saved = sem("block_saved")
        block_row = sem("block_row")
        rec_back = sem("rec_back")
        dloc_ready = sem("dloc_ready")
        recT = sem("recT")
        rec_done = sem("rec_done")
        node_a_zero = sem("node_a_zero")
        zero_ready = sem("zero_ready")
        tables_zero = sem("tables_zero")
        var_ready = sem("var_ready")
        std_ready = sem("std_ready")
        shift_ready = sem("shift_ready")
        xhat_ready = sem("xhat_ready")
        xhat_act = sem("xhat_act")
        colsum = sem("colsum")
        centered = sem("centered")
        sq_ready = sem("sq_ready")
        sq_used = sem("sq_used")
        cvar_ready = sem("cvar_ready")
        cstd_ready = sem("cstd_ready")
        h_ready = sem("h_ready")
        hT_psum = sem("hT_psum")
        hT_ready = sem("hT_ready")
        feat_psum = sem("feat_psum")
        feat_ready = sem("feat_ready")
        fi_saved = [sem(f"fi_saved{i}") for i in range(2)]

        diag_done = sem("diag_done")
        bcast_done = sem("bcast_done")
        sel_done = sem("sel_done")
        sel_own = sem("sel_own")
        gidx_ready = sem("gidx_ready")
        sidx_ready = sem("sidx_ready")
        idx_own = sem("idx_own")
        iw_done = sem("iw_done")
        issued = sem("issued")
        post_own = sem("post_own")
        mix_psum = sem("mix_psum")
        mix_ready = sem("mix_ready")
        out_psum = sem("out_psum")
        out_ready = sem("out_ready")
        in_psum = sem("in_psum")
        in_added = sem("in_added")
        gathered = [[sem(f"gathered{h}{u}") for u in range(G)] for h in range(2)]
        scattered = [sem(f"scattered{u}") for u in range(G)]

        BT = 2
        BATCHES = -(-NB // BT)
        in_batch = [min(BT, NB - BT * b) for b in range(BATCHES)]
        post = Cut(work, WORK, WORDS_FIXED)
        bx_b = post.take(2 * D)
        b2_b = post.take(D)
        wr_b = post.take(D)
        br_b = post.take(1)
        b1_c = post.take(HC)
        w_all = post.take(NB)
        small = post.take(NB * 8).rearrange("p (k t) -> p k t", k=8)
        minus_half = post.take(BT)
        st6 = post.take(BT * 6).rearrange("p (i s) -> p i s", i=BT)
        mv2 = post.take(BT * 2).rearrange("p (i s) -> p i s", i=BT)
        rs2 = post.take(BT)
        u32s = post.take(8).bitcast(i32)
        cnts = post.take(2)
        wx = post.take(4 * 2 * D).rearrange("p (k n) -> p k n", k=4)
        wh = post.take(2 * 2 * D).rearrange("p (k n) -> p k n", k=2)
        acc_t = [post.take(G * BT * D).rearrange("p (k i d) -> p k i d", k=G, i=BT) for _ in range(2)]
        x_t = [post.take(BT * D).rearrange("p (i d) -> p i d", i=BT) for _ in range(2)]
        aT = [post.take(BT * 6 * P).rearrange("p (i k n) -> p i k n", i=BT, k=6) for _ in range(2)]
        gates = post.take(BT * 2 * D).rearrange("p (i n) -> p i n", i=BT)
        x1 = post.take(BT * D).rearrange("p (i d) -> p i d", i=BT)
        xn = post.take(BT * D).rearrange("p (i d) -> p i d", i=BT)
        assert post.at <= WORK, post.at
        w1_s = acc_t[0].rearrange("p k i d -> p (k i d)").rearrange("p (k n) -> p k n", k=2)
        w2_s = acc_t[1].rearrange("p k i d -> p (k i d)").rearrange("p (k n) -> p k n", k=HC)
        ffn = Cut(node_h[:, :, :].rearrange("p t d -> p (t d)"), NB * D)
        hid = [ffn.take(HC * 512).rearrange("p (k n) -> p k n", k=HC) for _ in range(2)]
        y_t = [ffn.take(D) for _ in range(2)]
        o_t = [ffn.take(D) for _ in range(2)]

        main_done = sem("main_done")
        post_w = sem("post_w")
        acc_in = [sem(f"acc_in{i}") for i in range(2)]
        x_again = [sem(f"x_again{i}") for i in range(2)]
        inputs_used = sem("inputs_used")
        ffn_w = sem("ffn_w")
        pool_sum = sem("pool_sum")
        ao_ready = sem("ao_ready")
        trans6 = sem("trans6")
        aT_ready = sem("aT_ready")
        gate_psum = sem("gate_psum")
        gate_in = sem("gate_in")
        gate_out = sem("gate_out")
        var2 = sem("var2")
        rs2_ready = sem("rs2_ready")
        xn_ready = sem("xn_ready")
        xnT_psum = sem("xnT_psum")
        xnT_ready = sem("xnT_ready")
        pconst = sem("pconst")
        w_done = sem("w_done")
        w_padded = sem("w_padded")
        cnt_ready = sem("cnt_ready")
        tot_ready = sem("tot_ready")
        hid_psum = sem("hid_psum")
        hid_ready = sem("hid_ready")
        y_psum = sem("y_psum")
        y_taken = sem("y_taken")
        o_ready = sem("o_ready")
        o_saved = [sem(f"o_saved{i}") for i in range(2)]

        THRESH_ROUNDS = 32
        FG = -(-NB // 4)
        nblk = [min(4, NB - 4 * g) for g in range(FG)]

        block = ctx.enter_context(nc.Block())

        @block.sync
        def _(sp):
            sp.wait_ge(x_pad, 1)
            whole = x[0:(NB - 1) * P, :].rearrange("(t p) d -> p t d", p=P)
            for c in range(NX):
                n = min(XC, NB - 1 - c * XC)
                sp.dma_start(node_h[:, c * XC:c * XC + n, :], whole[:, c * XC:c * XC + n, :]).then_inc(x_in[c], 16)
            sp.dma_start(node_h[0:LAST, NB - 1, :], x[(NB - 1) * P:NODES, :]).then_inc(x_in[NX - 1], 16)
            sp.wait_ge(pads_ready, 5)
            for a, s in ((src, src_i), (dst, dst_i), (iw, iw_f), (ow, ow_f)):
                sp.dma_start(s[:, 0:CF, :], a[0:CF * P * P].rearrange("(c q e) -> q c e", q=P, e=P)).then_inc(edges_in, 16)
                sp.dma_start(s[0:REST, CF, :], a[CF * P * P:FULL * P].rearrange("(q e) -> q e", e=P)).then_inc(edges_in, 16)
                sp.dma_start(s[REST:REST + 1, CF, 0:TAIL], a[FULL * P:EDGES].rearrange("(q e) -> q e", q=1)).then_inc(edges_in, 16)
            sp.dma_start(next_i[:, 0:CF, :], dst[1:CF * P * P + 1].rearrange("(c q e) -> q c e", q=P, e=P)).then_inc(edges_in, 16)
            sp.dma_start(next_i[0:REST, CF, :], dst[CF * P * P + 1:FULL * P + 1].rearrange("(q e) -> q e", e=P)).then_inc(edges_in, 16)
            sp.dma_start(next_i[REST:REST + 1, CF, 0:TAIL - 1], dst[FULL * P + 1:EDGES].rearrange("(q e) -> q e", q=1)).then_inc(edges_in, 16)
            sp.wait_ge(rec_int, 2)
            sp.wait_ge(rec_flt, 2)
            sp.dma_start(records.rearrange("(c q) f -> q c f", q=P), rec.rearrange("p c e f -> p c (e f)")).then_inc(rec_saved, 16)
            sp.wait_ge(records_final, 1)
            with nc.allow_non_contiguous_dma(reason="one word per tile"):
                sp.dma_start(first_dst, records[:, 1:2].rearrange("(c q) f -> q (c f)", q=P)).then_inc(first_in, 16)
            sp.wait_ge(zero_ready, 1)
            for t in a_out_tables[:G // 2]:
                sp.dma_start(t.rearrange("(t p) d -> p t d", p=P),
                             zero_row.unsqueeze(1).to_broadcast([P, NB + 1, D])).then_inc(tables_zero, 16)
            for t in range(NB + 1):
                if t < NB:
                    sp.wait_ge(feat_ready, t + 1)
                    sp.dma_start(feat_in_table[t * P:(t + 1) * P, :], fi_stage[t % 2]).then_inc(fi_saved[t % 2], 16)
                for a in a_out_tables[G // 2:]:
                    sp.dma_start(a[t * P:(t + 1) * P, :], zero_row).then_inc(tables_zero, 16)

            sp.wait_ge(main_done, 3)
            sp.dma_start(wx, w_x2i.rearrange("(k p) n -> p k n", p=P)).then_inc(post_w, 16)
            sp.dma_start(wh, w_h2h.rearrange("(k p) n -> p k n", p=P)).then_inc(post_w, 16)
            sp.dma_start(bx_b, b_x2i.partition_broadcast(P)).then_inc(post_w, 16)
            sp.dma_start(b2_b, b2.partition_broadcast(P)).then_inc(post_w, 16)
            sp.dma_start(wr_b, wr.rearrange("d o -> (o d)").partition_broadcast(P)).then_inc(post_w, 16)
            sp.dma_start(br_b, br.partition_broadcast(P)).then_inc(post_w, 16)
            with nc.allow_non_contiguous_dma(reason="b1 by hidden unit"):
                sp.dma_start(b1_c, b1.rearrange("(k p) -> p k", p=P)).then_inc(post_w, 16)
            for b in range(BATCHES + 1):
                if b < BATCHES:
                    t, n, s = BT * b, in_batch[b], b % 2
                    if b >= 2:
                        sp.wait_ge(trans6, b - 1)
                    for k in range(G):
                        sp.dma_start(acc_t[s][:, k, 0:n, :], a_out_tables[k][t * P:(t + n) * P, :].rearrange(
                            "(i p) d -> p i d", p=P)).then_inc(acc_in[s], 16)
                if b:
                    t, n, s = BT * (b - 1), in_batch[b - 1], (b - 1) % 2
                    if b >= 3:
                        sp.wait_ge(inputs_used, b - 2)
                    if t + n < NB:
                        sp.dma_start(x_t[s][:, 0:n, :], x[t * P:(t + n) * P, :].rearrange(
                            "(i p) d -> p i d", p=P)).then_inc(x_again[s], 16)
                    else:
                        sp.dma_start(x_t[s][0:LAST, n - 1, :], x[(NB - 1) * P:NODES, :]).then_inc(x_again[s], 16)
            sp.wait_ge(inputs_used, BATCHES)
            sp.dma_start(w1_s, w1.rearrange("(k p) n -> p k n", p=P)).then_inc(ffn_w, 16)
            sp.dma_start(w2_s, w2.rearrange("(k p) n -> p k n", p=P)).then_inc(ffn_w, 16)
            for t in range(NB):
                n = P if t < NB - 1 else LAST
                sp.wait_ge(o_ready, t + 1)
                sp.dma_start(out[t * P:t * P + n, :], o_t[t % 2][0:n, :]).then_inc(o_saved[t % 2], 16)
            sp.wait_ge(o_saved[0], 16 * ((NB + 1) // 2))
            sp.wait_ge(o_saved[1], 16 * (NB // 2))

        @block.gpsimd
        def _(pool):
            pool.memset(src_i[:, CF, :], 0).then_inc(pads_ready, 1)
            pool.memset(dst_i[:, CF, :], NPAD).then_inc(pads_ready, 1)
            pool.memset(next_i[:, CF, :], NPAD).then_inc(pads_ready, 1)
            pool.memset(iw_f[:, CF, :], 0.0).then_inc(pads_ready, 1)
            pool.memset(ow_f[:, CF, :], 0.0).then_inc(pads_ready, 1)
            pool.memset(node_h[:, NB - 1, :], 0.0).then_inc(x_pad, 1)
            pool.memset(zero_row, 0.0).then_inc(zero_ready, 1)
            pool.memset(ident, 0.0).then_inc(const_dep, 1)
            pool.memset(lower, 1.0).then_inc(const_dep, 1)
            pool.memset(upper, 1.0).then_inc(const_dep, 1)
            pool.memset(ones, 1.0).then_inc(const_ready, 1)
            pool.iota(number, pattern=[[P, EC]], base=0, channel_multiplier=1,
                      allow_small_or_imprecise_dtypes=True).then_inc(const_ready, 1)
            pool.iota(spare_row, pattern=[[0, 1]], base=NPAD, channel_multiplier=1,
                      allow_small_or_imprecise_dtypes=True).then_inc(const_ready, 1)
            pool.iota(col_b, pattern=[[1, P]], base=0, channel_multiplier=0,
                      allow_small_or_imprecise_dtypes=True).then_inc(const_ready, 1)
            pool.wait_ge(const_dep, 3)
            pool.affine_select(out=ident, in_=ident, pattern=[[-1, P]], compare_op=ALU.not_equal, fill=1.0,
                               base=0, channel_multiplier=1).then_inc(const_ready, 1)
            pool.affine_select(out=lower, in_=lower, pattern=[[-1, P]], compare_op=ALU.is_gt, fill=0.0,
                               base=0, channel_multiplier=1).then_inc(const_ready, 1)
            pool.affine_select(out=upper, in_=upper, pattern=[[1, P]], compare_op=ALU.is_gt, fill=0.0,
                               base=0, channel_multiplier=-1).then_inc(const_ready, 1)
            pool.wait_ge(rec_saved, 16)
            pool.wait_ge(disorder_known, 1)
            with pool.If(pool.value_load(disorder[0:1, 0:1], min_val=0, max_val=1) > 0):
                for half in range(2):
                    pool.wait_ge(placed, half + 1)
                    for k in range(PLACE):
                        pool.indirect_dma_start(record_list, bass.IndirectOffsetOnAxis(place_idx[half][:, k:k + 1], 0),
                                                place_rec[half][:, k, :], None).then_inc(placed_out[half], 16)
                with pool.Fori(1, NT // (2 * PLACE)) as step:
                    for half in range(2):
                        pool.wait_ge(placed, step * 2 + half + 1)
                        pool.sem_inc(issued_place, 1)
                        for k in range(PLACE):
                            pool.indirect_dma_start(record_list, bass.IndirectOffsetOnAxis(place_idx[half][:, k:k + 1], 0),
                                                    place_rec[half][:, k, :], None).then_inc(placed_out[half], 16)
                for half in range(2):
                    pool.wait_ge(placed_out[half], 16 * PLACE * (NT // (2 * PLACE)))
            pool.memset(flags[:, 4:5], 0.0).then_inc(records_final, 1)
            pool.wait_ge(tiles_known, 1)
            for c in range(EC):
                pool.indirect_dma_start(rec[:, c, :, :].rearrange("p e f -> p (e f)"), None, records,
                                        bass.IndirectOffsetOnAxis(tile_i[:, c:c + 1], 0)).then_inc(rec_back, 16)
            pool.wait_ge(rec_done, EC)
            pool.wait_ge(block_saved, 16)
            pool.memset(node_a[:, :, :], 0.0).then_inc(node_a_zero, 1)

            pool.wait_ge(tables_zero, 16 * (G // 2) * (NB + 2))
            pool.wait_ge(fi_saved[0], 16 * ((NB + 1) // 2))
            pool.wait_ge(fi_saved[1], 16 * (NB // 2))

            def gather(g, h, u, first):
                pool.wait_ge(gidx_ready, g + 1)
                if not first:
                    pool.wait_ge(in_psum, G * (g - 2) + u + 1)
                pool.sem_inc(issued, 1)
                pool.indirect_dma_start(rows[h][u], None, feat_in_table,
                                        bass.IndirectOffsetOnAxis(gather_idx[h][:, u:u + 1], 0)).then_inc(gathered[h][u], 16)

            def scatter(g, h, u, first):
                pool.wait_ge(sidx_ready, g + 1)
                pool.wait_ge(out_ready, G * g + u + 1)
                if not first:
                    pool.wait_ge(scattered[u], 16 * g)
                pool.sem_inc(issued, 1)
                pool.indirect_dma_start(a_out_tables[u], bass.IndirectOffsetOnAxis(scatter_idx[h][:, u:u + 1], 0),
                                        out_rows[h][:, u * D:(u + 1) * D], None, compute_op=ALU.add).then_inc(scattered[u], 16)

            def turn_of(g, h, first_gather, first_scatter):
                for u in range(G):
                    gather(g, h, u, first_gather)
                    scatter(g - 1, 1 - h, u, first_scatter)

            for u in range(G):
                gather(0, 0, u, True)
            turn_of(1, 1, True, True)
            with pool.Fori(1, GROUPS // 2) as turn:
                for h in range(2):
                    turn_of(turn * 2 + h, h, False, False)
            for u in range(G):
                scatter(GROUPS - 1, 1, u, False)
            for u in range(G):
                pool.wait_ge(scattered[u], 16 * GROUPS)
            pool.memset(flags[:, 2:3], 0.0).then_inc(main_done, 1)

            pool.wait_ge(main_done, 3)
            pool.memset(minus_half, -0.5).then_inc(pconst, 1)
            pool.wait_ge(pconst, 1)

            def inverse_std(b):
                n = in_batch[b]
                pool.wait_ge(var2, b + 1)
                pool.tensor_tensor(out=rs2[:, 0:n], in0=mv2[:, 0:n, 1], in1=minus_half[:, 0:n],
                                   op=ALU.pow).then_inc(rs2_ready, 1)

            def pair_sums(b):
                n, s = in_batch[b], b % 2
                pool.wait_ge(acc_in[s], 16 * G * (b // 2 + 1))
                for k in (0, 2):
                    pool.tensor_tensor(out=acc_t[s][:, k, 0:n, :], in0=acc_t[s][:, k, 0:n, :],
                                       in1=acc_t[s][:, k + 1, 0:n, :], op=ALU.add).then_inc(pool_sum, 1)

            pair_sums(0)
            pair_sums(1)
            for b in range(BATCHES):
                if b + 2 < BATCHES:
                    pair_sums(b + 2)
                inverse_std(b)
            pool.wait_ge(w_done, 1)
            pool.affine_select(out=w_all, in_=w_all, pattern=[[-P, NB]], compare_op=ALU.is_ge, fill=-3.0e38,
                               base=NODES - 1, channel_multiplier=-1).then_inc(w_padded, 1)

        @block.scalar
        def _(act):
            with nc.allow_non_contiguous_dma(reason="parameters"):
                act.dma_start(w_io[:, :, 0:D], w_in.rearrange("(k p) n -> p k n", p=P)).then_inc(params_in, 16)
                act.dma_start(w_io[:, :, D:2 * D], w_out.rearrange("(k p) n -> p k n", p=P)).then_inc(params_in, 16)
                act.dma_start(b_io[:, 0:D], b_in.partition_broadcast(P)).then_inc(params_in, 16)
                act.dma_start(b_io[:, D:2 * D], b_out.partition_broadcast(P)).then_inc(params_in, 16)
                act.dma_start(gamma_b, gamma.partition_broadcast(P)).then_inc(params_in, 16)
                act.dma_start(beta_b, beta.partition_broadcast(P)).then_inc(params_in, 16)
            act.wait_ge(var_ready, 1)
            nc.scalar.activation(rstd, rstd, ACT.Sqrt).then_inc(std_ready, 1)
            act.wait_ge(shift_ready, 1)
            for t in range(1, NB, 2):
                nc.scalar.activation(node_h[:, t, :], node_h[:, t, :], ACT.Identity, bias=shift[:, t:t + 1],
                                     scale=rstd[:, t:t + 1]).then_inc(xhat_act, 1)
            act.wait_ge(edges_in, 16 * 15)
            nc.scalar.activation(rec[:, :, :, 2], iw_f, ACT.Copy).then_inc(rec_flt, 1)
            nc.scalar.activation(rec[:, :, :, 3], ow_f, ACT.Copy).then_inc(rec_flt, 1)
            for t in range(NB):
                act.wait_ge(centered, t // XC + 1)
                if t >= 2:
                    act.wait_ge(sq_used, t - 1)
                nc.scalar.activation(sq[t % 2], node_h[:, t, :], ACT.Square).then_inc(sq_ready, 1)
            act.wait_ge(cvar_ready, 1)
            nc.scalar.activation(tmp_b, tmp_b, ACT.Sqrt).then_inc(cstd_ready, 1)
            for t in range(NB):
                if t == REC_AT - 2 * XC // 3:
                    act.wait_ge(blocks_known, 1)
                    with nc.allow_non_contiguous_dma(reason="one word per pair"):
                        act.dma_start(block_list.rearrange("(c q) -> q c", q=P), blk_i).then_inc(block_saved, 16)
                if t == REC_AT:
                    act.wait_ge(block_saved, 16)
                    act.dma_start(pair_block[0:1, :], block_list.rearrange("(a n) -> a n", a=1)).then_inc(block_row, 16)
                    for c in range(EC):
                        act.wait_ge(recT, c + 1)
                        b = banks[4 + c % 4]
                        s = slice(c * P, (c + 1) * P)
                        nc.scalar.activation(pair_src[:, s], b[:, 0:P], ACT.Copy)
                        nc.scalar.activation(pair_dloc[:, s], b[:, P:2 * P], ACT.Copy)
                        nc.scalar.activation(pair_iw[:, s], b[:, 2 * P:3 * P], ACT.Copy)
                        nc.scalar.activation(pair_ow[:, s], b[:, 3 * P:4 * P], ACT.Copy).then_inc(rec_done, 1)
                act.wait_ge(hT_psum, t + 1)
                if t >= 2:
                    act.wait_ge(feat_psum, t - 1)
                nc.scalar.activation(hT[t % 2], banks[t % 2][:, 0:D].rearrange("p (k n) -> p k n", k=2),
                                     ACT.Copy).then_inc(hT_ready, 1)

            def weigh(g, h, first):
                act.wait_ge(sel_own, 4 * g + 1)
                if not first:
                    act.wait_ge(in_psum, G * (g - 1))
                for u in range(G):
                    ins = nc.scalar.activation(hot_iw[h][:, u, :], hot[:, u, :], ACT.Copy,
                                               scale=pair_iw[:, bass.ds(g * G + u, 1)])
                ins.then_inc(iw_done, 1)

            def group(g, h, first):
                act.wait_ge(mix_psum, g + 1)
                if not first:
                    act.wait_ge(out_psum, G * g)
                nc.scalar.activation(mix, banks[1][:, :].rearrange("p (u n) -> p u n", u=G), ACT.Copy).then_inc(mix_ready, 1)
                weigh(g + 1, 1 - h, first is True)
                for u in range(0, G, 2):
                    act.wait_ge(out_psum, G * g + u + 2)
                    if first is False:
                        act.wait_ge(scattered[u], 16 * (g - 1))
                        act.wait_ge(scattered[u + 1], 16 * (g - 1))
                    nc.scalar.activation(out_rows[h][:, u * D:(u + 2) * D], banks[2 + u // 2][:, :],
                                         ACT.Copy).then_inc(out_ready, 2)

            act.wait_ge(fi_saved[0], 16 * ((NB + 1) // 2))
            act.wait_ge(fi_saved[1], 16 * (NB // 2))
            weigh(0, 0, True)
            group(0, 0, True)
            group(1, 1, None)
            with act.Fori(1, GROUPS // 2) as turn:
                for h in range(2):
                    group(turn * 2 + h, h, False)

            def to_aT(b):
                act.wait_ge(trans6, b + 1)
                if b >= 2:
                    act.wait_ge(gate_psum, b - 1)
                f = aT[b % 2].rearrange("p i k n -> p (i k n)")
                for q in range(-(-in_batch[b] * 6 // 4)):
                    w = min(4, in_batch[b] * 6 - 4 * q) * P
                    ins = nc.scalar.activation(f[:, 512 * q:512 * q + w], banks[q][:, 0:w], ACT.Copy)
                ins.then_inc(aT_ready, 1)

            def to_xnT(b):
                n = in_batch[b]
                act.wait_ge(xnT_psum, b + 1)
                nc.scalar.activation(node_a[:, BT * b:BT * b + n, :].rearrange("p i d -> p (i d)"),
                                     banks[7][:, 0:n * D], ACT.Copy).then_inc(xnT_ready, 1)

            to_aT(0)
            for b in range(BATCHES):
                n = in_batch[b]
                if b + 1 < BATCHES:
                    to_aT(b + 1)
                act.wait_ge(gate_in, b + 1)
                nc.scalar.activation(gates[:, 0:n, 0:D], gates[:, 0:n, 0:D], ACT.Tanh, scale=0.5)
                nc.scalar.activation(gates[:, 0:n, D:2 * D], gates[:, 0:n, D:2 * D], ACT.Tanh).then_inc(gate_out, 1)
                if b:
                    to_xnT(b - 1)
            to_xnT(BATCHES - 1)
            k = 0
            for g in range(FG):
                n = nblk[g] * P
                for c in range(HC):
                    act.wait_ge(hid_psum, k + 1)
                    if g >= 2 and c == 0:
                        act.wait_ge(y_psum, 4 * (g - 1))
                    nc.scalar.activation(hid[g % 2][:, c, 0:n], banks[4 + k % 2][:, 0:n], ACT.Gelu_apprx_tanh,
                                         bias=b1_c[:, c:c + 1]).then_inc(hid_ready, 1)
                    k += 1

        @block.vector
        def _(v):
            chain = [0]

            def own(ins):
                chain[0] += 1
                ins.then_inc(dve, 1)
                v.wait_ge(dve, chain[0])

            for c in range(NX):
                v.wait_ge(x_in[c], 32 if c == NX - 1 else 16)
                for t in range(c * XC, (c + 1) * XC):
                    ins = nc.vector.bn_stats(stats[:, t, :], node_h[:, t, :])
            own(ins)
            for t in range(NB):
                ins = nc.vector.bn_aggr(mv[:, t, :], stats[:, t, :])
            own(ins)
            nc.vector.tensor_scalar(rstd, mv[:, :, 1], EPS, None, ALU.add).then_inc(var_ready, 1)
            v.wait_ge(std_ready, 1)
            own(nc.vector.reciprocal(rstd, rstd))
            nc.vector.scalar_tensor_tensor(shift, mv[:, :, 0], -1.0, rstd, ALU.mult, ALU.mult).then_inc(shift_ready, 1)
            for t in range(0, NB, 2):
                nc.vector.tensor_scalar(node_h[:, t, :], node_h[:, t, :], mv[:, t, 0:1], rstd[:, t:t + 1],
                                        ALU.subtract, ALU.mult).then_inc(xhat_ready, 1)
            v.wait_ge(edges_in, 16 * 15)
            nc.vector.tensor_copy(rec[:, :, :, 0], src_i).then_inc(rec_int, 1)
            nc.vector.tensor_copy(rec[:, :, :, 1], dst_i).then_inc(rec_int, 1)
            v.wait_ge(rec_int, 2)
            blk_now, blk_next = keys.bitcast(i32), count_e.bitcast(i32)
            own(nc.vector.tensor_scalar(blk_now, dst_i.rearrange(flat), 7, None, ALU.logical_shift_right))
            own(nc.vector.tensor_scalar(blk_next, next_i.rearrange(flat), 7, None, ALU.logical_shift_right))
            own(nc.vector.tensor_tensor(member, blk_next, blk_now, ALU.is_lt))
            nc.vector.tensor_reduce(wrong, member, AX.X, ALU.max).then_inc(wrong_ready, 1)
            v.wait_ge(wrong_sum, 1)
            nc.vector.tensor_scalar(disorder, banks[4][:, 0:1], 0.0, None, ALU.is_gt).then_inc(disorder_known, 1)
            v.wait_ge(disorder_known, 1)
            with v.If(v.value_load(disorder[0:1, 0:1], min_val=0, max_val=1) > 0):
                v.wait_ge(rec_flt, 2)
                nc.vector.memset(zero_e, 0.0).then_inc(place_own, 1)
                nc.vector.tensor_copy(blk_e, blk_now).then_inc(place_own, 1)
                v.wait_ge(place_own, 2)
                nc.vector.memset(place, 0.0).then_inc(place_own, 1)
                nc.vector.memset(base, -1.0).then_inc(place_own, 1)
                nc.vector.memset(this_blk, 0.0).then_inc(place_own, 1)
                v.wait_ge(place_own, 5)
                OWN = 6
                with v.Fori(0, NB + 1) as b:
                    nc.vector.tensor_scalar(member, blk_e, this_blk, None, ALU.is_equal).then_inc(place_own, 1)
                    v.wait_ge(place_own, b * OWN + 6)
                    nc.vector.tensor_tensor_scan(count_e, member, zero_e, 0.0, ALU.add, ALU.add).then_inc(place_cnt, 1)
                    v.wait_ge(place_off, b + 1)
                    nc.vector.tensor_tensor(off_e, banks[4][:, 0:1], base, ALU.add).then_inc(place_own, 1)
                    v.wait_ge(place_own, b * OWN + 7)
                    nc.vector.scalar_tensor_tensor(at_e, count_e, off_e, member, ALU.add, ALU.mult).then_inc(place_own, 1)
                    v.wait_ge(place_own, b * OWN + 8)
                    nc.vector.tensor_tensor(place, place, at_e, ALU.add).then_inc(place_own, 1)
                    nc.vector.tensor_tensor(base, banks[4][:, 1:2], base, ALU.add).then_inc(place_own, 1)
                    nc.vector.tensor_scalar(this_blk, this_blk, 1.0, None, ALU.add).then_inc(place_own, 1)
                    v.wait_ge(place_own, b * OWN + 11)
                nc.vector.tensor_copy(place_i, place).then_inc(place_own, 1)
                v.wait_ge(place_own, (NB + 1) * OWN + 6)
                rec_flat = rec.rearrange("p c e f -> p (c e) f")

                def stage(step, half):
                    at = (step * 2 + half) * PLACE
                    nc.vector.tensor_scalar(place_idx[half], place_i[:, bass.ds(at, PLACE)], 0.0, None, ALU.add)
                    nc.vector.tensor_scalar(place_rec[half], rec_flat[:, bass.ds(at, PLACE), :], 0.0, None,
                                            ALU.add).then_inc(placed, 1)

                for half in range(2):
                    stage(0, half)
                with v.Fori(1, NT // (2 * PLACE)) as step:
                    for half in range(2):
                        v.wait_ge(placed_out[half], step * (16 * PLACE))
                        stage(step, half)
            v.wait_ge(params_in, 16 * 6)
            v.wait_ge(colsum, 1)
            own(nc.vector.tensor_scalar(mean_b, banks[5][:, 0:D], 1.0 / NODES, None, ALU.mult))
            v.wait_ge(xhat_ready, (NB + 1) // 2)
            v.wait_ge(xhat_act, NB // 2)
            for c in range(NX):
                s = node_h[:, c * XC:(c + 1) * XC, :]
                nc.vector.tensor_tensor(s, s, mean_b.unsqueeze(1).to_broadcast([P, XC, D]),
                                        ALU.subtract).then_inc(centered, 1)
            v.wait_ge(first_in, 16)
            own(nc.vector.tensor_copy(first_i, first_dst))
            own(nc.vector.tensor_scalar(key_i, first_i, 7, None, ALU.logical_shift_right))
            v.wait_ge(const_ready, 7)
            own(nc.vector.tensor_tensor(key_f, key_i, number, ALU.add))
            own(nc.vector.memset(key_f[0:1, 0:1], 0.0))
            nc.vector.tensor_tensor(diag, ident.unsqueeze(1).to_broadcast([P, EC, P]),
                                    key_f.unsqueeze(2).to_broadcast([P, EC, P]), ALU.mult).then_inc(diag_ready, 1)
            v.wait_ge(keys_row, 1)
            for b in range(4):
                n = min(512, NT - 512 * b)
                ins = nc.vector.tensor_copy(keys[:, 512 * b:512 * b + n], banks[b][:, 0:n])
            own(ins)
            def count_tiles(c):
                own(nc.vector.tensor_scalar(junk, keys, number[:, c:c + 1], 0.0, ALU.is_le, ALU.add,
                                            accum_out=tile_f[:, c:c + 1]))

            def tiles_and_blocks():
                own(nc.vector.tensor_scalar(tile_f, tile_f, -1.0, None, ALU.add))
                nc.vector.tensor_copy(tile_i, tile_f).then_inc(tiles_known, 1)
                own(nc.vector.tensor_tensor(blk_f, number, tile_f, ALU.subtract))
                nc.vector.tensor_scalar(blk_i, blk_f, float(NB - 1), None, ALU.min).then_inc(blocks_known, 1)
                own(nc.vector.tensor_scalar(blk_off, blk_f, float(P), None, ALU.mult))

            for c in range(COUNTS_FIRST):
                count_tiles(c)
            v.wait_ge(colsum, 2)
            nc.vector.tensor_scalar(tmp_b, banks[6][:, 0:D], 1.0 / NODES, EPS, ALU.mult, ALU.add).then_inc(cvar_ready, 1)
            v.wait_ge(cstd_ready, 1)
            own(nc.vector.reciprocal(scale_b, tmp_b))
            own(nc.vector.tensor_tensor(scale_b, scale_b, gamma_b, ALU.mult))
            v.wait_ge(sq_ready, NB)
            v.wait_ge(rec_flt, 2)

            def scaled(c):
                s = node_h[:, c * XC:(c + 1) * XC, :]
                own(nc.vector.tensor_tensor(s, s, scale_b.unsqueeze(1).to_broadcast([P, XC, D]), ALU.mult))
                nc.vector.tensor_tensor(s, s, beta_b.unsqueeze(1).to_broadcast([P, XC, D]),
                                        ALU.add).then_inc(h_ready, 1)

            scaled(0)
            for c in range(NX):
                if c + 1 < NX:
                    scaled(c + 1)
                if c == REC_AT // XC:
                    v.wait_ge(rec_back, 16 * EC)
                    nc.vector.tensor_tensor(rec[:, :, :, 1], rec[:, :, :, 1],
                                            blk_off.unsqueeze(2).to_broadcast([P, EC, P]),
                                            ALU.subtract).then_inc(dloc_ready, 1)
                for t in range(c * XC, (c + 1) * XC):
                    v.wait_ge(feat_psum, t + 1)
                    b = banks[2 + t % 2]
                    if t >= 2:
                        v.wait_ge(fi_saved[t % 2], 16 * (t // 2))
                    nc.vector.tensor_tensor(node_f[:, t, :], b[:, D:2 * D], b_io[:, D:2 * D], ALU.add)
                    nc.vector.tensor_tensor(fi_stage[t % 2], b[:, 0:D], b_io[:, 0:D], ALU.add).then_inc(feat_ready, 1)
                    if t < EC - COUNTS_FIRST:
                        count_tiles(COUNTS_FIRST + t)
                    elif t == EC - COUNTS_FIRST:
                        tiles_and_blocks()

            v.wait_ge(fi_saved[0], 16 * ((NB + 1) // 2))
            v.wait_ge(fi_saved[1], 16 * (NB // 2))
            v.wait_ge(node_a_zero, 1)

            def cols(a, g):
                return a[:, bass.ds(g * G, G)]

            def wide(a):
                return a.unsqueeze(2).to_broadcast([P, G, P])

            def rows4(a):
                return a.unsqueeze(1).to_broadcast([P, G, P])

            def spread(g, first):
                if not first:
                    v.wait_ge(sel_own, 4 * g)
                nc.vector.tensor_tensor(eq, rows4(ident), wide(cols(pair_src, g)), ALU.mult).then_inc(diag_done, 1)

            def one_hot(g, first):
                if not first:
                    v.wait_ge(mix_psum, g)
                    v.wait_ge(iw_done, g)
                nc.vector.tensor_tensor(hot, rows4(col_b), wide(cols(pair_dloc, g)), ALU.is_equal).then_inc(sel_own, 1)

            def equal_src(g):
                v.wait_ge(bcast_done, g + 1)
                nc.vector.tensor_tensor(eq, banks[0][:, :].rearrange("p (u n) -> p u n", u=G), wide(cols(pair_src, g)),
                                        ALU.is_equal).then_inc(sel_own, 1)

            def weigh_equal(g):
                v.wait_ge(sel_own, 4 * g + 2)
                nc.vector.tensor_tensor(same_ow, eq, wide(cols(pair_ow, g)), ALU.mult).then_inc(sel_done, 1)

            def before_only(g):
                v.wait_ge(sel_done, g + 1)
                nc.vector.tensor_tensor(eq, eq, rows4(lower), ALU.mult).then_inc(sel_own, 1)

            def reduce(g, h):
                v.wait_ge(sel_own, 4 * g + 3)
                nc.vector.tensor_reduce(earlier[h], eq, AX.X, ALU.max).then_inc(sel_own, 1)

            def next_gather(g, h, first):
                if not first:
                    v.wait_ge(in_psum, G * (g - 1))
                nc.vector.tensor_scalar(gather_idx[h], cols(pair_src, g), 0.0, None, ALU.add).then_inc(gidx_ready, 1)

            def index(g, h, first):
                if not first:
                    for u in range(G):
                        v.wait_ge(scattered[u], 16 * (g - 1))
                v.wait_ge(sel_own, 4 * g + 4)
                nc.vector.tensor_scalar(spare, earlier[h], spare_row[:, 0:1], None, ALU.mult).then_inc(idx_own, 1)
                v.wait_ge(idx_own, g + 1)
                nc.vector.tensor_tensor(scatter_idx[h], spare, cols(pair_src, g), ALU.max).then_inc(sidx_ready, 1)

            def add(g, u, blocks):
                v.wait_ge(in_psum, G * g + u // 2 * 2 + 2)
                if not (isinstance(g, int) and g == 0 and u == 0):
                    v.wait_ge(in_added, G * g + u)
                a = node_a[:, bass.ds(blocks[u], 1), :].rearrange("p a d -> p (a d)")
                nc.vector.tensor_tensor(a, a, banks[4 + u // 2][:, (u % 2) * D:(u % 2 + 1) * D],
                                        ALU.add).then_inc(in_added, 1)

            def load_blocks(g):
                return nc.values_load_multi_w_load_instructions(
                    pair_block[0:1, bass.ds(g * G, G)], engines=[mybir.EngineType.DVE], min_val=0, max_val=NB - 1,
                    skip_runtime_bounds_check_because="block numbers lie in the range by construction")[1]

            def turn_of(g, h, start):
                one_hot(g + 1, False)
                blocks = load_blocks(g - 1) if start else None
                equal_src(g + 1)
                steps = (lambda: weigh_equal(g + 1), lambda: before_only(g + 1), lambda: reduce(g + 1, 1 - h),
                         lambda: spread(g + 2, False))
                for u in range(G):
                    steps[u]()
                    if start:
                        add(g - 1, u, blocks)
                next_gather(g + 1, 1 - h, start == 0)
                index(g, h, start < 2)

            v.wait_ge(rec_done, EC)
            v.wait_ge(block_row, 16)
            spread(0, True)
            one_hot(0, True)
            equal_src(0)
            weigh_equal(0)
            before_only(0)
            reduce(0, 0)
            spread(1, False)
            next_gather(0, 0, True)
            turn_of(0, 0, 0)
            turn_of(1, 1, 1)
            with v.Fori(1, GROUPS // 2) as turn:
                for h in range(2):
                    turn_of(turn * 2 + h, h, 2)
            last = load_blocks(GROUPS - 1)
            for u in range(G):
                add(GROUPS - 1, u, last)
            nc.vector.memset(flags[:, 1:2], 0.0).then_inc(main_done, 1)

            v.wait_ge(post_w, 16 * 7)
            v.wait_ge(main_done, 3)
            post = [0]

            def link(ins):
                post[0] += 1
                ins.then_inc(post_own, 1)
                v.wait_ge(post_own, post[0])

            def sum_tables(b):
                n, a = in_batch[b], acc_t[b % 2]
                v.wait_ge(pool_sum, 2 * b + 2)
                nc.vector.tensor_tensor(a[:, 0, 0:n, :], a[:, 0, 0:n, :], a[:, 2, 0:n, :], ALU.add).then_inc(ao_ready, 1)

            sum_tables(0)
            sum_tables(1)
            for b in range(BATCHES):
                n, t, s = in_batch[b], BT * b, b % 2
                if b + 2 < BATCHES:
                    sum_tables(b + 2)
                v.wait_ge(gate_psum, b + 1)
                for i in range(n):
                    ins = nc.vector.tensor_tensor(gates[:, i, :], banks[3 + 2 * s + i][:, :], bx_b, ALU.add)
                ins.then_inc(gate_in, 1)
                v.wait_ge(gate_out, b + 1)
                new, o = gates[:, 0:n, D:2 * D], x1[:, 0:n, :]
                link(nc.vector.tensor_tensor(o, node_h[:, t:t + n, :], new, ALU.subtract))
                link(nc.vector.scalar_tensor_tensor(o, gates[:, 0:n, 0:D], 1.0, o, ALU.add, ALU.mult))
                link(nc.vector.scalar_tensor_tensor(o, o, 0.5, new, ALU.mult, ALU.add))
                v.wait_ge(x_again[s], 16 * (b // 2 + 1))
                nc.vector.tensor_tensor(o, o, x_t[s][:, 0:n, :], ALU.add).then_inc(inputs_used, 1)
                v.wait_ge(inputs_used, b + 1)
                for i in range(n):
                    ins = nc.vector.bn_stats(st6[:, i, :], x1[:, i, :])
                link(ins)
                for i in range(n):
                    ins = nc.vector.bn_aggr(mv2[:, i, :], st6[:, i, :])
                link(ins)
                nc.vector.tensor_scalar(mv2[:, 0:n, 1], mv2[:, 0:n, 1], EPS, None, ALU.add).then_inc(var2, 1)
                v.wait_ge(rs2_ready, b + 1)
                if b:
                    v.wait_ge(xnT_psum, b)
                for i in range(n):
                    ins = nc.vector.tensor_scalar(xn[:, i, :], x1[:, i, :], mv2[:, i, 0:1], rs2[:, i:i + 1],
                                                  ALU.subtract, ALU.mult)
                ins.then_inc(xn_ready, 1)
                v.wait_ge(xn_ready, b + 1)
                for i in range(n):
                    nc.vector.scalar_tensor_tensor(gates[:, i, 0:D], xn[:, i, :], 1.0, wr_b, ALU.mult, ALU.mult,
                                                   accum_out=w_all[:, t + i:t + i + 1])
                link(nc.vector.tensor_tensor(node_f[:, t:t + n, :], o, xn[:, 0:n, :], ALU.add))
            link(nc.vector.tensor_scalar(w_all, w_all, br_b, None, ALU.add))
            nc.vector.memset(flags[:, 3:4], 0.0).then_inc(w_done, 1)
            v.wait_ge(w_padded, 1)
            cur, cand, msk, bits = (u32s[:, k:k + 1] for k in range(4))
            link(nc.vector.memset(cur, 0))
            for r in range(THRESH_ROUNDS):
                bit = 1 << (31 - r)
                bit = bit - (1 << 32) if r == 0 else bit
                link(nc.vector.tensor_scalar(cand, cur, bit, None, ALU.bitwise_or))
                link(nc.vector.tensor_scalar(msk, cand, 31, None, ALU.arith_shift_right))
                link(nc.vector.tensor_scalar(msk, msk, -1, -(1 << 31), ALU.bitwise_xor, ALU.bitwise_or))
                link(nc.vector.tensor_tensor(bits, cand, msk, ALU.bitwise_xor))
                nc.vector.tensor_scalar(small[:, 0, :], w_all, bits.bitcast(f32), 0.0, ALU.is_ge, ALU.add,
                                        accum_out=cnts[:, 0:1]).then_inc(cnt_ready, 1)
                v.wait_ge(tot_ready, r + 1)
                link(nc.vector.tensor_scalar(msk, banks[6][:, 0:1], float(TOPK), -1.0, ALU.is_ge, ALU.mult))
                link(nc.vector.tensor_scalar(msk, msk, bit, None, ALU.bitwise_and))
                link(nc.vector.tensor_tensor(cur, cur, msk, ALU.bitwise_or))
            link(nc.vector.tensor_scalar(msk, cur, 31, None, ALU.arith_shift_right))
            link(nc.vector.tensor_scalar(msk, msk, -1, -(1 << 31), ALU.bitwise_xor, ALU.bitwise_or))
            link(nc.vector.tensor_tensor(bits, cur, msk, ALU.bitwise_xor))
            thr = bits.bitcast(f32)
            above, equal, incl, rank, pick = (small[:, k, :] for k in range(1, 6))
            link(nc.vector.tensor_scalar(above, w_all, thr, 0.0, ALU.is_gt, ALU.add, accum_out=cnts[:, 0:1]))
            nc.vector.tensor_scalar(equal, w_all, thr, None, ALU.is_equal).then_inc(cnt_ready, 1)
            v.wait_ge(tot_ready, THRESH_ROUNDS + 1)
            link(nc.vector.tensor_copy(pick, banks[6][:, 64:64 + NB]))
            link(nc.vector.memset(small[:, 6, :], 0.0))
            link(nc.vector.tensor_tensor_scan(incl, pick, small[:, 6, :], 0.0, ALU.add, ALU.add))
            link(nc.vector.tensor_tensor(incl, incl, pick, ALU.subtract))
            link(nc.vector.tensor_tensor(rank, incl, banks[6][:, 128:128 + NB], ALU.add))
            link(nc.vector.tensor_scalar(rank, rank, banks[6][:, 0:1], None, ALU.add))
            link(nc.vector.scalar_tensor_tensor(pick, rank, float(TOPK), equal, ALU.is_lt, ALU.mult))
            link(nc.vector.tensor_tensor(pick, pick, above, ALU.add))
            link(nc.vector.tensor_tensor(w_all, w_all, pick, ALU.mult))
            for t in range(NB):
                v.wait_ge(y_psum, t + 1)
                b = banks[2 + t % 2][:, 0:D]
                nc.vector.tensor_tensor(y_t[t % 2], b, b2_b, ALU.add).then_inc(y_taken, 1)
                v.wait_ge(y_taken, t + 1)
                if t >= 2:
                    v.wait_ge(o_saved[t % 2], 16 * (t // 2))
                nc.vector.scalar_tensor_tensor(o_t[t % 2], y_t[t % 2], w_all[:, t:t + 1], node_f[:, t, :],
                                               ALU.mult, ALU.add).then_inc(o_ready, 1)

        @block.tensor
        def _(pe):
            mm, tr = nc.tensor.matmul, nc.tensor.transpose
            pe.wait_ge(const_ready, 7)
            for t in range(NB):
                n = P if t < NB - 1 else LAST
                if t % 2:
                    pe.wait_ge(xhat_act, t // 2 + 1)
                else:
                    pe.wait_ge(xhat_ready, t // 2 + 1)
                ins = mm(banks[5][:, 0:D], ones[0:n, :], node_h[0:n, t, :], start=t == 0, stop=t == NB - 1)
            ins.then_inc(colsum, 1)
            pe.wait_ge(wrong_ready, 1)
            mm(banks[4][:, 0:1], ones, wrong, start=True, stop=True).then_inc(wrong_sum, 1)
            pe.wait_ge(disorder_known, 1)
            with pe.If(pe.value_load(disorder[0:1, 0:1], min_val=0, max_val=1) > 0):
                with pe.Fori(0, NB + 1) as b:
                    pe.wait_ge(place_cnt, b + 1)
                    mm(banks[4][:, 0:1], upper, count_e[:, NT - 1:NT], start=True, stop=True)
                    mm(banks[4][:, 1:2], ones, count_e[:, NT - 1:NT], start=True, stop=True).then_inc(place_off, 1)
            for t in range(NB):
                n = P if t < NB - 1 else LAST
                pe.wait_ge(sq_ready, t + 1)
                ins = mm(banks[6][:, 0:D], ones[0:n, :], sq[t % 2][0:n, :], start=t == 0, stop=t == NB - 1)
                ins.then_inc(sq_used, 1)
                if t == KEYS_AT:
                    pe.wait_ge(diag_ready, 1)
                    diags = diag.rearrange(flat)
                    for b in range(4):
                        w = min(512, NT - 512 * b)
                        ins = mm(banks[b][:, 0:w], ones, diags[:, 512 * b:512 * b + w], start=True, stop=True)
                    ins.then_inc(keys_row, 1)
            pe.wait_ge(sq_used, NB)
            pe.nop().then_inc(colsum, 1)
            pe.wait_ge(params_in, 16 * 6)
            pe.wait_ge(cvar_ready, 1)

            def h_transposes(t):
                pe.wait_ge(h_ready, t // XC + 1)
                if t >= 2:
                    pe.wait_ge(hT_ready, t - 1)
                tr(banks[t % 2][:, 0:P], node_h[:, t, 0:P], ident)
                tr(banks[t % 2][:, P:2 * P], node_h[:, t, P:2 * P], ident).then_inc(hT_psum, 1)

            h_transposes(0)
            for t in range(NB):
                if t == REC_AT - 1:
                    pe.wait_ge(dloc_ready, 1)
                    for c in range(EC):
                        if c >= 4:
                            pe.wait_ge(rec_done, c - 3)
                        for f in range(4):
                            ins = tr(banks[4 + c % 4][:, f * P:(f + 1) * P], rec[:, c, :, f], ident)
                        ins.then_inc(recT, 1)
                if t + 1 < NB:
                    h_transposes(t + 1)
                pe.wait_ge(hT_ready, t + 1)
                if t >= 2:
                    pe.wait_ge(feat_ready, t - 1)
                mm(banks[2 + t % 2][:, :], hT[t % 2][:, 0, :], w_io[:, 0, :], start=True, stop=False)
                mm(banks[2 + t % 2][:, :], hT[t % 2][:, 1, :], w_io[:, 1, :], start=False, stop=True).then_inc(feat_psum, 1)

            pe.wait_ge(feat_ready, NB)
            pe.wait_ge(block_row, 16)

            def src_rows(g):
                pe.wait_ge(diag_done, g + 1)
                mm(banks[0][:, :], ones, eq.rearrange("p u n -> p (u n)"), start=True, stop=True).then_inc(bcast_done, 1)

            def sums(g, count, start):
                h = (start + 1) % 2
                for u in range(G):
                    if u == 0:
                        pe.wait_ge(iw_done, g + 1)
                    pe.wait_ge(gathered[h][u], 16 * count)
                    if u % 2 == 0 and not (isinstance(g, int) and g == 0):
                        pe.wait_ge(in_added, G * (g - 1) + u + 2)
                    mm(banks[4 + u // 2][:, (u % 2) * D:(u % 2 + 1) * D], hot_iw[h][:, u, :], rows[h][u],
                       start=True, stop=True).then_inc(in_psum, 1)

            def group(turn, h, first):
                g = turn * 2 + h
                blocks = nc.values_load_multi_w_load_instructions(
                    pair_block[0:1, bass.ds(g * G, G)], engines=[mybir.EngineType.PE], min_val=0, max_val=NB - 1,
                    skip_runtime_bounds_check_because="block numbers lie in the range by construction")[1]
                pe.wait_ge(sel_done, g + 1)
                if not first:
                    pe.wait_ge(mix_ready, g)
                for u in range(G):
                    ins = mm(banks[1][:, u * P:(u + 1) * P], hot[:, u, :], same_ow[:, u, :], start=True, stop=True)
                ins.then_inc(mix_psum, 1)
                if not first:
                    sums(g - 1, turn + h, h)
                pe.wait_ge(mix_ready, g + 1)
                for u in range(G):
                    if not first and u % 2 == 0:
                        pe.wait_ge(out_ready, G * (g - 1) + u + 2)
                    f = node_f[:, bass.ds(blocks[u], 1), :].rearrange("p a d -> p (a d)")
                    mm(banks[2 + u // 2][:, (u % 2) * D:(u % 2 + 1) * D], mix[:, u, :], f,
                       start=True, stop=True).then_inc(out_psum, 1)
                src_rows(g + 2)

            src_rows(0)
            src_rows(1)
            group(0, 0, True)
            group(0, 1, False)
            with pe.Fori(1, GROUPS // 2) as turn:
                for h in range(2):
                    group(turn, h, False)
            sums(GROUPS - 1, GROUPS // 2, 0)
            pe.wait_ge(in_psum, G * GROUPS)
            pe.nop().then_inc(main_done, 1)

            pe.wait_ge(main_done, 3)
            pe.wait_ge(post_w, 16 * 7)
            def transposes(b):
                if b:
                    pe.wait_ge(aT_ready, b)
                for part in range(2):
                    if part:
                        pe.wait_ge(ao_ready, b + 1)
                    for i in range(in_batch[b]):
                        t = BT * b + i
                        ao = acc_t[b % 2][:, 0, i, :]
                        for k in (range(2, 4) if part else (0, 1, 4, 5)):
                            a = node_a[:, t, :] if k < 2 else ao if k < 4 else node_h[:, t, :]
                            at = 6 * i + k
                            ins = tr(banks[at // 4][:, at % 4 * P:(at % 4 + 1) * P], a[:, k % 2 * P:(k % 2 + 1) * P], ident)
                ins.then_inc(trans6, 1)

            def xn_transposes(b):
                pe.wait_ge(xn_ready, b + 1)
                if b:
                    pe.wait_ge(xnT_ready, b)
                for i in range(in_batch[b]):
                    for k in range(2):
                        ins = tr(banks[7][:, (2 * i + k) * P:(2 * i + k + 1) * P], xn[:, i, k * P:(k + 1) * P], ident)
                ins.then_inc(xnT_psum, 1)

            transposes(0)
            for b in range(BATCHES):
                if b + 1 < BATCHES:
                    transposes(b + 1)
                pe.wait_ge(aT_ready, b + 1)
                if b >= 2:
                    pe.wait_ge(gate_in, b - 1)
                for i in range(in_batch[b]):
                    for k in range(6):
                        ins = mm(banks[3 + 2 * (b % 2) + i][:, :], aT[b % 2][:, i, k, :],
                                 wx[:, k, :] if k < 4 else wh[:, k - 4, :], start=k == 0, stop=k == 5)
                ins.then_inc(gate_psum, 1)
                if b:
                    xn_transposes(b - 1)
            xn_transposes(BATCHES - 1)
            rounds = [0]

            def count():
                r = rounds[0]
                if r > THRESH_ROUNDS:
                    return
                pe.wait_ge(cnt_ready, r + 1)
                if r < THRESH_ROUNDS:
                    mm(banks[6][:, 0:1], ones, cnts[:, 0:1], start=True, stop=True).then_inc(tot_ready, 1)
                else:
                    mm(banks[6][:, 0:1], ones, cnts[:, 0:1], start=True, stop=True)
                    mm(banks[6][:, 64:64 + NB], ones, small[:, 2, :], start=True, stop=True)
                    mm(banks[6][:, 128:128 + NB], upper, small[:, 2, :], start=True, stop=True).then_inc(tot_ready, 1)
                rounds[0] += 1

            pe.wait_ge(xnT_ready, BATCHES)
            pe.wait_ge(ffn_w, 32)
            def hidden(g):
                n = nblk[g]
                for c in range(HC):
                    k = HC * g + c
                    if k >= 2:
                        pe.wait_ge(hid_ready, k - 1)
                    for kk in range(2):
                        ins = mm(banks[4 + k % 2][:, 0:n * P], w1_s[:, kk, c * P:(c + 1) * P],
                                 node_a[:, 4 * g:4 * g + n, kk * P:(kk + 1) * P], start=kk == 0, stop=kk == 1)
                    ins.then_inc(hid_psum, 1)
                    count()
                    count()

            hidden(0)
            for g in range(FG):
                if g + 1 < FG:
                    hidden(g + 1)
                while rounds[0] <= THRESH_ROUNDS:
                    count()
                pe.wait_ge(hid_ready, HC * (g + 1))
                for b in range(nblk[g]):
                    y = 4 * g + b
                    if y >= 2:
                        pe.wait_ge(y_taken, y - 1)
                    for c in range(HC):
                        ins = mm(banks[2 + y % 2][:, 0:D], hid[g % 2][:, c, b * P:(b + 1) * P],
                                 w2_s[:, c, :], start=c == 0, stop=c == HC - 1)
                    ins.then_inc(y_psum, 1)


def kernel(x, src, dst, edge_weight, edge_weight_n2, L0_gnn_gamma, L0_gnn_beta, L0_gnn_W_in, L0_gnn_b_in,
           L0_gnn_W_out, L0_gnn_b_out, L0_gnn_W_x2i, L0_gnn_b_x2i, L0_gnn_W_h2h, L0_ffn_attention_mask,
           L0_ffn_wr, L0_ffn_br, L0_ffn_w1, L0_ffn_b1, L0_ffn_w2, L0_ffn_b2):
    import concourse.bacc as bacc
    from concourse.bass_utils import run_bass_kernel_spmd
    nc = bacc.Bacc("TRN2", target_bir_lowering=False, num_devices=1)
    given = dict(x=x, src=src, dst=dst, iw=edge_weight, ow=edge_weight_n2, gamma=L0_gnn_gamma, beta=L0_gnn_beta,
                 w_in=L0_gnn_W_in, b_in=L0_gnn_b_in, w_out=L0_gnn_W_out, b_out=L0_gnn_b_out, w_x2i=L0_gnn_W_x2i,
                 b_x2i=L0_gnn_b_x2i, w_h2h=L0_gnn_W_h2h, wr=L0_ffn_wr, br=L0_ffn_br, w1=L0_ffn_w1, b1=L0_ffn_b1,
                 w2=L0_ffn_w2, b2=L0_ffn_b2)
    arrays, args = {}, []
    for name, a in given.items():
        a = np.ascontiguousarray(a)
        arrays[f"{name}_dram"] = a
        args.append(nc.dram_tensor(f"{name}_dram", a.shape, mybir.dt.from_np(a.dtype), kind="ExternalInput").ap())
    args.append(nc.dram_tensor("out_dram", x.shape, mybir.dt.float32, kind="ExternalOutput").ap())
    gnn_ffn(nc, *args)
    return run_bass_kernel_spmd(nc, [arrays], core_ids=[0]).results[0]["out_dram"]
```

```python
import numpy as np
import concourse.bass as bass
from concourse import mybir
from contextlib import ExitStack

P = 128
EPS = 1e-5


def gnn_ffn(nc, x, src, dst, iw, ow, gamma, beta, w_in, b_in, w_out, b_out, w_x2i, b_x2i, w_h2h,
            wr, br, w1, b1, w2, b2, out):
    f32, bf16, i32 = mybir.dt.float32, mybir.dt.bfloat16, mybir.dt.int32
    ALU, ACT, AX = mybir.AluOpType, mybir.ActivationFunctionType, mybir.AxisListType

    NODES, D = x.shape
    EDGES = src.shape[0]
    H = w1.shape[1]
    NB = -(-NODES // P)
    LAST = NODES - (NB - 1) * P
    NPAD = NB * P
    TILES = -(-EDGES // P)
    FULL = EDGES // P
    TAIL = EDGES - FULL * P
    G = 4
    GROUPS = -(-(TILES + NB - 1) // G)
    GROUPS += GROUPS % 2
    EC = -(-((GROUPS + 2) * G) // P)
    NT = EC * P
    CF, REST = FULL // P, FULL % P
    assert EC == CF + 1 and TILES < NT
    TOPK = max(1, NODES // 2) - 1
    PICKS = -(-TOPK // P)
    PLACE = 8
    assert NT % (2 * PLACE) == 0
    XC = 7
    NX = NB // XC
    assert NX * XC == NB and D == 2 * P
    HC = H // P
    KEYS_AT = 4 * XC
    ZEROS = 16 * (G // 2) * (NB + 2)
    SHIFT_ON_DVE = (0, 4)
    COUNTS_FIRST = 3
    REC_AT = 4 * XC + 3

    records = nc.dram_tensor("edge_records", [NT, 4 * P], f32, kind="Internal").ap()
    record_list = records.rearrange("t (e f) -> (t e) f", f=4)
    feat_in_table = nc.dram_tensor("feat_in_table", [NPAD, D], f32, kind="Internal").ap()
    a_out_tables = [nc.dram_tensor(f"a_out_table{k}", [NPAD + P, D], f32, kind="Internal").ap() for k in range(G)]
    hT_table = nc.dram_tensor("hT_table", [NPAD, D], f32, kind="Internal").ap()
    xn_table = nc.dram_tensor("xn_table", [NPAD, D], f32, kind="Internal").ap()
    block_list = nc.dram_tensor("pair_blocks", [NT], i32, kind="Internal").ap()

    with ExitStack() as ctx:
        def sem(name):
            return ctx.enter_context(nc.semaphore(name))

        node_h = ctx.enter_context(nc.sbuf_tensor("node_h", [P, NB, D], f32))
        node_f = ctx.enter_context(nc.sbuf_tensor("node_f", [P, NB, D], f32))
        node_a = ctx.enter_context(nc.sbuf_tensor("node_a", [P, NB, D], f32))
        WORK = 15576
        work = ctx.enter_context(nc.sbuf_tensor("work", [P, WORK], f32))
        banks = [ctx.enter_context(nc.psum_tensor(f"bank{i}", [P, 512], f32)) for i in range(8)]

        class Cut:
            def __init__(self, tensor, words, at=0):
                self.tensor, self.words, self.at = tensor, words, at

            def take(self, n):
                a = self.tensor[:, self.at:self.at + n]
                self.at += n
                assert self.at <= self.words, self.at
                return a

        fixed = Cut(work, WORK)
        ident = fixed.take(P)
        ones = fixed.take(P)
        lower = fixed.take(P)
        upper = fixed.take(P)
        number = fixed.take(NT // P)
        spare_row = fixed.take(1)
        col_b = fixed.take(P // 2).bitcast(bf16)
        flags = fixed.take(6)
        WORDS_FIXED = fixed.at
        assert WORDS_FIXED % 4 == 0

        cut = Cut(work, WORK, WORDS_FIXED)
        pair_src = cut.take(NT)
        pair_iw = cut.take(NT)
        pair_ow = cut.take(NT)
        pair_dloc = cut.take(NT // 2).bitcast(bf16)
        pair_block = cut.take(NT).bitcast(i32)
        ring_at = cut.at
        hot = cut.take(G * P).rearrange("p (u n) -> p u n", u=G)
        hot_iw = [cut.take(G * P).rearrange("p (u n) -> p u n", u=G) for _ in range(2)]
        same_ow = cut.take(G * P).rearrange("p (u n) -> p u n", u=G)
        eq = cut.take(G * P).rearrange("p (u n) -> p u n", u=G)
        mix = cut.take(G * P).rearrange("p (u n) -> p u n", u=G)
        rows = [[cut.take(D) for _ in range(G)] for _ in range(2)]
        out_rows = [cut.take(G * D) for _ in range(2)]
        gather_idx = [cut.take(G).bitcast(i32) for _ in range(2)]
        scatter_idx = [cut.take(G).bitcast(i32) for _ in range(2)]
        earlier = [cut.take(G) for _ in range(2)]
        repeat_row = cut.take(G)

        pre = Cut(work, WORK, ring_at)
        w_io = pre.take(2 * 2 * D).rearrange("p (k n) -> p k n", k=2)
        b_io = pre.take(2 * D)
        gamma_b = pre.take(D)
        beta_b = pre.take(D)
        mean_b = pre.take(D)
        scale_b = pre.take(D)
        batch_std = pre.take(D)
        SB = 4
        sq = [pre.take(D) for _ in range(SB)]
        HB = 4
        hT = [pre.take(D).rearrange("p (k n) -> p k n", k=2) for _ in range(HB)]
        fi_stage = [pre.take(D) for _ in range(2)]
        zero_row = pre.take(D)
        assert pre.at <= WORK
        stats = node_a[:, 0:2, :].rearrange("p a b -> p (a b)")[:, 0:NB * 6].rearrange("p (t s) -> p t s", t=NB)
        mv = node_a[:, 2, 0:NB * 2].rearrange("p (t s) -> p t s", t=NB)
        rstd = node_a[:, 3, 0:NB]
        shift = node_a[:, 3, NB:2 * NB]

        edge = Cut(node_f[:, :, :].rearrange("p t d -> p (t d)"), NB * D)
        src_i = edge.take(NT).bitcast(i32).rearrange("p (c e) -> p c e", e=P)
        dst_i = edge.take(NT).bitcast(i32).rearrange("p (c e) -> p c e", e=P)
        iw_f = edge.take(NT).rearrange("p (c e) -> p c e", e=P)
        ow_f = edge.take(NT).rearrange("p (c e) -> p c e", e=P)
        keys = edge.take(NT)
        diag = edge.take(NT).rearrange("p (c e) -> p c e", e=P)
        not_read = edge.take(NT)
        next_i = not_read.bitcast(i32).rearrange("p (c e) -> p c e", e=P)
        key_i = edge.take(EC).bitcast(i32)
        key_f = edge.take(EC)
        tile_f = edge.take(EC)
        blk_f = edge.take(EC)
        first_dst = edge.take(EC)
        first_i = edge.take(EC).bitcast(i32)
        wrong = edge.take(1)
        disorder = edge.take(1).bitcast(i32)
        edge_a = Cut(node_a[:, :, :].rearrange("p t d -> p (t d)"), NB * D, 4 * D)
        rec = edge_a.take(EC * 4 * P).rearrange("p (c e f) -> p c e f", c=EC, f=4)
        tile_i = edge_a.take(EC).bitcast(i32)
        blk_i = edge_a.take(EC).bitcast(i32)
        blk_off = edge_a.take(EC)

        flat = "p c e -> p (c e)"
        blk_e, place, member, count_e = not_read, keys, src_i.bitcast(f32).rearrange(flat), diag.rearrange(flat)
        zero_e, at_e = iw_f.rearrange(flat), ow_f.rearrange(flat)
        place_i = dst_i.rearrange(flat)
        base = edge_a.take(1)
        this_blk = edge_a.take(1)
        off_e = edge_a.take(1)
        edge_a.take(1)
        place_rec = [edge_a.take(PLACE * 4).rearrange("p (k f) -> p k f", f=4) for _ in range(2)]
        place_idx = [edge_a.take(PLACE).bitcast(i32) for _ in range(2)]

        disorder_known = sem("disorder_known")
        wrong_ready = sem("wrong_ready")
        wrong_sum = sem("wrong_sum")
        records_final = sem("records_final")
        first_in = sem("first_in")
        placed = sem("placed")
        placed_out = [sem(f"placed_out{i}") for i in range(2)]
        issued_place = sem("issued_place")
        place_own = sem("place_own")
        place_cnt = sem("place_cnt")
        place_off = sem("place_off")
        const_ready = sem("const_ready")
        const_dep = sem("const_dep")
        pads_ready = sem("pads_ready")
        edges_in = sem("edges_in")
        x_in = [sem(f"x_in{c}") for c in range(NX)]
        x_pad = sem("x_pad")
        params_in = sem("params_in")
        rec_int = sem("rec_int")
        rec_flt = sem("rec_flt")
        rec_saved = sem("rec_saved")
        diag_ready = sem("diag_ready")
        keys_row = sem("keys_row")
        dve = sem("dve")
        tiles_known = sem("tiles_known")
        blocks_known = sem("blocks_known")
        block_saved = sem("block_saved")
        block_row = sem("block_row")
        rec_back = sem("rec_back")
        dloc_ready = sem("dloc_ready")
        recT = sem("recT")
        rec_done = sem("rec_done")
        node_a_zero = sem("node_a_zero")
        zero_ready = sem("zero_ready")
        tables_zero = sem("tables_zero")
        var_ready = sem("var_ready")
        std_ready = sem("std_ready")
        shift_ready = sem("shift_ready")
        xhat_ready = sem("xhat_ready")
        xhat_act = sem("xhat_act")
        colsum = sem("colsum")
        centered = sem("centered")
        sq_ready = sem("sq_ready")
        sq_used = sem("sq_used")
        cvar_ready = sem("cvar_ready")
        cstd_ready = sem("cstd_ready")
        h_scaled = sem("h_scaled")
        h_ready = [sem(f"h_ready{c}") for c in range(NX)]
        hT_psum = sem("hT_psum")
        hT_ready = sem("hT_ready")
        hT_saved = [sem(f"hT_saved{i}") for i in range(HB)]
        feat_psum = sem("feat_psum")
        feat_ready = sem("feat_ready")
        fi_saved = [sem(f"fi_saved{i}") for i in range(2)]

        diag_done = sem("diag_done")
        bcast_done = sem("bcast_done")
        sel_done = sem("sel_done")
        sel_own = sem("sel_own")
        gidx_ready = sem("gidx_ready")
        sidx_ready = sem("sidx_ready")
        idx_own = sem("idx_own")
        iw_done = sem("iw_done")
        issued = sem("issued")
        post_own = sem("post_own")
        mix_psum = sem("mix_psum")
        mix_ready = sem("mix_ready")
        out_psum = sem("out_psum")
        out_ready = sem("out_ready")
        in_psum = sem("in_psum")
        in_added = sem("in_added")
        gathered = [[sem(f"gathered{h}{u}") for u in range(G)] for h in range(2)]
        scattered = [sem(f"scattered{u}") for u in range(G)]

        BT = 2
        BATCHES = -(-NB // BT)
        in_batch = [min(BT, NB - BT * b) for b in range(BATCHES)]
        post = Cut(work, WORK, WORDS_FIXED)
        bx_b = post.take(2 * D)
        b2_b = post.take(D)
        wr_b = post.take(D)
        br_b = post.take(1)
        b1_c = post.take(HC)
        w_all = post.take(NB)
        small = post.take(NB * 8).rearrange("p (k t) -> p k t", k=8)
        node_id = post.take(NB)
        minus_half = post.take(BT)
        st6 = post.take(BT * 6).rearrange("p (i s) -> p i s", i=BT)
        mv2 = post.take(BT * 2).rearrange("p (i s) -> p i s", i=BT)
        rs2 = post.take(BT)
        WAYS = 7
        shifts = [28, 25, 23, 20, 17, 14, 11, 8, 5, 2, 0]
        ROUNDS = len(shifts)
        ways = [min(WAYS, (1 << (above - low)) - 1) for above, low in zip([31] + shifts, shifts)]
        steps = post.take(ROUNDS * WAYS).bitcast(i32).rearrange("p (r c) -> p r c", c=WAYS)
        u32s = post.take(2 + WAYS).bitcast(i32)
        passed = post.take(WAYS + 1)
        cnts = post.take(WAYS)
        wx = post.take(4 * 2 * D).rearrange("p (k n) -> p k n", k=4)
        wh = post.take(2 * 2 * D).rearrange("p (k n) -> p k n", k=2)
        acc_t = [post.take(G * BT * D).rearrange("p (k i d) -> p k i d", k=G, i=BT) for _ in range(2)]
        x_t = [post.take(BT * D).rearrange("p (i d) -> p i d", i=BT) for _ in range(2)]
        hT_t = [post.take(BT * D).rearrange("p (i d) -> p i d", i=BT) for _ in range(2)]
        aT = [post.take(BT * 4 * P).rearrange("p (i k n) -> p i k n", i=BT, k=4) for _ in range(2)]
        aT_banks = [(0, 1), (2, 7)]
        gates = post.take(BT * 2 * D).rearrange("p (i n) -> p i n", i=BT)
        x1 = post.take(BT * D).rearrange("p (i d) -> p i d", i=BT)
        pick_id = post.take(PICKS).bitcast(i32)
        pick_w = post.take(PICKS)
        assert post.at <= WORK, post.at
        w1_s = acc_t[0].rearrange("p k i d -> p (k i d)").rearrange("p (k n) -> p k n", k=2)
        w2_s = acc_t[1].rearrange("p k i d -> p (k i d)").rearrange("p (k n) -> p k n", k=HC)
        ffn = Cut(node_h[:, :, :].rearrange("p t d -> p (t d)"), NB * D)
        hid = [ffn.take(HC * 512).rearrange("p (k n) -> p k n", k=HC) for _ in range(2)]
        y_t = [ffn.take(D) for _ in range(2)]
        o_t = [ffn.take(D) for _ in range(2)]
        picked_rows = node_f[:, 0:PICKS, :]
        picked_T = node_a[:, 0:PICKS, :]
        lists = Cut(node_h[:, :, :].rearrange("p t d -> p (t d)"), NB * D)
        slot_hot = lists.take(NB * P).rearrange("p (t q) -> p t q", t=NB)
        tile_hot = lists.take(NB * 2 * PICKS).rearrange("p (t k s) -> p t k s", t=NB, k=2)

        main_done = sem("main_done")
        post_w = sem("post_w")
        acc_in = [sem(f"acc_in{i}") for i in range(2)]
        hT_in = [sem(f"hT_in{i}") for i in range(2)]
        x_again = [sem(f"x_again{i}") for i in range(2)]
        inputs_used = sem("inputs_used")
        ffn_w = sem("ffn_w")
        pool_sum = sem("pool_sum")
        ao_ready = sem("ao_ready")
        aT_psum = sem("aT_psum")
        aT_ready = sem("aT_ready")
        gate_psum = sem("gate_psum")
        gate_in = sem("gate_in")
        gate_out = sem("gate_out")
        var2 = sem("var2")
        rs2_ready = sem("rs2_ready")
        xn_ready = sem("xn_ready")
        base_ready = sem("base_ready")
        xn_saved = sem("xn_saved")
        base_saved = sem("base_saved")
        search_const = sem("search_const")
        w_done = sem("w_done")
        w_padded = sem("w_padded")
        cnt_ready = sem("cnt_ready")
        tot_ready = sem("tot_ready")
        hid_psum = sem("hid_psum")
        hid_ready = sem("hid_ready")
        y_psum = sem("y_psum")
        y_taken = sem("y_taken")
        o_ready = sem("o_ready")
        pick_ready = sem("pick_ready")
        pick_sums = sem("pick_sums")
        hots_ready = sem("hots_ready")
        list_psum = sem("list_psum")
        list_ready = sem("list_ready")
        pickT_psum = sem("pickT_psum")
        pickT_ready = sem("pickT_ready")
        o_added = sem("o_added")

        FG = -(-PICKS // 4)
        ntile = [min(4, PICKS - 4 * g) for g in range(FG)]
        BASES = BATCHES + (in_batch[-1] > 1)
        picked = [sem(f"picked{g}") for g in range(FG)]

        block = ctx.enter_context(nc.Block())

        @block.sync
        def _(sp):
            sp.wait_ge(x_pad, 1)
            whole = x[0:(NB - 1) * P, :].rearrange("(t p) d -> p t d", p=P)
            for c in range(NX):
                n = min(XC, NB - 1 - c * XC)
                sp.dma_start(node_h[:, c * XC:c * XC + n, :], whole[:, c * XC:c * XC + n, :]).then_inc(x_in[c], 16)
            sp.dma_start(node_h[0:LAST, NB - 1, :], x[(NB - 1) * P:NODES, :]).then_inc(x_in[NX - 1], 16)
            sp.wait_ge(pads_ready, 5)
            for a, s in ((src, src_i), (dst, dst_i), (iw, iw_f), (ow, ow_f)):
                sp.dma_start(s[:, 0:CF, :], a[0:CF * P * P].rearrange("(c q e) -> q c e", q=P, e=P)).then_inc(edges_in, 16)
                sp.dma_start(s[0:REST, CF, :], a[CF * P * P:FULL * P].rearrange("(q e) -> q e", e=P)).then_inc(edges_in, 16)
                sp.dma_start(s[REST:REST + 1, CF, 0:TAIL], a[FULL * P:EDGES].rearrange("(q e) -> q e", q=1)).then_inc(edges_in, 16)
            sp.dma_start(next_i[:, 0:CF, :], dst[1:CF * P * P + 1].rearrange("(c q e) -> q c e", q=P, e=P)).then_inc(edges_in, 16)
            sp.dma_start(next_i[0:REST, CF, :], dst[CF * P * P + 1:FULL * P + 1].rearrange("(q e) -> q e", e=P)).then_inc(edges_in, 16)
            sp.dma_start(next_i[REST:REST + 1, CF, 0:TAIL - 1], dst[FULL * P + 1:EDGES].rearrange("(q e) -> q e", q=1)).then_inc(edges_in, 16)
            sp.wait_ge(rec_int, 2)
            sp.wait_ge(rec_flt, 2)
            sp.dma_start(records.rearrange("(c q) f -> q c f", q=P), rec.rearrange("p c e f -> p c (e f)")).then_inc(rec_saved, 16)
            sp.wait_ge(records_final, 1)
            with nc.allow_non_contiguous_dma(reason="one word per tile"):
                sp.dma_start(first_dst, records[:, 1:2].rearrange("(c q) f -> q (c f)", q=P)).then_inc(first_in, 16)
            sp.wait_ge(zero_ready, 1)
            for t in a_out_tables[:G // 2]:
                sp.dma_start(t.rearrange("(t p) d -> p t d", p=P),
                             zero_row.unsqueeze(1).to_broadcast([P, NB + 1, D])).then_inc(tables_zero, 16)
            for t in range(NB + 1):
                if t < NB:
                    sp.wait_ge(hT_ready, t + 1)
                    sp.dma_start(hT_table[t * P:(t + 1) * P, :],
                                 hT[t % HB].rearrange("p k n -> p (k n)")).then_inc(hT_saved[t % HB], 16)
                    sp.wait_ge(feat_ready, t + 1)
                    sp.dma_start(feat_in_table[t * P:(t + 1) * P, :], fi_stage[t % 2]).then_inc(fi_saved[t % 2], 16)
                for a in a_out_tables[G // 2:]:
                    sp.dma_start(a[t * P:(t + 1) * P, :], zero_row).then_inc(tables_zero, 16)

            sp.wait_ge(main_done, 3)
            for b in range(BATCHES + 1):
                if b < BATCHES:
                    t, n, s = BT * b, in_batch[b], b % 2
                    if b >= 2:
                        sp.wait_ge(aT_psum, b - 1)
                    for k in range(G):
                        sp.dma_start(acc_t[s][:, k, 0:n, :], a_out_tables[k][t * P:(t + n) * P, :].rearrange(
                            "(i p) d -> p i d", p=P)).then_inc(acc_in[s], 16)
                    if b == 0:
                        sp.dma_start(wx, w_x2i.rearrange("(k p) n -> p k n", p=P)).then_inc(post_w, 16)
                        sp.dma_start(wh, w_h2h.rearrange("(k p) n -> p k n", p=P)).then_inc(post_w, 16)
                        sp.dma_start(bx_b, b_x2i.partition_broadcast(P)).then_inc(post_w, 16)
                        sp.dma_start(b2_b, b2.partition_broadcast(P)).then_inc(post_w, 16)
                        sp.dma_start(wr_b, wr.rearrange("d o -> (o d)").partition_broadcast(P)).then_inc(post_w, 16)
                        sp.dma_start(br_b, br.partition_broadcast(P)).then_inc(post_w, 16)
                        with nc.allow_non_contiguous_dma(reason="b1 by hidden unit"):
                            sp.dma_start(b1_c, b1.rearrange("(k p) -> p k", p=P)).then_inc(post_w, 16)
                if b:
                    t, n, s = BT * (b - 1), in_batch[b - 1], (b - 1) % 2
                    if b >= 3:
                        sp.wait_ge(gate_psum, b - 2)
                    sp.dma_start(hT_t[s][:, 0:n, :], hT_table[t * P:(t + n) * P, :].rearrange(
                        "(i p) d -> p i d", p=P)).then_inc(hT_in[s], 16)
                    if b >= 3:
                        sp.wait_ge(inputs_used, b - 2)
                    if t + n < NB:
                        sp.dma_start(x_t[s][:, 0:n, :], x[t * P:(t + n) * P, :].rearrange(
                            "(i p) d -> p i d", p=P)).then_inc(x_again[s], 16)
                    else:
                        sp.dma_start(x_t[s][0:LAST, n - 1, :], x[(NB - 1) * P:NODES, :]).then_inc(x_again[s], 16)
            sp.wait_ge(inputs_used, BATCHES)
            sp.dma_start(w1_s, w1.rearrange("(k p) n -> p k n", p=P)).then_inc(ffn_w, 16)
            sp.dma_start(w2_s, w2.rearrange("(k p) n -> p k n", p=P)).then_inc(ffn_w, 16)

        @block.gpsimd
        def _(pool):
            pool.memset(src_i[:, CF, :], 0).then_inc(pads_ready, 1)
            pool.memset(dst_i[:, CF, :], NPAD).then_inc(pads_ready, 1)
            pool.memset(next_i[:, CF, :], NPAD).then_inc(pads_ready, 1)
            pool.memset(iw_f[:, CF, :], 0.0).then_inc(pads_ready, 1)
            pool.memset(ow_f[:, CF, :], 0.0).then_inc(pads_ready, 1)
            pool.memset(node_h[:, NB - 1, :], 0.0).then_inc(x_pad, 1)
            pool.memset(zero_row, 0.0).then_inc(zero_ready, 1)
            pool.memset(ident, 0.0).then_inc(const_dep, 1)
            pool.memset(lower, 1.0).then_inc(const_dep, 1)
            pool.memset(upper, 1.0).then_inc(const_dep, 1)
            pool.memset(ones, 1.0).then_inc(const_ready, 1)
            pool.iota(number, pattern=[[P, EC]], base=0, channel_multiplier=1,
                      allow_small_or_imprecise_dtypes=True).then_inc(const_ready, 1)
            pool.iota(spare_row, pattern=[[0, 1]], base=NPAD, channel_multiplier=1,
                      allow_small_or_imprecise_dtypes=True).then_inc(const_ready, 1)
            pool.iota(col_b, pattern=[[1, P]], base=0, channel_multiplier=0,
                      allow_small_or_imprecise_dtypes=True).then_inc(const_ready, 1)
            pool.wait_ge(const_dep, 3)
            pool.affine_select(out=ident, in_=ident, pattern=[[-1, P]], compare_op=ALU.not_equal, fill=1.0,
                               base=0, channel_multiplier=1).then_inc(const_ready, 1)
            pool.affine_select(out=lower, in_=lower, pattern=[[-1, P]], compare_op=ALU.is_gt, fill=0.0,
                               base=0, channel_multiplier=1).then_inc(const_ready, 1)
            pool.affine_select(out=upper, in_=upper, pattern=[[1, P]], compare_op=ALU.is_gt, fill=0.0,
                               base=0, channel_multiplier=-1).then_inc(const_ready, 1)
            pool.wait_ge(rec_saved, 16)
            pool.wait_ge(disorder_known, 1)
            with pool.If(pool.value_load(disorder[0:1, 0:1], min_val=0, max_val=1) > 0):
                for half in range(2):
                    pool.wait_ge(placed, half + 1)
                    for k in range(PLACE):
                        pool.indirect_dma_start(record_list, bass.IndirectOffsetOnAxis(place_idx[half][:, k:k + 1], 0),
                                                place_rec[half][:, k, :], None).then_inc(placed_out[half], 16)
                with pool.Fori(1, NT // (2 * PLACE)) as step:
                    for half in range(2):
                        pool.wait_ge(placed, step * 2 + half + 1)
                        pool.sem_inc(issued_place, 1)
                        for k in range(PLACE):
                            pool.indirect_dma_start(record_list, bass.IndirectOffsetOnAxis(place_idx[half][:, k:k + 1], 0),
                                                    place_rec[half][:, k, :], None).then_inc(placed_out[half], 16)
                for half in range(2):
                    pool.wait_ge(placed_out[half], 16 * PLACE * (NT // (2 * PLACE)))
            pool.memset(flags[:, 4:5], 0.0).then_inc(records_final, 1)
            def shift_chunk(c):
                pool.wait_ge(h_scaled, c + 1)
                a = node_h[:, c * XC:(c + 1) * XC, :]
                pool.tensor_tensor(out=a, in0=a, in1=beta_b.unsqueeze(1).to_broadcast([P, XC, D]),
                                   op=ALU.add).then_inc(h_ready[c], 1)

            for c in range(1, 4):
                shift_chunk(c)
            pool.wait_ge(tiles_known, 1)
            for c in range(EC):
                pool.indirect_dma_start(rec[:, c, :, :].rearrange("p e f -> p (e f)"), None, records,
                                        bass.IndirectOffsetOnAxis(tile_i[:, c:c + 1], 0)).then_inc(rec_back, 16)
            for c in range(5, NX):
                shift_chunk(c)
            pool.wait_ge(rec_done, EC)
            pool.wait_ge(block_saved, 16)
            pool.memset(node_a[:, :, :], 0.0).then_inc(node_a_zero, 1)

            pool.wait_ge(tables_zero, ZEROS)
            pool.wait_ge(fi_saved[0], 16 * ((NB + 1) // 2))
            pool.wait_ge(fi_saved[1], 16 * (NB // 2))
            for i in range(HB):
                pool.wait_ge(hT_saved[i], 16 * ((NB - i + HB - 1) // HB))

            def gather(g, h, u, first):
                pool.wait_ge(gidx_ready, g + 1)
                if not first:
                    pool.wait_ge(in_psum, G * (g - 2) + u + 1)
                pool.sem_inc(issued, 1)
                pool.indirect_dma_start(rows[h][u], None, feat_in_table,
                                        bass.IndirectOffsetOnAxis(gather_idx[h][:, u:u + 1], 0)).then_inc(gathered[h][u], 16)

            def scatter(g, h, u, first):
                pool.wait_ge(sidx_ready, g + 1)
                pool.wait_ge(out_ready, G * g + u + 1)
                if not first:
                    pool.wait_ge(scattered[u], 16 * g)
                pool.sem_inc(issued, 1)
                pool.indirect_dma_start(a_out_tables[u], bass.IndirectOffsetOnAxis(scatter_idx[h][:, u:u + 1], 0),
                                        out_rows[h][:, u * D:(u + 1) * D], None, compute_op=ALU.add).then_inc(scattered[u], 16)

            def turn_of(g, h, first_gather, first_scatter):
                for u in range(G):
                    gather(g, h, u, first_gather)
                    scatter(g - 1, 1 - h, u, first_scatter)

            for u in range(G):
                gather(0, 0, u, True)
            turn_of(1, 1, True, True)
            with pool.Fori(1, GROUPS // 2) as turn:
                for h in range(2):
                    turn_of(turn * 2 + h, h, False, False)
            for u in range(G):
                scatter(GROUPS - 1, 1, u, False)
            for u in range(G):
                pool.wait_ge(scattered[u], 16 * GROUPS)
            pool.memset(flags[:, 2:3], 0.0).then_inc(main_done, 1)

            pool.wait_ge(main_done, 3)
            pool.memset(minus_half, -0.5).then_inc(search_const, 1)
            pool.iota(node_id, pattern=[[P, NB]], base=0, channel_multiplier=1,
                      allow_small_or_imprecise_dtypes=True).then_inc(search_const, 1)
            pool.wait_ge(search_const, 2)

            def inverse_std(b):
                n = in_batch[b]
                pool.wait_ge(var2, b + 1)
                pool.tensor_tensor(out=rs2[:, 0:n], in0=mv2[:, 0:n, 1], in1=minus_half[:, 0:n],
                                   op=ALU.pow).then_inc(rs2_ready, 1)

            def pair_sums(b):
                n, s = in_batch[b], b % 2
                pool.wait_ge(acc_in[s], 16 * G * (b // 2 + 1))
                for k in (0, 2):
                    pool.tensor_tensor(out=acc_t[s][:, k, 0:n, :], in0=acc_t[s][:, k, 0:n, :],
                                       in1=acc_t[s][:, k + 1, 0:n, :], op=ALU.add).then_inc(pool_sum, 1)

            pair_sums(0)
            pair_sums(1)
            for r, low in enumerate(shifts):
                for k in range(ways[r]):
                    pool.memset(steps[:, r, k:k + 1], (k + 1) << low).then_inc(search_const, 1)
            for b in range(BATCHES):
                if b + 2 < BATCHES:
                    pair_sums(b + 2)
                inverse_std(b)
            pool.wait_ge(w_done, 1)
            pool.affine_select(out=w_all, in_=w_all, pattern=[[-P, NB]], compare_op=ALU.is_ge, fill=-3.0e38,
                               base=NODES - 1, channel_multiplier=-1).then_inc(w_padded, 1)
            pool.wait_ge(xn_saved, 16 * BATCHES)
            pool.wait_ge(base_saved, 16 * BASES)
            pool.wait_ge(list_ready, 2)
            for y in range(PICKS):
                pool.indirect_dma_start(picked_rows[:, y, :], None, xn_table,
                                        bass.IndirectOffsetOnAxis(pick_id[:, y:y + 1], 0)).then_inc(picked[y // 4], 16)
            for y in range(PICKS):
                n = min(P, TOPK - y * P)
                pool.wait_ge(o_ready, y + 1)
                if y:
                    pool.wait_ge(o_added, 16 * y)
                pool.indirect_dma_start(out, bass.IndirectOffsetOnAxis(pick_id[0:n, y:y + 1], 0), o_t[y % 2][0:n, :],
                                        None, compute_op=ALU.add).then_inc(o_added, 16)
            pool.wait_ge(o_added, 16 * PICKS)

        @block.scalar
        def _(act):
            with nc.allow_non_contiguous_dma(reason="parameters"):
                act.dma_start(w_io[:, :, 0:D], w_in.rearrange("(k p) n -> p k n", p=P)).then_inc(params_in, 16)
                act.dma_start(w_io[:, :, D:2 * D], w_out.rearrange("(k p) n -> p k n", p=P)).then_inc(params_in, 16)
                act.dma_start(b_io[:, 0:D], b_in.partition_broadcast(P)).then_inc(params_in, 16)
                act.dma_start(b_io[:, D:2 * D], b_out.partition_broadcast(P)).then_inc(params_in, 16)
                act.dma_start(gamma_b, gamma.partition_broadcast(P)).then_inc(params_in, 16)
                act.dma_start(beta_b, beta.partition_broadcast(P)).then_inc(params_in, 16)
            act.wait_ge(var_ready, 1)
            nc.scalar.activation(rstd, rstd, ACT.Sqrt).then_inc(std_ready, 1)
            act.wait_ge(shift_ready, 1)
            for t in range(1, NB, 2):
                nc.scalar.activation(node_h[:, t, :], node_h[:, t, :], ACT.Identity, bias=shift[:, t:t + 1],
                                     scale=rstd[:, t:t + 1]).then_inc(xhat_act, 1)
            act.wait_ge(edges_in, 16 * 15)
            nc.scalar.activation(rec[:, :, :, 2], iw_f, ACT.Copy).then_inc(rec_flt, 1)
            nc.scalar.activation(rec[:, :, :, 3], ow_f, ACT.Copy).then_inc(rec_flt, 1)
            for t in range(NB):
                act.wait_ge(centered, t // XC + 1)
                if t >= SB:
                    act.wait_ge(sq_used, t - SB + 1)
                nc.scalar.activation(sq[t % SB], node_h[:, t, :], ACT.Square).then_inc(sq_ready, 1)
            act.wait_ge(cvar_ready, 1)
            nc.scalar.activation(batch_std, batch_std, ACT.Sqrt).then_inc(cstd_ready, 1)
            for t in range(NB):
                if t == REC_AT - 2 * XC // 3:
                    act.wait_ge(blocks_known, 1)
                    with nc.allow_non_contiguous_dma(reason="one word per pair"):
                        act.dma_start(block_list.rearrange("(c q) -> q c", q=P), blk_i).then_inc(block_saved, 16)
                if t == REC_AT:
                    act.wait_ge(block_saved, 16)
                    act.dma_start(pair_block[0:1, :], block_list.rearrange("(a n) -> a n", a=1)).then_inc(block_row, 16)
                    for c in range(EC):
                        act.wait_ge(recT, c + 1)
                        b = banks[4 + c % 4]
                        s = slice(c * P, (c + 1) * P)
                        nc.scalar.activation(pair_src[:, s], b[:, 0:P], ACT.Copy)
                        nc.scalar.activation(pair_dloc[:, s], b[:, P:2 * P], ACT.Copy)
                        nc.scalar.activation(pair_iw[:, s], b[:, 2 * P:3 * P], ACT.Copy)
                        nc.scalar.activation(pair_ow[:, s], b[:, 3 * P:4 * P], ACT.Copy).then_inc(rec_done, 1)
                act.wait_ge(hT_psum, t + 1)
                if t >= HB:
                    act.wait_ge(feat_psum, t - HB + 1)
                    act.wait_ge(hT_saved[t % HB], 16 * (t // HB))
                nc.scalar.activation(hT[t % HB], banks[t % 2][:, 0:D].rearrange("p (k n) -> p k n", k=2),
                                     ACT.Copy).then_inc(hT_ready, 1)

            def weigh(g, h, first):
                act.wait_ge(sel_own, 4 * g + 1)
                if not first:
                    act.wait_ge(in_psum, G * (g - 1))
                for u in range(G):
                    ins = nc.scalar.activation(hot_iw[h][:, u, :], hot[:, u, :], ACT.Copy,
                                               scale=pair_iw[:, bass.ds(g * G + u, 1)])
                ins.then_inc(iw_done, 1)

            def group(g, h, first):
                act.wait_ge(mix_psum, g + 1)
                if not first:
                    act.wait_ge(out_psum, G * g)
                nc.scalar.activation(mix, banks[1][:, :].rearrange("p (u n) -> p u n", u=G), ACT.Copy).then_inc(mix_ready, 1)
                weigh(g + 1, 1 - h, first is True)
                for u in range(0, G, 2):
                    act.wait_ge(out_psum, G * g + u + 2)
                    if first is False:
                        act.wait_ge(scattered[u], 16 * (g - 1))
                        act.wait_ge(scattered[u + 1], 16 * (g - 1))
                    nc.scalar.activation(out_rows[h][:, u * D:(u + 2) * D], banks[2 + u // 2][:, :],
                                         ACT.Copy).then_inc(out_ready, 2)

            act.wait_ge(tables_zero, ZEROS)
            act.wait_ge(fi_saved[0], 16 * ((NB + 1) // 2))
            act.wait_ge(fi_saved[1], 16 * (NB // 2))
            for i in range(HB):
                act.wait_ge(hT_saved[i], 16 * ((NB - i + HB - 1) // HB))
            weigh(0, 0, True)
            group(0, 0, True)
            group(1, 1, None)
            with act.Fori(1, GROUPS // 2) as turn:
                for h in range(2):
                    group(turn * 2 + h, h, False)

            def to_aT(b):
                act.wait_ge(aT_psum, b + 1)
                if b >= 2:
                    act.wait_ge(gate_psum, b - 1)
                for i in range(in_batch[b]):
                    ins = nc.scalar.activation(aT[b % 2][:, i, :, :].rearrange("p k n -> p (k n)"),
                                               banks[aT_banks[b % 2][i]][:, :], ACT.Copy)
                ins.then_inc(aT_ready, 1)

            def save(b):
                n, t = in_batch[b], BT * b
                act.wait_ge(xn_ready, b + 1)
                act.dma_start(xn_table[t * P:(t + n) * P, :].rearrange("(i p) d -> p i d", p=P),
                              node_a[:, t:t + n, :]).then_inc(xn_saved, 16)
                act.wait_ge(base_ready, b + 1)
                whole = n if t + n < NB else n - 1
                if whole:
                    act.dma_start(out[t * P:(t + whole) * P, :].rearrange("(i p) d -> p i d", p=P),
                                  node_f[:, t:t + whole, :]).then_inc(base_saved, 16)
                if whole < n:
                    act.dma_start(out[(NB - 1) * P:NODES, :], node_f[0:LAST, NB - 1, :]).then_inc(base_saved, 16)

            to_aT(0)
            for b in range(BATCHES):
                n = in_batch[b]
                if b + 1 < BATCHES:
                    to_aT(b + 1)
                act.wait_ge(gate_in, b + 1)
                nc.scalar.activation(gates[:, 0:n, 0:D], gates[:, 0:n, 0:D], ACT.Tanh, scale=0.5)
                nc.scalar.activation(gates[:, 0:n, D:2 * D], gates[:, 0:n, D:2 * D], ACT.Tanh).then_inc(gate_out, 1)
                if b:
                    save(b - 1)
            save(BATCHES - 1)
            k = 0
            for g in range(FG):
                n = ntile[g] * P
                for c in range(HC):
                    act.wait_ge(hid_psum, k + 1)
                    if g >= 2 and c == 0:
                        act.wait_ge(y_psum, 4 * (g - 1))
                    nc.scalar.activation(hid[g % 2][:, c, 0:n], banks[4 + k % 2][:, 0:n], ACT.Gelu_apprx_tanh,
                                         bias=b1_c[:, c:c + 1]).then_inc(hid_ready, 1)
                    k += 1

        @block.vector
        def _(v):
            chain = [0]

            def own(ins):
                chain[0] += 1
                ins.then_inc(dve, 1)
                v.wait_ge(dve, chain[0])

            for c in range(NX):
                v.wait_ge(x_in[c], 32 if c == NX - 1 else 16)
                for t in range(c * XC, (c + 1) * XC):
                    ins = nc.vector.bn_stats(stats[:, t, :], node_h[:, t, :])
            own(ins)
            for t in range(NB):
                ins = nc.vector.bn_aggr(mv[:, t, :], stats[:, t, :])
            own(ins)
            nc.vector.tensor_scalar(rstd, mv[:, :, 1], EPS, None, ALU.add).then_inc(var_ready, 1)
            v.wait_ge(std_ready, 1)
            own(nc.vector.reciprocal(rstd, rstd))
            nc.vector.scalar_tensor_tensor(shift, mv[:, :, 0], -1.0, rstd, ALU.mult, ALU.mult).then_inc(shift_ready, 1)
            for t in range(0, NB, 2):
                nc.vector.tensor_scalar(node_h[:, t, :], node_h[:, t, :], mv[:, t, 0:1], rstd[:, t:t + 1],
                                        ALU.subtract, ALU.mult).then_inc(xhat_ready, 1)
            v.wait_ge(edges_in, 16 * 15)
            nc.vector.tensor_copy(rec[:, :, :, 0], src_i).then_inc(rec_int, 1)
            nc.vector.tensor_copy(rec[:, :, :, 1], dst_i).then_inc(rec_int, 1)
            v.wait_ge(rec_int, 2)
            blk_now, blk_next = keys.bitcast(i32), count_e.bitcast(i32)
            own(nc.vector.tensor_scalar(blk_now, dst_i.rearrange(flat), 7, None, ALU.logical_shift_right))
            own(nc.vector.tensor_scalar(blk_next, next_i.rearrange(flat), 7, None, ALU.logical_shift_right))
            own(nc.vector.tensor_tensor(member, blk_next, blk_now, ALU.is_lt))
            nc.vector.tensor_reduce(wrong, member, AX.X, ALU.max).then_inc(wrong_ready, 1)
            v.wait_ge(wrong_sum, 1)
            nc.vector.tensor_scalar(disorder, banks[4][:, 0:1], 0.0, None, ALU.is_gt).then_inc(disorder_known, 1)
            v.wait_ge(disorder_known, 1)
            with v.If(v.value_load(disorder[0:1, 0:1], min_val=0, max_val=1) > 0):
                v.wait_ge(rec_flt, 2)
                nc.vector.memset(zero_e, 0.0).then_inc(place_own, 1)
                nc.vector.tensor_copy(blk_e, blk_now).then_inc(place_own, 1)
                v.wait_ge(place_own, 2)
                nc.vector.memset(place, 0.0).then_inc(place_own, 1)
                nc.vector.memset(base, -1.0).then_inc(place_own, 1)
                nc.vector.memset(this_blk, 0.0).then_inc(place_own, 1)
                v.wait_ge(place_own, 5)
                OWN = 6
                with v.Fori(0, NB + 1) as b:
                    nc.vector.tensor_scalar(member, blk_e, this_blk, None, ALU.is_equal).then_inc(place_own, 1)
                    v.wait_ge(place_own, b * OWN + 6)
                    nc.vector.tensor_tensor_scan(count_e, member, zero_e, 0.0, ALU.add, ALU.add).then_inc(place_cnt, 1)
                    v.wait_ge(place_off, b + 1)
                    nc.vector.tensor_tensor(off_e, banks[4][:, 0:1], base, ALU.add).then_inc(place_own, 1)
                    v.wait_ge(place_own, b * OWN + 7)
                    nc.vector.scalar_tensor_tensor(at_e, count_e, off_e, member, ALU.add, ALU.mult).then_inc(place_own, 1)
                    v.wait_ge(place_own, b * OWN + 8)
                    nc.vector.tensor_tensor(place, place, at_e, ALU.add).then_inc(place_own, 1)
                    nc.vector.tensor_tensor(base, banks[4][:, 1:2], base, ALU.add).then_inc(place_own, 1)
                    nc.vector.tensor_scalar(this_blk, this_blk, 1.0, None, ALU.add).then_inc(place_own, 1)
                    v.wait_ge(place_own, b * OWN + 11)
                nc.vector.tensor_copy(place_i, place).then_inc(place_own, 1)
                v.wait_ge(place_own, (NB + 1) * OWN + 6)
                rec_flat = rec.rearrange("p c e f -> p (c e) f")

                def stage(step, half):
                    at = (step * 2 + half) * PLACE
                    nc.vector.tensor_scalar(place_idx[half], place_i[:, bass.ds(at, PLACE)], 0.0, None, ALU.add)
                    nc.vector.tensor_scalar(place_rec[half], rec_flat[:, bass.ds(at, PLACE), :], 0.0, None,
                                            ALU.add).then_inc(placed, 1)

                for half in range(2):
                    stage(0, half)
                with v.Fori(1, NT // (2 * PLACE)) as step:
                    for half in range(2):
                        v.wait_ge(placed_out[half], step * (16 * PLACE))
                        stage(step, half)
            v.wait_ge(params_in, 16 * 6)
            v.wait_ge(colsum, 1)
            own(nc.vector.tensor_scalar(mean_b, banks[5][:, 0:D], 1.0 / NODES, None, ALU.mult))
            v.wait_ge(xhat_ready, (NB + 1) // 2)
            v.wait_ge(xhat_act, NB // 2)
            for c in range(NX):
                s = node_h[:, c * XC:(c + 1) * XC, :]
                nc.vector.tensor_tensor(s, s, mean_b.unsqueeze(1).to_broadcast([P, XC, D]),
                                        ALU.subtract).then_inc(centered, 1)
            v.wait_ge(first_in, 16)
            own(nc.vector.tensor_copy(first_i, first_dst))
            own(nc.vector.tensor_scalar(key_i, first_i, 7, None, ALU.logical_shift_right))
            v.wait_ge(const_ready, 7)
            own(nc.vector.tensor_tensor(key_f, key_i, number, ALU.add))
            own(nc.vector.memset(key_f[0:1, 0:1], 0.0))
            nc.vector.tensor_tensor(diag, ident.unsqueeze(1).to_broadcast([P, EC, P]),
                                    key_f.unsqueeze(2).to_broadcast([P, EC, P]), ALU.mult).then_inc(diag_ready, 1)
            v.wait_ge(keys_row, 1)
            for b in range(4):
                n = min(512, NT - 512 * b)
                ins = nc.vector.tensor_copy(keys[:, 512 * b:512 * b + n], banks[b][:, 0:n])
            own(ins)
            def count_tiles(c):
                own(nc.vector.tensor_scalar(not_read, keys, number[:, c:c + 1], 0.0, ALU.is_le, ALU.add,
                                            accum_out=tile_f[:, c:c + 1]))

            def tiles_and_blocks():
                own(nc.vector.tensor_scalar(tile_f, tile_f, -1.0, None, ALU.add))
                nc.vector.tensor_copy(tile_i, tile_f).then_inc(tiles_known, 1)
                own(nc.vector.tensor_tensor(blk_f, number, tile_f, ALU.subtract))
                nc.vector.tensor_scalar(blk_i, blk_f, float(NB - 1), None, ALU.min).then_inc(blocks_known, 1)
                own(nc.vector.tensor_scalar(blk_off, blk_f, float(P), None, ALU.mult))

            for c in range(COUNTS_FIRST):
                count_tiles(c)
            v.wait_ge(colsum, 2)
            nc.vector.tensor_scalar(batch_std, banks[6][:, 0:D], 1.0 / NODES, EPS, ALU.mult, ALU.add).then_inc(cvar_ready, 1)
            v.wait_ge(cstd_ready, 1)
            own(nc.vector.reciprocal(scale_b, batch_std))
            own(nc.vector.tensor_tensor(scale_b, scale_b, gamma_b, ALU.mult))
            v.wait_ge(sq_ready, NB)
            v.wait_ge(rec_flt, 2)

            def scale_chunk(c):
                a = node_h[:, c * XC:(c + 1) * XC, :]
                nc.vector.tensor_tensor(a, a, scale_b.unsqueeze(1).to_broadcast([P, XC, D]), ALU.mult).then_inc(h_scaled, 1)

            def shift_chunk(c):
                v.wait_ge(h_scaled, c + 1)
                a = node_h[:, c * XC:(c + 1) * XC, :]
                nc.vector.tensor_tensor(a, a, beta_b.unsqueeze(1).to_broadcast([P, XC, D]), ALU.add).then_inc(h_ready[c], 1)

            scale_chunk(0)
            shift_chunk(0)
            for c in range(NX):
                if c == REC_AT // XC:
                    v.wait_ge(rec_back, 16 * EC)
                    nc.vector.tensor_tensor(rec[:, :, :, 1], rec[:, :, :, 1],
                                            blk_off.unsqueeze(2).to_broadcast([P, EC, P]),
                                            ALU.subtract).then_inc(dloc_ready, 1)
                for t in range(c * XC, (c + 1) * XC):
                    v.wait_ge(feat_psum, t + 1)
                    b = banks[2 + t % 2]
                    if t >= 2:
                        v.wait_ge(fi_saved[t % 2], 16 * (t // 2))
                    nc.vector.tensor_tensor(node_f[:, t, :], b[:, D:2 * D], b_io[:, D:2 * D], ALU.add)
                    nc.vector.tensor_tensor(fi_stage[t % 2], b[:, 0:D], b_io[:, 0:D], ALU.add).then_inc(feat_ready, 1)
                    if t % XC == 1 and c + 1 < NX:
                        scale_chunk(c + 1)
                    if t % XC == 3 and c + 1 in SHIFT_ON_DVE:
                        shift_chunk(c + 1)
                    if t % 2 == 0 and t // 2 < EC - COUNTS_FIRST:
                        count_tiles(COUNTS_FIRST + t // 2)
                    elif t % 2 == 0 and t // 2 == EC - COUNTS_FIRST:
                        tiles_and_blocks()

            v.wait_ge(tables_zero, ZEROS)
            v.wait_ge(fi_saved[0], 16 * ((NB + 1) // 2))
            v.wait_ge(fi_saved[1], 16 * (NB // 2))
            for i in range(HB):
                v.wait_ge(hT_saved[i], 16 * ((NB - i + HB - 1) // HB))
            v.wait_ge(node_a_zero, 1)

            def cols(a, g):
                return a[:, bass.ds(g * G, G)]

            def wide(a):
                return a.unsqueeze(2).to_broadcast([P, G, P])

            def rows4(a):
                return a.unsqueeze(1).to_broadcast([P, G, P])

            def spread(g, first):
                if not first:
                    v.wait_ge(sel_own, 4 * g)
                nc.vector.tensor_tensor(eq, rows4(ident), wide(cols(pair_src, g)), ALU.mult).then_inc(diag_done, 1)

            def one_hot(g, first):
                if not first:
                    v.wait_ge(mix_psum, g)
                    v.wait_ge(iw_done, g)
                nc.vector.tensor_tensor(hot, rows4(col_b), wide(cols(pair_dloc, g)), ALU.is_equal).then_inc(sel_own, 1)

            def equal_src(g):
                v.wait_ge(bcast_done, g + 1)
                nc.vector.tensor_tensor(eq, banks[0][:, :].rearrange("p (u n) -> p u n", u=G), wide(cols(pair_src, g)),
                                        ALU.is_equal).then_inc(sel_own, 1)

            def weigh_equal(g):
                v.wait_ge(sel_own, 4 * g + 2)
                nc.vector.tensor_tensor(same_ow, eq, wide(cols(pair_ow, g)), ALU.mult).then_inc(sel_done, 1)

            def before_only(g):
                v.wait_ge(sel_done, g + 1)
                nc.vector.tensor_tensor(eq, eq, rows4(lower), ALU.mult).then_inc(sel_own, 1)

            def reduce(g, h):
                v.wait_ge(sel_own, 4 * g + 3)
                nc.vector.tensor_reduce(earlier[h], eq, AX.X, ALU.max).then_inc(sel_own, 1)

            def next_gather(g, h, first):
                if not first:
                    v.wait_ge(in_psum, G * (g - 1))
                nc.vector.tensor_scalar(gather_idx[h], cols(pair_src, g), 0.0, None, ALU.add).then_inc(gidx_ready, 1)

            def index(g, h, first):
                if not first:
                    for u in range(G):
                        v.wait_ge(scattered[u], 16 * (g - 1))
                v.wait_ge(sel_own, 4 * g + 4)
                nc.vector.tensor_scalar(repeat_row, earlier[h], spare_row[:, 0:1], None, ALU.mult).then_inc(idx_own, 1)
                v.wait_ge(idx_own, g + 1)
                nc.vector.tensor_tensor(scatter_idx[h], repeat_row, cols(pair_src, g), ALU.max).then_inc(sidx_ready, 1)

            def add(g, u, blocks):
                v.wait_ge(in_psum, G * g + u // 2 * 2 + 2)
                if not (isinstance(g, int) and g == 0 and u == 0):
                    v.wait_ge(in_added, G * g + u)
                a = node_a[:, bass.ds(blocks[u], 1), :].rearrange("p a d -> p (a d)")
                nc.vector.tensor_tensor(a, a, banks[4 + u // 2][:, (u % 2) * D:(u % 2 + 1) * D],
                                        ALU.add).then_inc(in_added, 1)

            def load_blocks(g):
                return nc.values_load_multi_w_load_instructions(
                    pair_block[0:1, bass.ds(g * G, G)], engines=[mybir.EngineType.DVE], min_val=0, max_val=NB - 1,
                    skip_runtime_bounds_check_because="block numbers lie in the range by construction")[1]

            def turn_of(g, h, start):
                one_hot(g + 1, False)
                blocks = load_blocks(g - 1) if start else None
                equal_src(g + 1)
                steps = (lambda: weigh_equal(g + 1), lambda: before_only(g + 1), lambda: reduce(g + 1, 1 - h),
                         lambda: spread(g + 2, False))
                for u in range(G):
                    steps[u]()
                    if start:
                        add(g - 1, u, blocks)
                next_gather(g + 1, 1 - h, start == 0)
                index(g, h, start < 2)

            v.wait_ge(rec_done, EC)
            v.wait_ge(block_row, 16)
            spread(0, True)
            one_hot(0, True)
            equal_src(0)
            weigh_equal(0)
            before_only(0)
            reduce(0, 0)
            spread(1, False)
            next_gather(0, 0, True)
            turn_of(0, 0, 0)
            turn_of(1, 1, 1)
            with v.Fori(1, GROUPS // 2) as turn:
                for h in range(2):
                    turn_of(turn * 2 + h, h, 2)
            last = load_blocks(GROUPS - 1)
            for u in range(G):
                add(GROUPS - 1, u, last)
            nc.vector.memset(flags[:, 1:2], 0.0).then_inc(main_done, 1)

            v.wait_ge(main_done, 3)
            post = [0]

            def link(ins):
                post[0] += 1
                ins.then_inc(post_own, 1)
                v.wait_ge(post_own, post[0])

            def sum_tables(b):
                n, a = in_batch[b], acc_t[b % 2]
                v.wait_ge(pool_sum, 2 * b + 2)
                nc.vector.tensor_tensor(a[:, 0, 0:n, :], a[:, 0, 0:n, :], a[:, 2, 0:n, :], ALU.add).then_inc(ao_ready, 1)

            sum_tables(0)
            sum_tables(1)
            v.wait_ge(post_w, 16 * 7)
            for b in range(BATCHES):
                n, t, s = in_batch[b], BT * b, b % 2
                if b + 2 < BATCHES:
                    sum_tables(b + 2)
                v.wait_ge(gate_psum, b + 1)
                for i in range(n):
                    ins = nc.vector.tensor_tensor(gates[:, i, :], banks[3 + 2 * s + i][:, :], bx_b, ALU.add)
                ins.then_inc(gate_in, 1)
                v.wait_ge(gate_out, b + 1)
                new, o = gates[:, 0:n, D:2 * D], x1[:, 0:n, :]
                link(nc.vector.tensor_tensor(o, node_h[:, t:t + n, :], new, ALU.subtract))
                link(nc.vector.scalar_tensor_tensor(o, gates[:, 0:n, 0:D], 1.0, o, ALU.add, ALU.mult))
                link(nc.vector.scalar_tensor_tensor(o, o, 0.5, new, ALU.mult, ALU.add))
                v.wait_ge(x_again[s], 16 * (b // 2 + 1))
                nc.vector.tensor_tensor(o, o, x_t[s][:, 0:n, :], ALU.add).then_inc(inputs_used, 1)
                v.wait_ge(inputs_used, b + 1)
                for i in range(n):
                    ins = nc.vector.bn_stats(st6[:, i, :], x1[:, i, :])
                link(ins)
                for i in range(n):
                    ins = nc.vector.bn_aggr(mv2[:, i, :], st6[:, i, :])
                link(ins)
                nc.vector.tensor_scalar(mv2[:, 0:n, 1], mv2[:, 0:n, 1], EPS, None, ALU.add).then_inc(var2, 1)
                v.wait_ge(rs2_ready, b + 1)
                for i in range(n):
                    ins = nc.vector.tensor_scalar(node_a[:, t + i, :], x1[:, i, :], mv2[:, i, 0:1], rs2[:, i:i + 1],
                                                  ALU.subtract, ALU.mult)
                ins.then_inc(xn_ready, 1)
                v.wait_ge(xn_ready, b + 1)
                for i in range(n):
                    nc.vector.scalar_tensor_tensor(gates[:, i, 0:D], node_a[:, t + i, :], 1.0, wr_b, ALU.mult, ALU.mult,
                                                   accum_out=w_all[:, t + i:t + i + 1])
                nc.vector.tensor_tensor(node_f[:, t:t + n, :], o, node_a[:, t:t + n, :], ALU.add).then_inc(base_ready, 1)
                v.wait_ge(base_ready, b + 1)
            link(nc.vector.tensor_scalar(w_all, w_all, br_b, None, ALU.add))
            nc.vector.memset(flags[:, 3:4], 0.0).then_inc(w_done, 1)
            v.wait_ge(w_padded, 1)
            cur, step, cand = u32s[:, 0:1], u32s[:, 1:2], u32s[:, 2:2 + WAYS]
            reached, count_f = passed[:, 0:WAYS], passed[:, WAYS:WAYS + 1]
            v.wait_ge(search_const, 2 + sum(ways))
            nc.vector.tensor_scalar(small[:, 0, :], w_all, 0.0, 0.0, ALU.is_ge, ALU.add,
                                    accum_out=cnts[:, 0:1]).then_inc(cnt_ready, 1)
            v.wait_ge(tot_ready, 1)
            link(nc.vector.tensor_scalar(cur, banks[6][:, 0:1], float(TOPK), -1.0, ALU.is_lt, ALU.mult))
            for r, low in enumerate(shifts):
                n = ways[r]
                link(nc.vector.tensor_tensor(cand[:, 0:n], steps[:, r, 0:n], cur.to_broadcast([P, n]), ALU.bitwise_xor))
                for k in range(n):
                    ins = nc.vector.tensor_scalar(small[:, k, :], w_all, cand[:, k:k + 1].bitcast(f32), 0.0, ALU.is_ge,
                                                  ALU.add, accum_out=cnts[:, k:k + 1])
                ins.then_inc(cnt_ready, 1)
                v.wait_ge(tot_ready, r + 2)
                link(nc.vector.tensor_scalar(reached[:, 0:n], banks[6][:, 0:n], float(TOPK), 0.0, ALU.is_ge, ALU.add,
                                             accum_out=count_f))
                link(nc.vector.tensor_copy(step, count_f))
                link(nc.vector.tensor_scalar(step, step, low, None, ALU.logical_shift_left))
                link(nc.vector.tensor_tensor(cur, cur, step, ALU.bitwise_xor))
            thr = cur.bitcast(f32)
            above, equal, incl, rank, pick = (small[:, k, :] for k in range(1, 6))
            link(nc.vector.tensor_scalar(above, w_all, thr, 0.0, ALU.is_gt, ALU.add, accum_out=cnts[:, 0:1]))
            nc.vector.tensor_scalar(equal, w_all, thr, None, ALU.is_equal).then_inc(cnt_ready, 1)
            v.wait_ge(tot_ready, ROUNDS + 2)
            link(nc.vector.tensor_copy(pick, banks[6][:, 64:64 + NB]))
            link(nc.vector.memset(small[:, 6, :], 0.0))
            link(nc.vector.tensor_tensor_scan(incl, pick, small[:, 6, :], 0.0, ALU.add, ALU.add))
            link(nc.vector.tensor_tensor(incl, incl, pick, ALU.subtract))
            link(nc.vector.tensor_tensor(rank, incl, banks[6][:, 128:128 + NB], ALU.add))
            link(nc.vector.tensor_scalar(rank, rank, banks[6][:, 0:1], None, ALU.add))
            link(nc.vector.scalar_tensor_tensor(pick, rank, float(TOPK), equal, ALU.is_lt, ALU.mult))
            nc.vector.tensor_tensor(pick, pick, above, ALU.add).then_inc(pick_ready, 1)
            v.wait_ge(pick_sums, 1)
            slot, slot_i, tile_of, in_tile = small[:, 0, :], small[:, 1, :], small[:, 2, :], small[:, 3, :]
            link(nc.vector.tensor_copy(rank, banks[6][:, 192:192 + NB]))
            link(nc.vector.tensor_tensor_scan(incl, rank, small[:, 6, :], 0.0, ALU.add, ALU.add))
            link(nc.vector.tensor_tensor(incl, incl, rank, ALU.subtract))
            slot_i = slot_i.bitcast(i32)
            link(nc.vector.tensor_tensor(slot, incl, banks[6][:, 256:256 + NB], ALU.add))
            link(nc.vector.tensor_copy(slot_i, slot))
            link(nc.vector.tensor_scalar(slot_i, slot_i, 7, None, ALU.logical_shift_right))
            link(nc.vector.tensor_copy(tile_of, slot_i))
            link(nc.vector.scalar_tensor_tensor(in_tile, tile_of, float(-P), slot, ALU.mult, ALU.add))
            spread_t = lambda a, n: a.unsqueeze(2).to_broadcast([P, NB, n])
            link(nc.vector.tensor_tensor(tile_hot[:, :, 1, :], col_b[:, 0:PICKS].unsqueeze(1).to_broadcast([P, NB, PICKS]),
                                         spread_t(tile_of, PICKS), ALU.is_equal))
            link(nc.vector.tensor_tensor(tile_hot[:, :, 1, :], tile_hot[:, :, 1, :], spread_t(pick, PICKS), ALU.mult))
            link(nc.vector.tensor_tensor(tile_hot[:, :, 0, :], tile_hot[:, :, 1, :], spread_t(node_id, PICKS), ALU.mult))
            link(nc.vector.tensor_tensor(tile_hot[:, :, 1, :], tile_hot[:, :, 1, :], spread_t(w_all, PICKS), ALU.mult))
            for c in range(NX):
                a = slice(c * XC, (c + 1) * XC)
                nc.vector.tensor_tensor(slot_hot[:, a, :], col_b.unsqueeze(1).to_broadcast([P, XC, P]),
                                        in_tile[:, a].unsqueeze(2).to_broadcast([P, XC, P]),
                                        ALU.is_equal).then_inc(hots_ready, 1)
            v.wait_ge(list_psum, 1)
            nc.vector.tensor_copy(pick_id, banks[7][:, 0:PICKS]).then_inc(list_ready, 1)
            nc.vector.tensor_copy(pick_w, banks[7][:, PICKS:2 * PICKS]).then_inc(list_ready, 1)
            v.wait_ge(list_ready, 2)

            def picked_to_T(g):
                for y in range(4 * g, 4 * g + ntile[g], 2):
                    n = min(2, PICKS - y)
                    v.wait_ge(pickT_psum, y // 2 + 1)
                    nc.vector.tensor_copy(picked_T[:, y:y + n, :].rearrange("p i d -> p (i d)"),
                                          banks[y // 2 % 2][:, 0:n * D]).then_inc(pickT_ready, 1)

            v.wait_ge(xn_saved, 16 * BATCHES)
            picked_to_T(0)
            picked_to_T(1)
            for g in range(FG):
                if g + 2 < FG:
                    picked_to_T(g + 2)
                for y in range(4 * g, 4 * g + ntile[g]):
                    v.wait_ge(y_psum, y + 1)
                    nc.vector.tensor_tensor(y_t[y % 2], banks[2 + y % 2][:, 0:D], b2_b, ALU.add).then_inc(y_taken, 1)
                    v.wait_ge(y_taken, y + 1)
                    if y >= 2:
                        v.wait_ge(o_added, 16 * (y - 1))
                    nc.vector.tensor_scalar(o_t[y % 2], y_t[y % 2], pick_w[:, y:y + 1], None, ALU.mult).then_inc(o_ready, 1)

        @block.tensor
        def _(pe):
            mm, tr = nc.tensor.matmul, nc.tensor.transpose
            pe.wait_ge(const_ready, 7)
            for t in range(NB):
                n = P if t < NB - 1 else LAST
                if t % 2:
                    pe.wait_ge(xhat_act, t // 2 + 1)
                else:
                    pe.wait_ge(xhat_ready, t // 2 + 1)
                ins = mm(banks[5][:, 0:D], ones[0:n, :], node_h[0:n, t, :], start=t == 0, stop=t == NB - 1)
            ins.then_inc(colsum, 1)
            pe.wait_ge(wrong_ready, 1)
            mm(banks[4][:, 0:1], ones, wrong, start=True, stop=True).then_inc(wrong_sum, 1)
            pe.wait_ge(disorder_known, 1)
            with pe.If(pe.value_load(disorder[0:1, 0:1], min_val=0, max_val=1) > 0):
                with pe.Fori(0, NB + 1) as b:
                    pe.wait_ge(place_cnt, b + 1)
                    mm(banks[4][:, 0:1], upper, count_e[:, NT - 1:NT], start=True, stop=True)
                    mm(banks[4][:, 1:2], ones, count_e[:, NT - 1:NT], start=True, stop=True).then_inc(place_off, 1)
            for t in range(NB):
                n = P if t < NB - 1 else LAST
                pe.wait_ge(sq_ready, t + 1)
                ins = mm(banks[6][:, 0:D], ones[0:n, :], sq[t % SB][0:n, :], start=t == 0, stop=t == NB - 1)
                ins.then_inc(sq_used, 1)
                if t == KEYS_AT:
                    pe.wait_ge(diag_ready, 1)
                    diags = diag.rearrange(flat)
                    for b in range(4):
                        w = min(512, NT - 512 * b)
                        ins = mm(banks[b][:, 0:w], ones, diags[:, 512 * b:512 * b + w], start=True, stop=True)
                    ins.then_inc(keys_row, 1)
            pe.wait_ge(sq_used, NB)
            pe.nop().then_inc(colsum, 1)
            pe.wait_ge(params_in, 16 * 6)
            pe.wait_ge(cvar_ready, 1)

            def h_transposes(t):
                pe.wait_ge(h_ready[t // XC], 1)
                if t >= 2:
                    pe.wait_ge(hT_ready, t - 1)
                tr(banks[t % 2][:, 0:P], node_h[:, t, 0:P], ident)
                tr(banks[t % 2][:, P:2 * P], node_h[:, t, P:2 * P], ident).then_inc(hT_psum, 1)

            h_transposes(0)
            for t in range(NB):
                if t == REC_AT - 1:
                    pe.wait_ge(dloc_ready, 1)
                    for c in range(EC):
                        if c >= 4:
                            pe.wait_ge(rec_done, c - 3)
                        for f in range(4):
                            ins = tr(banks[4 + c % 4][:, f * P:(f + 1) * P], rec[:, c, :, f], ident)
                        ins.then_inc(recT, 1)
                if t + 1 < NB:
                    h_transposes(t + 1)
                pe.wait_ge(hT_ready, t + 1)
                if t >= 2:
                    pe.wait_ge(feat_ready, t - 1)
                mm(banks[2 + t % 2][:, :], hT[t % HB][:, 0, :], w_io[:, 0, :], start=True, stop=False)
                mm(banks[2 + t % 2][:, :], hT[t % HB][:, 1, :], w_io[:, 1, :], start=False, stop=True).then_inc(feat_psum, 1)

            pe.wait_ge(feat_ready, NB)
            pe.wait_ge(block_row, 16)

            def src_rows(g):
                pe.wait_ge(diag_done, g + 1)
                mm(banks[0][:, :], ones, eq.rearrange("p u n -> p (u n)"), start=True, stop=True).then_inc(bcast_done, 1)

            def sums(g, h, count):
                for u in range(G):
                    if u == 0:
                        pe.wait_ge(iw_done, g + 1)
                    pe.wait_ge(gathered[h][u], 16 * count)
                    if u % 2 == 0 and not (isinstance(g, int) and g == 0):
                        pe.wait_ge(in_added, G * (g - 1) + u + 2)
                    mm(banks[4 + u // 2][:, (u % 2) * D:(u % 2 + 1) * D], hot_iw[h][:, u, :], rows[h][u],
                       start=True, stop=True).then_inc(in_psum, 1)

            def group(turn, h, first):
                g = turn * 2 + h
                blocks = nc.values_load_multi_w_load_instructions(
                    pair_block[0:1, bass.ds(g * G, G)], engines=[mybir.EngineType.PE], min_val=0, max_val=NB - 1,
                    skip_runtime_bounds_check_because="block numbers lie in the range by construction")[1]
                pe.wait_ge(sel_done, g + 1)
                if not first:
                    pe.wait_ge(mix_ready, g)
                for u in range(G):
                    ins = mm(banks[1][:, u * P:(u + 1) * P], hot[:, u, :], same_ow[:, u, :], start=True, stop=True)
                ins.then_inc(mix_psum, 1)
                if not first:
                    sums(g - 1, 1 - h, turn + h)
                pe.wait_ge(mix_ready, g + 1)
                for u in range(G):
                    if not first and u % 2 == 0:
                        pe.wait_ge(out_ready, G * (g - 1) + u + 2)
                    f = node_f[:, bass.ds(blocks[u], 1), :].rearrange("p a d -> p (a d)")
                    mm(banks[2 + u // 2][:, (u % 2) * D:(u % 2 + 1) * D], mix[:, u, :], f,
                       start=True, stop=True).then_inc(out_psum, 1)
                src_rows(g + 2)

            src_rows(0)
            src_rows(1)
            group(0, 0, True)
            group(0, 1, False)
            with pe.Fori(1, GROUPS // 2) as turn:
                for h in range(2):
                    group(turn, h, False)
            sums(GROUPS - 1, 1, GROUPS // 2)
            pe.wait_ge(in_psum, G * GROUPS)
            pe.nop().then_inc(main_done, 1)

            pe.wait_ge(main_done, 3)

            def transposes(b):
                if b >= 2:
                    pe.wait_ge(aT_ready, b - 1)
                for part in range(2):
                    if part:
                        pe.wait_ge(ao_ready, b + 1)
                    for i in range(in_batch[b]):
                        a = acc_t[b % 2][:, 0, i, :] if part else node_a[:, BT * b + i, :]
                        for k in range(2):
                            at = 2 * part + k
                            ins = tr(banks[aT_banks[b % 2][i]][:, at * P:(at + 1) * P], a[:, k * P:(k + 1) * P], ident)
                ins.then_inc(aT_psum, 1)

            transposes(0)
            pe.wait_ge(post_w, 16 * 7)
            for b in range(BATCHES):
                if b + 1 < BATCHES:
                    transposes(b + 1)
                pe.wait_ge(aT_ready, b + 1)
                if b >= 2:
                    pe.wait_ge(gate_in, b - 1)
                pe.wait_ge(hT_in[b % 2], 16 * (b // 2 + 1))
                for i in range(in_batch[b]):
                    for k in range(6):
                        if k < 2:
                            lhsT, rhs = hT_t[b % 2][:, i, k * P:(k + 1) * P], wh[:, k, :]
                        else:
                            lhsT, rhs = aT[b % 2][:, i, k - 2, :], wx[:, k - 2, :]
                        ins = mm(banks[3 + 2 * (b % 2) + i][:, :], lhsT, rhs, start=k == 0, stop=k == 5)
                ins.then_inc(gate_psum, 1)
            for r in range(ROUNDS + 2):
                pe.wait_ge(cnt_ready, r + 1)
                if r < ROUNDS + 1:
                    n = ways[r - 1] if r else 1
                    mm(banks[6][:, 0:n], ones, cnts[:, 0:n], start=True, stop=True).then_inc(tot_ready, 1)
                else:
                    mm(banks[6][:, 0:1], ones, cnts[:, 0:1], start=True, stop=True)
                    mm(banks[6][:, 64:64 + NB], ones, small[:, 2, :], start=True, stop=True)
                    mm(banks[6][:, 128:128 + NB], upper, small[:, 2, :], start=True, stop=True).then_inc(tot_ready, 1)
            pe.wait_ge(pick_ready, 1)
            mm(banks[6][:, 192:192 + NB], ones, small[:, 5, :], start=True, stop=True)
            mm(banks[6][:, 256:256 + NB], upper, small[:, 5, :], start=True, stop=True).then_inc(pick_sums, 1)
            for t in range(NB):
                pe.wait_ge(hots_ready, t // XC + 1)
                ins = mm(banks[7][:, 0:2 * PICKS], slot_hot[:, t, :], tile_hot[:, t, :, :].rearrange("p k s -> p (k s)"),
                         start=t == 0, stop=t == NB - 1)
            ins.then_inc(list_psum, 1)

            def picked_transposes(g):
                pe.wait_ge(picked[g], 16 * ntile[g])
                for y in range(4 * g, 4 * g + ntile[g], 2):
                    if y >= 4:
                        pe.wait_ge(pickT_ready, y // 2 - 1)
                    for i in range(min(2, PICKS - y)):
                        for k in range(2):
                            ins = tr(banks[y // 2 % 2][:, (2 * i + k) * P:(2 * i + k + 1) * P],
                                     picked_rows[:, y + i, k * P:(k + 1) * P], ident)
                    ins.then_inc(pickT_psum, 1)

            def hidden(g):
                n = ntile[g]
                pe.wait_ge(pickT_ready, -(-(4 * g + n) // 2))
                for c in range(HC):
                    k = HC * g + c
                    if k >= 2:
                        pe.wait_ge(hid_ready, k - 1)
                    for kk in range(2):
                        ins = mm(banks[4 + k % 2][:, 0:n * P], w1_s[:, kk, c * P:(c + 1) * P],
                                 picked_T[:, 4 * g:4 * g + n, kk * P:(kk + 1) * P], start=kk == 0, stop=kk == 1)
                    ins.then_inc(hid_psum, 1)

            pe.wait_ge(ffn_w, 32)
            picked_transposes(0)
            hidden(0)
            picked_transposes(1)
            for g in range(FG):
                if g + 2 < FG:
                    picked_transposes(g + 2)
                if g + 1 < FG:
                    hidden(g + 1)
                pe.wait_ge(hid_ready, HC * (g + 1))
                for y in range(4 * g, 4 * g + ntile[g]):
                    if y >= 2:
                        pe.wait_ge(y_taken, y - 1)
                    for c in range(HC):
                        ins = mm(banks[2 + y % 2][:, 0:D], hid[g % 2][:, c, y % 4 * P:(y % 4 + 1) * P],
                                 w2_s[:, c, :], start=c == 0, stop=c == HC - 1)
                    ins.then_inc(y_psum, 1)


def kernel(x, src, dst, edge_weight, edge_weight_n2, L0_gnn_gamma, L0_gnn_beta, L0_gnn_W_in, L0_gnn_b_in,
           L0_gnn_W_out, L0_gnn_b_out, L0_gnn_W_x2i, L0_gnn_b_x2i, L0_gnn_W_h2h, L0_ffn_attention_mask,
           L0_ffn_wr, L0_ffn_br, L0_ffn_w1, L0_ffn_b1, L0_ffn_w2, L0_ffn_b2):
    import concourse.bacc as bacc
    from concourse.bass_utils import run_bass_kernel_spmd
    nc = bacc.Bacc("TRN2", target_bir_lowering=False, num_devices=1)
    given = dict(x=x, src=src, dst=dst, iw=edge_weight, ow=edge_weight_n2, gamma=L0_gnn_gamma, beta=L0_gnn_beta,
                 w_in=L0_gnn_W_in, b_in=L0_gnn_b_in, w_out=L0_gnn_W_out, b_out=L0_gnn_b_out, w_x2i=L0_gnn_W_x2i,
                 b_x2i=L0_gnn_b_x2i, w_h2h=L0_gnn_W_h2h, wr=L0_ffn_wr, br=L0_ffn_br, w1=L0_ffn_w1, b1=L0_ffn_b1,
                 w2=L0_ffn_w2, b2=L0_ffn_b2)
    arrays, args = {}, []
    for name, a in given.items():
        a = np.ascontiguousarray(a)
        arrays[f"{name}_dram"] = a
        args.append(nc.dram_tensor(f"{name}_dram", a.shape, mybir.dt.from_np(a.dtype), kind="ExternalInput").ap())
    args.append(nc.dram_tensor("out_dram", x.shape, mybir.dt.float32, kind="ExternalOutput").ap())
    gnn_ffn(nc, *args)
    return run_bass_kernel_spmd(nc, [arrays], core_ids=[0]).results[0]["out_dram"]
```
